# Optimizing a Trainium2 kernel written in Bass

```python
import numpy as np
import jax
import jax.numpy as jnp

def _softmax(x, axis=-1):
    return jax.nn.softmax(x, axis=axis)

def _gelu(x):
    return jax.nn.gelu(x, approximate=True)

def _silu(x):
    return jax.nn.silu(x)

def _sigmoid(x):
    return jax.nn.sigmoid(x)

def _layernorm(x, axis=-1, eps=1e-05):
    m = jnp.mean(x, axis=axis, keepdims=True)
    v = jnp.var(x, axis=axis, keepdims=True)
    return (x - m) / jnp.sqrt(v + eps)

def _scatter_add(tgt, idx, src, axis=0):
    return tgt.at[idx].add(src)

def _segment_sum(src, seg, n):
    return jax.ops.segment_sum(src, seg, n)
kernel_name = 'mk_gnn_preln_d4_gnn_r8_15e052'

def setup_inputs(seed: int=0):
    np.random.seed(seed)
    _w = jnp.asarray

    def _rec_inputs():
        import jax
        import jax.numpy as jnp
        _gk = jax.random.key(seed)
        x = -0.000202 + 1 * jax.random.normal(jax.random.fold_in(_gk, 1), (6250, 128), jnp.float32)
        src = jax.random.randint(jax.random.fold_in(_gk, 2), (100000,), 0, 6250, jnp.int32)
        dst = jax.random.randint(jax.random.fold_in(_gk, 3), (100000,), 0, 6250, jnp.int32)
        _o = jnp.argsort(dst, stable=True)
        src = src[_o]
        dst = dst[_o]
        return (x, src, dst)
    x, src, dst = _rec_inputs()

    def _L0_gnn_setup():
        import jax, jax.numpy as jnp
        import numpy as np
        N_NODES = 6250
        N_EDGES = 75000
        D = 128
        D_OUT = 128
        key = jax.random.key(seed)
        ks = jax.random.split(key, 6)
        features = jax.random.normal(ks[0], (N_NODES, D), dtype=jnp.float32)
        edge_index = jax.random.randint(ks[1], (2, N_EDGES), 0, N_NODES, dtype=jnp.int64)

        def xavier(k, shape):
            gain = float(np.sqrt(2.0))
            fan_out, fan_in = shape
            bound = gain * float(np.sqrt(6.0 / (fan_in + fan_out)))
            return jax.random.uniform(k, shape, jnp.float32, -bound, bound)
        W_neigh = xavier(ks[2], (D, D))
        b_neigh = jnp.zeros((D,), jnp.float32)
        W_edge = xavier(ks[3], (D, 2 * D))
        b_edge = jnp.zeros((D,), jnp.float32)
        W_lin = xavier(ks[4], (D_OUT, 2 * D))
        b_lin = jnp.zeros((D_OUT,), jnp.float32)
        return {'features': features, 'edge_index': edge_index, 'W_neigh': W_neigh, 'b_neigh': b_neigh, 'W_edge': W_edge, 'b_edge': b_edge, 'W_lin': W_lin, 'b_lin': b_lin}
    _L0_gnn_all = _L0_gnn_setup()
    _L0_gnn_in = {k: v for k, v in _L0_gnn_all.items() if k in ('W_neigh', 'b_neigh', 'W_edge', 'b_edge', 'W_lin', 'b_lin')}
    del _L0_gnn_all

    def _L1_gnn_setup():
        import jax, jax.numpy as jnp
        import numpy as np
        N, E, D, H, L, FF = (6250, 62500, 128, 8, 2, 512)
        HD = D // H

        def _layernorm(x, g, b):
            mu = jnp.mean(x, axis=-1, keepdims=True)
            var = jnp.mean(jnp.square(x - mu), axis=-1, keepdims=True)
            return (x - mu) * jax.lax.rsqrt(var + 1e-05) * g + b

        def _forward(edge_index, x, Wq, bq, Wk, bk, Wv, bv, Wo, bo, Wpos, bpos, Wdeg, bdeg, ln1_g, ln1_b, ln2_g, ln2_b, W1, b1, W2, b2):
            n = x.shape[0]
            loops = jnp.arange(n, dtype=edge_index.dtype)
            src = jnp.concatenate([edge_index[0], loops])
            dst = jnp.concatenate([edge_index[1], loops])
            scale = np.float32(np.sqrt(HD))
            for l in range(L):
                xn = _layernorm(x, ln1_g[l], ln1_b[l])
                deg = jax.ops.segment_sum(jnp.ones_like(src, dtype=x.dtype), src, num_segments=n)
                deg = (deg - deg.mean()) / (jnp.std(deg, ddof=1) + 1e-06)
                pos = xn @ Wpos[l] + bpos[l] + deg[:, None] * Wdeg[l][0] + bdeg[l]
                xp = xn + pos
                q = (xp @ Wq[l] + bq[l]).reshape(n, H, HD)
                k = (xp @ Wk[l] + bk[l]).reshape(n, H, HD)
                v = (xp @ Wv[l] + bv[l]).reshape(n, H, HD)
                att = jnp.einsum('ehd,ehd->eh', q[dst], k[src]) / scale
                att = jnp.nan_to_num(jnp.clip(att, -50.0, 50.0), nan=0.0, posinf=50.0, neginf=-50.0)
                m = jax.ops.segment_max(att, dst, num_segments=n)
                ex = jnp.exp(att - m[dst])
                s = jax.ops.segment_sum(ex, dst, num_segments=n)
                alpha = ex / (s[dst] + 1e-16)
                msg = (v[src] * alpha[:, :, None]).reshape(-1, D)
                aggr = jax.ops.segment_sum(msg, dst, num_segments=n)
                x = x + (aggr @ Wo[l] + bo[l])
                h = jax.nn.gelu(_layernorm(x, ln2_g[l], ln2_b[l]) @ W1[l] + b1[l], approximate=False)
                x = x + (h @ W2[l] + b2[l])
            return x
        key = jax.random.key(seed)
        ks = jax.random.split(key, 16)
        inp = {'x': jax.random.normal(ks[0], (N, D), jnp.float32), 'edge_index': jax.random.randint(ks[1], (2, E), 0, N, jnp.int32)}

        def w(k, shape, fan_in):
            return jax.random.normal(k, shape, jnp.float32) / np.float32(np.sqrt(fan_in))
        inp['Wq'] = w(ks[2], (L, D, D), D)
        inp['Wk'] = w(ks[3], (L, D, D), D)
        inp['Wv'] = w(ks[4], (L, D, D), D)
        inp['Wo'] = w(ks[5], (L, D, D), D)
        inp['Wpos'] = w(ks[6], (L, D, D), D)
        inp['Wdeg'] = w(ks[7], (L, 1, D), 1)
        inp['W1'] = w(ks[8], (L, D, FF), D)
        inp['W2'] = w(ks[9], (L, FF, D), FF)
        for name, shape in [('bq', (L, D)), ('bk', (L, D)), ('bv', (L, D)), ('bo', (L, D)), ('bpos', (L, D)), ('bdeg', (L, D)), ('ln1_b', (L, D)), ('ln2_b', (L, D)), ('b1', (L, FF)), ('b2', (L, D))]:
            inp[name] = jnp.zeros(shape, jnp.float32)
        inp['ln1_g'] = jnp.ones((L, D), jnp.float32)
        inp['ln2_g'] = jnp.ones((L, D), jnp.float32)
        return inp
    _L1_gnn_all = _L1_gnn_setup()
    _L1_gnn_in = {k: v for k, v in _L1_gnn_all.items() if k in ('Wq', 'bq', 'Wk', 'bk', 'Wv', 'bv', 'Wo', 'bo', 'Wpos', 'bpos', 'Wdeg', 'bdeg', 'ln1_g', 'ln1_b', 'ln2_g', 'ln2_b', 'W1', 'b1', 'W2', 'b2')}
    del _L1_gnn_all

    def _L2_gnn_setup():
        import jax, jax.numpy as jnp
        import numpy as np
        N_NODES = 12500
        N_EDGES = 200000
        IN_FEATS = 128
        N_HIDDEN = 128
        key = jax.random.key(seed)
        k1, k2, k3, k4 = jax.random.split(key, 4)
        features = jax.random.normal(k1, (N_NODES, IN_FEATS), dtype=jnp.float32)
        src = jax.random.randint(k2, (N_EDGES,), 0, N_NODES, dtype=jnp.int32)
        dst = jax.random.randint(k3, (N_EDGES,), 0, N_NODES, dtype=jnp.int32)
        weight = jax.random.normal(k4, (IN_FEATS, N_HIDDEN), dtype=jnp.float32) * (1.0 / np.sqrt(IN_FEATS))
        bias = jnp.zeros((N_HIDDEN,), dtype=jnp.float32)
        return {'features': features, 'src': src, 'dst': dst, 'weight': weight, 'bias': bias}
    _L2_gnn_all = _L2_gnn_setup()
    _L2_gnn_in = {k: v for k, v in _L2_gnn_all.items() if k in ('weight', 'bias')}
    del _L2_gnn_all

    def _L3_gnn_setup():
        import jax, jax.numpy as jnp
        import numpy as np
        N_NODES = 6250
        N_EDGES = 100000
        D_IN = 128
        D_HID = 128
        D_Z = 64

        def _gcn_conv(x, src, dst, W, b, num_nodes):
            h = x @ W
            deg = jax.ops.segment_sum(jnp.ones_like(dst, dtype=x.dtype), dst, num_segments=num_nodes)
            dinv = jnp.where(deg > 0, jax.lax.rsqrt(deg), 0.0)
            norm = dinv[src] * dinv[dst]
            out = jax.ops.segment_sum(norm[:, None] * h[src], dst, num_segments=num_nodes)
            return out + b
        key = jax.random.key(seed)
        ks = jax.random.split(key, 6)
        x = jax.random.normal(ks[0], (N_NODES, D_IN), dtype=jnp.float32)
        edge_index = jax.random.randint(ks[1], (2, N_EDGES), 0, N_NODES, dtype=jnp.int64)
        W1 = jax.random.normal(ks[2], (D_IN, D_HID), dtype=jnp.float32) / np.sqrt(D_IN)
        b1 = jnp.zeros((D_HID,), dtype=jnp.float32)
        W2 = jax.random.normal(ks[3], (D_HID, D_Z), dtype=jnp.float32) / np.sqrt(D_HID)
        b2 = jnp.zeros((D_Z,), dtype=jnp.float32)
        Wd = jax.random.normal(ks[4], (D_Z, D_IN), dtype=jnp.float32) / np.sqrt(D_Z)
        bd = jnp.zeros((D_IN,), dtype=jnp.float32)
        return {'x': x, 'edge_index': edge_index, 'W1': W1, 'b1': b1, 'W2': W2, 'b2': b2, 'Wd': Wd, 'bd': bd}
    _L3_gnn_all = _L3_gnn_setup()
    _L3_gnn_in = {k: v for k, v in _L3_gnn_all.items() if k in ('W1', 'b1', 'W2', 'b2', 'Wd', 'bd')}
    del _L3_gnn_all
    return {'x': x, 'src': src, 'dst': dst, 'L0_gnn_W_neigh': _L0_gnn_in['W_neigh'], 'L0_gnn_b_neigh': _L0_gnn_in['b_neigh'], 'L0_gnn_W_edge': _L0_gnn_in['W_edge'], 'L0_gnn_b_edge': _L0_gnn_in['b_edge'], 'L0_gnn_W_lin': _L0_gnn_in['W_lin'], 'L0_gnn_b_lin': _L0_gnn_in['b_lin'], 'L1_gnn_Wq': _L1_gnn_in['Wq'], 'L1_gnn_bq': _L1_gnn_in['bq'], 'L1_gnn_Wk': _L1_gnn_in['Wk'], 'L1_gnn_bk': _L1_gnn_in['bk'], 'L1_gnn_Wv': _L1_gnn_in['Wv'], 'L1_gnn_bv': _L1_gnn_in['bv'], 'L1_gnn_Wo': _L1_gnn_in['Wo'], 'L1_gnn_bo': _L1_gnn_in['bo'], 'L1_gnn_Wpos': _L1_gnn_in['Wpos'], 'L1_gnn_bpos': _L1_gnn_in['bpos'], 'L1_gnn_Wdeg': _L1_gnn_in['Wdeg'], 'L1_gnn_bdeg': _L1_gnn_in['bdeg'], 'L1_gnn_ln1_g': _L1_gnn_in['ln1_g'], 'L1_gnn_ln1_b': _L1_gnn_in['ln1_b'], 'L1_gnn_ln2_g': _L1_gnn_in['ln2_g'], 'L1_gnn_ln2_b': _L1_gnn_in['ln2_b'], 'L1_gnn_W1': _L1_gnn_in['W1'], 'L1_gnn_b1': _L1_gnn_in['b1'], 'L1_gnn_W2': _L1_gnn_in['W2'], 'L1_gnn_b2': _L1_gnn_in['b2'], 'L2_gnn_weight': _L2_gnn_in['weight'], 'L2_gnn_bias': _L2_gnn_in['bias'], 'L3_gnn_W1': _L3_gnn_in['W1'], 'L3_gnn_b1': _L3_gnn_in['b1'], 'L3_gnn_W2': _L3_gnn_in['W2'], 'L3_gnn_b2': _L3_gnn_in['b2'], 'L3_gnn_Wd': _L3_gnn_in['Wd'], 'L3_gnn_bd': _L3_gnn_in['bd']}

def reference(x, src, dst, L0_gnn_W_neigh, L0_gnn_b_neigh, L0_gnn_W_edge, L0_gnn_b_edge, L0_gnn_W_lin, L0_gnn_b_lin, L1_gnn_Wq, L1_gnn_bq, L1_gnn_Wk, L1_gnn_bk, L1_gnn_Wv, L1_gnn_bv, L1_gnn_Wo, L1_gnn_bo, L1_gnn_Wpos, L1_gnn_bpos, L1_gnn_Wdeg, L1_gnn_bdeg, L1_gnn_ln1_g, L1_gnn_ln1_b, L1_gnn_ln2_g, L1_gnn_ln2_b, L1_gnn_W1, L1_gnn_b1, L1_gnn_W2, L1_gnn_b2, L2_gnn_weight, L2_gnn_bias, L3_gnn_W1, L3_gnn_b1, L3_gnn_W2, L3_gnn_b2, L3_gnn_Wd, L3_gnn_bd):
    import jax
    import jax.numpy as jnp

    def _L0_gnn_ref(features, edge_index, W_neigh, b_neigh, W_edge, b_edge, W_lin, b_lin):
        import jax, jax.numpy as jnp
        import numpy as np
        N_NODES = 6250
        N_EDGES = 75000
        D = 128
        D_OUT = 128
        n = features.shape[0]
        dst = edge_index[0]
        src = edge_index[1]
        h = features @ W_neigh.T + b_neigh
        h_src = h[src]
        edge_feats = jnp.abs(h[dst] - h_src)
        new_h = jnp.concatenate([h_src, edge_feats], axis=-1) @ W_edge.T + b_edge
        seg_sum = jax.ops.segment_sum(new_h, dst, num_segments=n)
        cnt = jax.ops.segment_sum(jnp.ones((dst.shape[0],), jnp.float32), dst, num_segments=n)[:, None]
        s = (h + seg_sum) / jnp.maximum(cnt, 1.0)
        z = jnp.concatenate([features, s], axis=-1) @ W_lin.T + b_lin
        return z

    def _L1_gnn_ref(x, edge_index, Wq, bq, Wk, bk, Wv, bv, Wo, bo, Wpos, bpos, Wdeg, bdeg, ln1_g, ln1_b, ln2_g, ln2_b, W1, b1, W2, b2):
        import jax, jax.numpy as jnp
        import numpy as np
        N, E, D, H, L, FF = (6250, 62500, 128, 8, 2, 512)
        HD = D // H

        def _layernorm(x, g, b):
            mu = jnp.mean(x, axis=-1, keepdims=True)
            var = jnp.mean(jnp.square(x - mu), axis=-1, keepdims=True)
            return (x - mu) * jax.lax.rsqrt(var + 1e-05) * g + b

        def _forward(edge_index, x, Wq, bq, Wk, bk, Wv, bv, Wo, bo, Wpos, bpos, Wdeg, bdeg, ln1_g, ln1_b, ln2_g, ln2_b, W1, b1, W2, b2):
            n = x.shape[0]
            loops = jnp.arange(n, dtype=edge_index.dtype)
            src = jnp.concatenate([edge_index[0], loops])
            dst = jnp.concatenate([edge_index[1], loops])
            scale = np.float32(np.sqrt(HD))
            for l in range(L):
                xn = _layernorm(x, ln1_g[l], ln1_b[l])
                deg = jax.ops.segment_sum(jnp.ones_like(src, dtype=x.dtype), src, num_segments=n)
                deg = (deg - deg.mean()) / (jnp.std(deg, ddof=1) + 1e-06)
                pos = xn @ Wpos[l] + bpos[l] + deg[:, None] * Wdeg[l][0] + bdeg[l]
                xp = xn + pos
                q = (xp @ Wq[l] + bq[l]).reshape(n, H, HD)
                k = (xp @ Wk[l] + bk[l]).reshape(n, H, HD)
                v = (xp @ Wv[l] + bv[l]).reshape(n, H, HD)
                att = jnp.einsum('ehd,ehd->eh', q[dst], k[src]) / scale
                att = jnp.nan_to_num(jnp.clip(att, -50.0, 50.0), nan=0.0, posinf=50.0, neginf=-50.0)
                m = jax.ops.segment_max(att, dst, num_segments=n)
                ex = jnp.exp(att - m[dst])
                s = jax.ops.segment_sum(ex, dst, num_segments=n)
                alpha = ex / (s[dst] + 1e-16)
                msg = (v[src] * alpha[:, :, None]).reshape(-1, D)
                aggr = jax.ops.segment_sum(msg, dst, num_segments=n)
                x = x + (aggr @ Wo[l] + bo[l])
                h = jax.nn.gelu(_layernorm(x, ln2_g[l], ln2_b[l]) @ W1[l] + b1[l], approximate=False)
                x = x + (h @ W2[l] + b2[l])
            return x
        return _forward(edge_index, x, Wq, bq, Wk, bk, Wv, bv, Wo, bo, Wpos, bpos, Wdeg, bdeg, ln1_g, ln1_b, ln2_g, ln2_b, W1, b1, W2, b2)

    def _L2_gnn_ref(features, src, dst, weight, bias):
        import jax, jax.numpy as jnp
        import numpy as np
        N_NODES = 12500
        N_EDGES = 200000
        IN_FEATS = 128
        N_HIDDEN = 128
        "DGL GraphConv with norm='both' + relu activation.\n            out = relu( D_dst^{-1/2} * segment_sum( (D_src^{-1/2} x)[src] -> dst ) @ W + b )\n            "
        n = features.shape[0]
        ones_e = jnp.ones(src.shape[0], dtype=features.dtype)
        deg_out = jnp.clip(jax.ops.segment_sum(ones_e, src, num_segments=n), 1.0)
        deg_in = jnp.clip(jax.ops.segment_sum(ones_e, dst, num_segments=n), 1.0)
        h = features * jax.lax.rsqrt(deg_out)[:, None]
        agg = jax.ops.segment_sum(h[src], dst, num_segments=n)
        agg = agg * jax.lax.rsqrt(deg_in)[:, None]
        out = agg @ weight + bias
        return jax.nn.relu(out)

    def _L3_gnn_ref(x, edge_index, W1, b1, W2, b2, Wd, bd):
        import jax, jax.numpy as jnp
        import numpy as np
        N_NODES = 6250
        N_EDGES = 100000
        D_IN = 128
        D_HID = 128
        D_Z = 64

        def _gcn_conv(x, src, dst, W, b, num_nodes):
            h = x @ W
            deg = jax.ops.segment_sum(jnp.ones_like(dst, dtype=x.dtype), dst, num_segments=num_nodes)
            dinv = jnp.where(deg > 0, jax.lax.rsqrt(deg), 0.0)
            norm = dinv[src] * dinv[dst]
            out = jax.ops.segment_sum(norm[:, None] * h[src], dst, num_segments=num_nodes)
            return out + b
        n = x.shape[0]
        loops = jnp.arange(n, dtype=edge_index.dtype)
        src = jnp.concatenate([edge_index[0], loops])
        dst = jnp.concatenate([edge_index[1], loops])
        h = jax.nn.relu(_gcn_conv(x, src, dst, W1, b1, n))
        z = _gcn_conv(h, src, dst, W2, b2, n)
        return jax.nn.sigmoid(z @ Wd + bd)
    edge_index = jnp.stack([src, dst])
    h = jnp.maximum(_layernorm(x, axis=-1), 0.0)
    x = x + _L0_gnn_ref(h, edge_index, L0_gnn_W_neigh, L0_gnn_b_neigh, L0_gnn_W_edge, L0_gnn_b_edge, L0_gnn_W_lin, L0_gnn_b_lin)
    h = jnp.maximum(_layernorm(x, axis=-1), 0.0)
    x = x + _L1_gnn_ref(h, edge_index, L1_gnn_Wq, L1_gnn_bq, L1_gnn_Wk, L1_gnn_bk, L1_gnn_Wv, L1_gnn_bv, L1_gnn_Wo, L1_gnn_bo, L1_gnn_Wpos, L1_gnn_bpos, L1_gnn_Wdeg, L1_gnn_bdeg, L1_gnn_ln1_g, L1_gnn_ln1_b, L1_gnn_ln2_g, L1_gnn_ln2_b, L1_gnn_W1, L1_gnn_b1, L1_gnn_W2, L1_gnn_b2)
    h = jnp.maximum(_layernorm(x, axis=-1), 0.0)
    x = x + _L2_gnn_ref(h, src, dst, L2_gnn_weight, L2_gnn_bias)
    h = jnp.maximum(_layernorm(x, axis=-1), 0.0)
    x = x + _L3_gnn_ref(h, edge_index, L3_gnn_W1, L3_gnn_b1, L3_gnn_W2, L3_gnn_b2, L3_gnn_Wd, L3_gnn_bd)
    return x

_drawn_inputs = setup_inputs


def setup_inputs(seed=0):
    import zlib

    import numpy as np

    out = dict(_drawn_inputs(seed))
    spreads = {'L0_gnn_b_neigh': (0.0, 0.1),
     'L0_gnn_b_edge': (0.0, 0.1),
     'L0_gnn_b_lin': (0.0, 0.1),
     'L1_gnn_bq': (0.0, 0.1),
     'L1_gnn_bk': (0.0, 2.0),
     'L1_gnn_bv': (0.0, 0.1),
     'L1_gnn_bo': (0.0, 0.1),
     'L1_gnn_bpos': (0.0, 0.1),
     'L1_gnn_bdeg': (0.0, 0.1),
     'L1_gnn_ln1_g': (1.0, 0.2),
     'L1_gnn_ln1_b': (0.0, 0.1),
     'L1_gnn_ln2_g': (1.0, 0.2),
     'L1_gnn_ln2_b': (0.0, 0.274),
     'L1_gnn_b1': (0.0, 0.269),
     'L1_gnn_b2': (0.0, 0.1),
     'L2_gnn_bias': (0.0, 0.504),
     'L3_gnn_b1': (0.0, 2.0),
     'L3_gnn_b2': (0.0, 2.0),
     'L3_gnn_bd': (0.0, 0.8)}
    factors = {'L3_gnn_W1': 3.596}
    for name, (base, spread) in spreads.items():
        noise = np.random.default_rng([zlib.crc32(name.encode()), seed]).standard_normal(out[name].shape)
        drawn = base * np.exp(spread * noise) if base else spread * noise
        out[name] = jnp.asarray(drawn.astype(out[name].dtype))
    for name, factor in factors.items():
        out[name] = (out[name] * factor).astype(out[name].dtype)
    return out
```

```python
import concourse.bass as bass
from concourse import mybir
from contextlib import ExitStack

F32 = mybir.dt.float32
I32 = mybir.dt.int32
ALU = mybir.AluOpType
ACT = mybir.ActivationFunctionType
AX = mybir.AxisListType

P = 128
N, E, D = 6250, 100000, 128
HEADS, HD, FF, DZ = 8, 16, 512, 64
NT = -(-N // P)
LAST = N - (NT - 1) * P
TG = 7
NG = NT // TG
assert NG * TG == NT
SB = 28
EC = -(-E // (P * 2 * SB)) * 2 * SB
EFULL, EREST = E // EC, E % EC
S4 = 4
PB = 16
STEPS = -(-((E - NT) // P + NT) // (2 * PB)) * 2 * PB
GROUPS = STEPS // S4
AW = 2 * HEADS * HD
L1W = D + HEADS + 1
OUT_OF_RANGE = 1 << 20
ENGINES = 5
CHAIN = {"a": 5, "b": 10, "d0": 13, "e0": 9, "d1": 13, "e1": 14, "f": 7, "g": 3, "h": 2}


class Events(dict):
    pass


def wait(eng, s, what, value, slot=None):
    if isinstance(value, int) and value <= 0:
        return
    eng.wait_ge(s[what] if slot is None else s[what][slot], value + s.base[what])


def gated(eng, passed):
    eng.sem_inc(passed)


class Chain:

    def __init__(self, eng, sem, per, base=0):
        self.eng, self.sem, self.per, self.base = eng, sem, per, base

    def turn(self, g):
        self.start, self.k = g * self.per + self.base, 0

    def link(self, ins):
        self.k += 1
        ins.then_inc(self.sem, 1)
        self.eng.wait_ge(self.sem, self.start + self.k)

    def end(self):
        assert self.k == self.per, (self.base, self.k, self.per)


def build(nc, a, out, debug=None):
    with ExitStack() as ctx:
        def sb(name, shape, dt=F32):
            return ctx.enter_context(nc.sbuf_tensor(name, shape, dt))

        def sem(name):
            return ctx.enter_context(nc.semaphore(name))

        tab_h = nc.dram_tensor("tab_h", (NT * P, D), F32, kind="Internal").ap()
        tab_kv = nc.dram_tensor("tab_kv", (NT * P, 2 * D), F32, kind="Internal").ap()
        tab_z = nc.dram_tensor("tab_z", (NT * P, DZ), F32, kind="Internal").ap()
        lists = [nc.dram_tensor(f"list{o}", (P * STEPS, 2), I32, kind="Internal").ap() for o in range(2)]

        X = sb("X", [P, NT, D])
        Y = sb("Y", [P, NT, D])
        Q = sb("Q", [P, NT, D])
        ACC = sb("ACC", [P, NT * AW])
        accv = {w: ACC[:, 0:NT * w].rearrange("p (t w) -> p t w", w=w) for w in (AW, L1W, D, DZ)}
        EL = [sb(f"EL{o}", [P, STEPS, 2], I32) for o in range(2)]
        LO = [sb(f"LO{o}", [P, STEPS]) for o in range(2)]
        TILE = [sb(f"TILE{o}", [1, STEPS], I32) for o in range(2)]
        SCR = sb("SCR", [P, 7296])
        IOTA = sb("IOTA", [P, P])
        IDENT = sb("IDENT", [P, P])
        ONES = sb("ONES", [P, P])
        ZERO = sb("ZERO", [P, D])
        STAGE = sb("STAGE", [P, 2, SB], I32)
        PAIRS = sb("PAIRS", [P, 2, SB, 2], I32)
        WMAT = sb("WMAT", [P, 11, D])
        WL1 = sb("WL1", [P, 5, D])
        WF1 = sb("WF1", [P, FF])
        WF2 = sb("WF2", [P, FF // P, D])
        B1T = sb("B1T", [P, FF // P])
        BL1 = sb("BL1", [P, 12, D])
        BIAS = sb("BIAS", [P, 7, D])
        NODE = sb("NODE", [P, 8, NT])
        OUTD, IND, DEGN, RO, RI, DI, TMPN, MASK = (NODE[:, i, :] for i in range(8))
        ST = sb("ST", [P, TG, 6])
        MV = sb("MV", [P, TG, 2])
        RSTD = sb("RSTD", [P, TG])
        SD = sb("SD", [P, TG])
        EPS = sb("EPS", [P, 1])
        CT = sb("CT", [P, 2, TG])
        SMALL = sb("SMALL", [P, 8])
        RSUM = sb("RSUM", [P, TG, HEADS])
        EX = sb("EX", [P, TG, HEADS])
        ATT = sb("ATT", [P, TG, HEADS])

        G = SCR[:, 0:2048].rearrange("p (r s w) -> p r s w", r=2, s=S4)
        OH = SCR[:, 2048:4096].rearrange("p (r s w) -> p r s w", r=4, s=S4)
        OHT = SCR[:, 4096:5120].rearrange("p (r s w) -> p r s w", r=2, s=S4)
        M = SCR[:, 5120:5120 + 2 * S4 * L1W].rearrange("p (r s w) -> p r s w", r=2, s=S4)
        PROD = SCR[:, 6656:7168].rearrange("p (s w) -> p s w", s=S4)
        EATT = SCR[:, 7168:7168 + S4 * HEADS].rearrange("p (s h) -> p s h", s=S4)
        def tmp(i, w=1):
            return SCR[:, i * TG * D:(i + w) * TG * D]
        XN = tmp(0).rearrange("p (t d) -> p t d", t=TG)
        XP = tmp(1).rearrange("p (t d) -> p t d", t=TG)
        T1, T2, T3 = tmp(2), tmp(3), tmp(4)
        KV = tmp(5, 2).rearrange("p (t d) -> p t d", t=TG)
        HT = tmp(3, 4).rearrange("p (c n) -> p c n", c=FF // P)
        HS = tmp(5).rearrange("p (t d) -> p t d", t=TG)
        HS64 = tmp(5)[:, 0:TG * DZ].rearrange("p (t d) -> p t d", t=TG)
        Z64 = tmp(6)[:, 0:TG * DZ].rearrange("p (t d) -> p t d", t=TG)
        col = [ACC[:, i * EC:(i + 1) * EC] for i in range(16)]
        SRCI, DSTI = col[0].bitcast(I32), col[1].bitcast(I32)
        HII, HI, EQ, CUM, RANK = col[2].bitcast(I32), col[3], col[4], col[5], col[6]
        PAIR = [ACC[:, (7 + 2 * o) * EC:(9 + 2 * o) * EC].bitcast(I32).rearrange("p (c two) -> p c two", two=2)
                for o in range(2)]
        SLOT = [col[11 + o].bitcast(I32) for o in range(2)]
        POSA, POSB = col[13].bitcast(I32), col[14].bitcast(I32)
        Qf = Q[:, :, :].rearrange("p t d -> p (t d)")
        IOTAS, GE, ONESC = Qf[:, 0:STEPS], Qf[:, STEPS:2 * STEPS], Qf[:, 2 * STEPS:2 * STEPS + EC]
        BEFORE = Qf[:, 3000:3000 + P]
        CNT, NST, INCL, STARTS = (Qf[:, 3200 + 128 * i:3200 + 128 * i + NT] for i in range(4))
        STARTP = Qf[:, 4000:4000 + P]
        STARTT = Qf[:, 4200:4201]
        BASE = Qf[:, 4300:4300 + NT]
        NSTI = Qf[:, 4400:4400 + NT].bitcast(I32)

        R = [ctx.enter_context(nc.psum_tensor(f"R{i}", [P, 1024], F32)) for i in range(4)]
        Rt = [r[:, 0:TG * D].rearrange("p (t d) -> p t d", t=TG) for r in R]

        phase_done, passed = sem("phase_done"), sem("passed")
        phase = {}

        def end_phase(eng, key):
            n = phase[key] = phase.get(key, 0) + 1
            eng.drain().then_inc(phase_done, 1)
            eng.wait_ge(phase_done, ENGINES * n)

        MATS = ["Wn", "We1", "We2", "Wl1", "Wl2", "Wg", "W31", "W32", "Wd"]
        mat = {n: WMAT[:, i, :] for i, n in enumerate(MATS)}
        BIASES = ["bn", "be", "bl", "bg", "b31", "b32", "bd"]
        bias = {n: BIAS[:, i, :] for i, n in enumerate(BIASES)}
        L1MATS = ["Wpos", "Wq", "Wk", "Wv", "Wo"]
        l1mat = {n: WL1[:, i, :] for i, n in enumerate(L1MATS)}
        L1ROWS = ["bpos", "bdeg", "Wdeg", "bq", "bk", "bv", "bo", "ln1_g", "ln1_b", "ln2_g", "ln2_b", "b2"]
        row = {n: BL1[:, i, :] for i, n in enumerate(L1ROWS)}

        def over_tiles(b, n=TG):
            return b.unsqueeze(1).broadcast_to([P, n, b.shape[1]])

        def over_features(s, w=D):
            return s.unsqueeze(2).broadcast_to([P, s.shape[1], w])

        def over_heads(s):
            return s.unsqueeze(3).broadcast_to([P, s.shape[1], HEADS, HD])

        def heads(ap):
            return ap.rearrange("p t (h d) -> p t h d", h=HEADS)

        edges_in, x_in, w_in, w_l1, x_pad = sem("edges_in"), sem("x_in"), sem("w_in"), sem("w_l1"), sem("x_pad")
        const_ready, const_step = sem("const_ready"), sem("const_step")
        ids_cleared, list_cleared, clear_ready = sem("ids_cleared"), sem("list_cleared"), sem("clear_ready")
        sort = [dict(step=sem(f"rank_step{o}"), step2=sem(f"base_step{o}"), misc=sem(f"sort_step{o}"),
                     counts=sem(f"counts_ready{o}"), sums=sem(f"bucket_sums{o}"), startp=sem(f"starts_ready{o}"),
                     startt=sem(f"starts_transposed{o}"), ge=sem(f"reached_ready{o}"), tiles=sem(f"tiles_summed{o}"),
                     slots=sem(f"slots_ready{o}"), staged=sem(f"scatter_staged{o}"),
                     sent=[sem(f"scattered{o}_{u}") for u in range(2)], listed=sem(f"list_loaded{o}"))
                for o in range(2)]
        PASSES = ["diff", "att0", "att1", "conv", "gcn1", "gcn2"]
        once = ("oh", "tr", "oht", "exp", "prod", "att", "ex", "msg", "agg")
        names = dict(staged="indices_staged", oh="onehot_built", tr="onehot_transposed", oht="onehot_t_copied",
                     exp="rows_expanded", prod="products_ready", red="products_reduced", att="scores_ready",
                     ex="exp_ready", msg="messages_ready", agg="edges_summed", acc="sums_added")
        sems = {k: sem(v) for k, v in names.items()}
        sems["gath"] = [sem(f"gathered{u}") for u in range(2)]

        def kind_of(n):
            return "att" if n.startswith("att") else "diff" if n == "diff" else "sum"

        def counts_of(n):
            c = {k: GROUPS for k in once}
            c.update(staged=STEPS // PB, gath=16 * S4 * GROUPS // 2, acc=S4 * GROUPS, red=GROUPS)
            unused = {"att": (), "diff": ("prod", "ex"), "sum": ("tr", "oht", "exp", "prod", "red", "att", "ex", "msg")}
            c.update({k: 0 for k in unused[kind_of(n)]})
            if n == "diff":
                c["red"] = S4 * GROUPS
            return c

        ps, base = {}, dict.fromkeys(list(sems), 0)
        for n in PASSES:
            ps[n] = Events(sems)
            ps[n].base = dict(base)
            base = {k: base[k] + v for k, v in counts_of(n).items()}

        STAGES = {
            "a": "mv sd h t tc mm hp st free", "b": "mv sd cp fresh s t tc mm zt ztc z",
            "d0": "mv sd xn xt xtc pos xp pt ptc qkv kv st free att ex", "e0": "mv sd ag at atc o xn xt xtc hid gelu o2",
            "d1": "mv sd xn xt xtc pos xp pt ptc qkv kv st free att ex", "e1": "mv sd mv2 sd2 ag at atc o xn xt xtc hid gelu o2 hs st free",
            "f": "mv sd ag at atc o h ht htc mm hs st free", "g": "h ht htc mm hs st free", "h": "z zt ztc mm y sg",
        }
        meaning = dict(mv="variance_ready", sd="deviation_ready", h="h_ready", t="transposed", tc="transposed_copied", mm="product_ready", hp="table_rows",
                       st="rows_stored", free="rows_free", cp="copies_ready", fresh="copies_free", s="mean_ready",
                       zt="z_transposed", ztc="z_t_copied", z="z_ready", xn="normed_ready", xt="normed_transposed",
                       xtc="normed_t_copied", pos="pos_ready", xp="xp_ready", pt="xp_transposed", ptc="xp_t_copied",
                       qkv="qkv_ready", kv="kv_rows", att="self_scores", ex="self_exp", ag="aggregate_ready",
                       at="aggregate_transposed", atc="aggregate_t_copied", o="projected", hid="hidden_ready",
                       gelu="gelu_ready", o2="ffn_ready", hs="scaled_rows", ht="h_transposed", htc="h_t_copied",
                       y="logits_ready", sg="sigmoid_ready", steps="vector_steps")
        stage_sems = {k: sem(v) for k, v in meaning.items()}
        per_turn = dict(st=16, hid=FF // P, gelu=FF // P)
        dense, base = {}, dict.fromkeys(stage_sems, 0)
        for n, events in STAGES.items():
            dense[n] = Events(stage_sems)
            dense[n].base = dict(base)
            for k in events.split():
                base[k.rstrip("2") if k in ("mv2", "sd2") else k] += \
                    NG * per_turn.get(k, 1) + (k in ("free", "fresh"))
            base["steps"] += NG * CHAIN[n]
        dA, dB, dF, dG, dH = (dense[n] for n in "abfgh")
        dD, dE = [dense["d0"], dense["d1"]], [dense["e0"], dense["e1"]]
        deg_step, deg_sum, deg_tot = sem("deg_step"), sem("deg_sum"), sem("deg_tot")
        out_done = sem("out_done")
        dD_pre = [sem(f"bias_step{l}") for l in range(2)]
        root_in, root_out = sem("root_operand_ready"), sem("root_ready")
        ind_step = sem("indegree_step")

        block = ctx.enter_context(nc.Block())

        def per_group(eng, body):
            n = GROUPS // 4
            for u in range(4):
                body(0, u)
            with eng.Fori(1, n - 1) as it:
                for u in range(4):
                    body(it, u)
            for u in range(4):
                body(n - 1, u)

        def exists(gi):
            return not isinstance(gi, int) or gi < GROUPS

        def step_tiles(eng, o, gi):
            return [eng.value_load(TILE[o][0:1, bass.ds(gi * S4 + j, 1)], min_val=0, max_val=NT - 1)
                    for j in range(S4)]

        TABLE = {"diff": (tab_h, D), "att0": (tab_kv, 2 * D), "att1": (tab_kv, 2 * D), "conv": (tab_h, D),
                 "gcn1": (tab_h, D), "gcn2": (tab_z, DZ)}

        @block.sync
        def _(sp):
            sp.wait_ge(ids_cleared, 1)
            for ids, dst in ((a["src"], SRCI), (a["dst"], DSTI)):
                sp.dma_start(dst[0:EFULL, :], ids[0:EFULL * EC].rearrange("(p c) -> p c", c=EC)).then_inc(edges_in, 16)
                sp.dma_start(dst[EFULL:EFULL + 1, 0:EREST],
                             ids[EFULL * EC:E].rearrange("(p c) -> p c", c=EREST)).then_inc(edges_in, 16)
            sp.wait_ge(clear_ready, 1)
            for o in range(2):
                sp.dma_start(lists[o].rearrange("(p s) two -> p s two", s=STEPS), EL[o][:, :, :])\
                    .then_inc(list_cleared, 16)
            sp.wait_ge(x_pad, 1)
            sp.dma_start(X[:, 0:NT - 1, :], a["x"][0:(NT - 1) * P, :].rearrange("(t p) d -> p t d", p=P))\
                .then_inc(x_in, 16)
            sp.dma_start(X[0:LAST, NT - 1, :], a["x"][(NT - 1) * P:N, :]).then_inc(x_in, 16)
            for o in range(2):
                for u in range(2):
                    sp.wait_ge(sort[o]["sent"][u], 16 * EC // 2)
                sp.dma_start(EL[o][:, :, :], lists[o].rearrange("(p s) two -> p s two", s=STEPS))\
                    .then_inc(sort[o]["listed"], 16)
            end_phase(sp, "sp")

            def store(table, src, s, ready):
                view = table.rearrange("(t p) d -> p t d", p=P)
                sp.sem_inc(s["free"])
                with sp.Fori(0, NG) as g:
                    wait(sp, s, ready, g + 1)
                    sp.dma_start(view[:, bass.ds(g * TG, TG), :], src).then_inc(s["st"], 16)
                    wait(sp, s, "st", (g + 1) * 16)
                    sp.sem_inc(s["free"])

            def load_l1(l):
                for n in L1MATS:
                    sp.dma_start(l1mat[n], a[n][l]).then_inc(w_l1, 16)
                for n in L1ROWS:
                    v = a[n][l, 0] if n == "Wdeg" else a[n][l]
                    sp.dma_start(row[n], v.partition_broadcast(P)).then_inc(w_l1, 16)
                sp.dma_start(WF1[:, :], a["W1"][l]).then_inc(w_l1, 16)
                sp.dma_start(WF2[:, :, :], a["W2"][l].rearrange("(c k) d -> k c d", k=P)).then_inc(w_l1, 16)
                sp.dma_start(B1T[:, :], a["b1t"][l]).then_inc(w_l1, 16)

            load_l1(0)
            store(tab_h, HS[:, :, :], dA, "hp")
            end_phase(sp, "sp")
            end_phase(sp, "sp")
            end_phase(sp, "sp")
            for l in range(2):
                store(tab_kv, KV[:, :, :], dD[l], "kv")
                end_phase(sp, "sp")
                end_phase(sp, "sp")
                if l == 1:
                    store(tab_h, XP[:, :, :], dE[l], "hs")
                end_phase(sp, "sp")
                if l == 0:
                    load_l1(1)
            end_phase(sp, "sp")
            store(tab_h, HS[:, :, :], dF, "hs")
            end_phase(sp, "sp")
            end_phase(sp, "sp")
            store(tab_z, HS64[:, :, :], dG, "hs")
            end_phase(sp, "sp")
            end_phase(sp, "sp")
            end_phase(sp, "sp")
            sp.dma_start(out[0:(NT - 1) * P, :].rearrange("(t p) d -> p t d", p=P), X[:, 0:NT - 1, :])\
                .then_inc(out_done, 16)
            sp.dma_start(out[(NT - 1) * P:N, :], X[0:LAST, NT - 1, :]).then_inc(out_done, 16)
            sp.wait_ge(out_done, 32)

        @block.gpsimd
        def _(pool):
            n = [0]

            def step(ins):
                n[0] += 1
                ins.then_inc(const_step, 1)
                pool.wait_ge(const_step, n[0])

            nc.gpsimd.memset(IDENT[:, :], 0.0)
            nc.gpsimd.memset(ONES[:, :], 1.0)
            nc.gpsimd.memset(ZERO[:, :], 0.0)
            nc.gpsimd.memset(EPS[:, :], 1e-5)
            nc.gpsimd.memset(ONESC, 1.0)
            nc.gpsimd.memset(MASK, 1.0)
            step(nc.gpsimd.memset(BEFORE, 1.0))
            step(nc.gpsimd.iota(IOTA[:, :], [[1, P]], base=0, channel_multiplier=0,
                                allow_small_or_imprecise_dtypes=True))
            step(nc.gpsimd.iota(IOTAS, [[1, STEPS]], base=0, channel_multiplier=0,
                                allow_small_or_imprecise_dtypes=True))
            step(nc.gpsimd.affine_select(out=IDENT[:, :], in_=IDENT[:, :], compare_op=ALU.not_equal, fill=1.0,
                                         base=0, pattern=[[-1, P]], channel_multiplier=1))
            step(nc.gpsimd.affine_select(out=BEFORE, in_=BEFORE, compare_op=ALU.is_gt, fill=0.0,
                                         base=0, pattern=[[1, P]], channel_multiplier=-1))
            nc.gpsimd.affine_select(out=MASK, in_=MASK, compare_op=ALU.is_gt, fill=0.0,
                                    base=N, pattern=[[-P, NT]], channel_multiplier=-1).then_inc(const_ready, 1)

            pool.wait_ge(list_cleared, 32)
            for o in range(2):
                s = sort[o]
                pool.wait_ge(s["slots"], 1)

                def scatter(b, it, u, first):
                    if not first:
                        pool.wait_ge(s["sent"][u], it * (16 * SB))
                        gated(pool, passed)
                    elif o == 1:
                        for v in range(2):
                            pool.wait_ge(sort[0]["sent"][v], 16 * EC // 2)
                    nc.gpsimd.tensor_copy(PAIRS[:, u, :, :], PAIR[o][:, bass.ds(b * SB, SB), :])
                    nc.gpsimd.tensor_copy(STAGE[:, u, :], SLOT[o][:, bass.ds(b * SB, SB)]).then_inc(s["staged"], 1)
                    pool.wait_ge(s["staged"], b + 1)
                    gated(pool, passed)
                    for j in range(SB):
                        nc.gpsimd.indirect_dma_start(
                            lists[o], bass.IndirectOffsetOnAxis(STAGE[:, u, j:j + 1], 0), PAIRS[:, u, j, :], None,
                            bounds_check=P * STEPS - 1, oob_is_err=False).then_inc(s["sent"][u], 16)

                for u in range(2):
                    scatter(u, 0, u, True)
                with pool.Fori(1, EC // SB // 2) as it:
                    for u in range(2):
                        scatter(it * 2 + u, it, u, False)
            end_phase(pool, "pool")
            end_phase(pool, "pool")

            def gathers(name, o):
                s, kind = ps[name], kind_of(name)
                table, w = TABLE[name]
                freed = "msg" if kind == "att" else "agg"

                def half(b, it, u, first):
                    if not (first and u < 2 and it == 0 and b < 2):
                        wait(pool, s, freed, b * (PB // S4) - PB // S4)
                        gated(pool, passed)
                    nc.gpsimd.tensor_copy(STAGE[:, u, 0:PB], EL[o][:, bass.ds(b * PB, PB), 0]).then_inc(s["staged"], 1)
                    wait(pool, s, "staged", b + 1)
                    gated(pool, passed)
                    for q in range(PB // S4):
                        r = q % 2
                        if not (first and b == 0 and q < 2):
                            wait(pool, s, freed, b * (PB // S4) + (q - 1))
                            gated(pool, passed)
                        for j in range(S4):
                            nc.gpsimd.indirect_dma_start(
                                G[:, r, j, 0:w], None, table,
                                bass.IndirectOffsetOnAxis(STAGE[:, u, q * S4 + j:q * S4 + j + 1], 0))\
                                .then_inc(s["gath"][r], 16)

                for u in range(2):
                    half(u, 0, u, True)
                with pool.Fori(1, STEPS // PB // 2) as it:
                    for u in range(2):
                        half(it * 2 + u, it, u, False)
                end_phase(pool, "pool")

            gathers("diff", 0)
            with pool.Fori(0, NG) as g:
                wait(pool, dB, "fresh", g + 1)
                gated(pool, passed)
                nc.gpsimd.tensor_copy(KV[:, :, :], accv[AW][:, bass.ds(g * TG, TG), :])
                nc.gpsimd.tensor_copy(XP[:, :, :], Y[:, bass.ds(g * TG, TG), :]).then_inc(dB["cp"], 1)
            end_phase(pool, "pool")
            for l in range(2):
                end_phase(pool, "pool")
                gathers(f"att{l}", 1)
                end_phase(pool, "pool")
            gathers("conv", 1)
            end_phase(pool, "pool")
            gathers("gcn1", 1)
            end_phase(pool, "pool")
            gathers("gcn2", 1)
            end_phase(pool, "pool")

        @block.tensor
        def _(pe):
            pe.wait_ge(const_ready, 1)
            for o in range(2):
                s = sort[o]
                pe.wait_ge(s["counts"], 1)
                nc.tensor.matmul(R[0][:, 0:NT], BEFORE, CNT, start=True, stop=True)
                nc.tensor.matmul(R[0][:, 512:512 + NT], ONES[:, :], CNT, start=True, stop=True).then_inc(s["sums"], 1)
                pe.wait_ge(s["startp"], 1)
                nc.tensor.transpose(R[1][:, 0:P], STARTP, IDENT[:, :]).then_inc(s["startt"], 1)
                pe.wait_ge(s["ge"], 1)
                h = STEPS // 2
                nc.tensor.matmul(R[2][:, 0:h], ONES[:, :], GE[:, 0:h], start=True, stop=True)
                nc.tensor.matmul(R[2][:, 512:512 + h], ONES[:, :], GE[:, h:STEPS], start=True, stop=True)\
                    .then_inc(s["tiles"], 1)
            end_phase(pe, "pe")

            def transposes(dst, src, sig, w=D):
                for j in range(TG):
                    ins = nc.tensor.transpose(dst[0:w, j * P:(j + 1) * P], src(j), IDENT[:, :])
                if sig is not None:
                    ins.then_inc(sig, 1)

            def products(dst, pairs, sig):
                for j in range(TG):
                    for k, (t, w) in enumerate(pairs):
                        ins = nc.tensor.matmul(dst[:, j, :], t(j), w, start=k == 0, stop=k == len(pairs) - 1)
                if sig is not None:
                    ins.then_inc(sig, 1)

            def tile_of(t, k=P):
                return lambda j: t[0:k, j * P:(j + 1) * P]

            pe.wait_ge(w_in, 16 * (len(MATS) + len(BIASES)))
            with pe.Fori(0, NG) as g:
                wait(pe, dA, "h", g + 1)
                transposes(R[0], lambda j: XN[:, j, :], dA["t"])
                wait(pe, dA, "tc", g + 1)
                products(Rt[1], [(tile_of(T1), mat["Wn"])], dA["mm"])
            end_phase(pe, "pe")

            def edge_pass(name, o):
                s, kind = ps[name], kind_of(name)
                w = {"att": L1W, "diff": D}.get(kind, TABLE[name][1])

                def transpose(it, u):
                    gi = it * 4 + u
                    wait(pe, s, "oh", gi + 1)
                    wait(pe, s, "oht", gi - 1)
                    for j in range(S4):
                        ins = nc.tensor.transpose(R[0][:, (u % 2) * 512 + j * P:(u % 2) * 512 + (j + 1) * P],
                                                  OH[:, u % 4, j, :], IDENT[:, :])
                    ins.then_inc(s["tr"], 1)

                def expand(it, u):
                    gi = it * 4 + u
                    tiles = step_tiles(pe, o, gi)
                    wait(pe, s, "oht", gi + 1)
                    wait(pe, s, "att", gi - 1)
                    for j in range(S4):
                        ins = nc.tensor.matmul(R[1][:, (u % 2) * 512 + j * P:(u % 2) * 512 + (j + 1) * P],
                                               OHT[:, u % 2, j, :], Qf[:, bass.ds(tiles[j] * D, D)],
                                               start=True, stop=True)
                    ins.then_inc(s["exp"], 1)

                def summed(it, u):
                    gi = it * 4 + u
                    wait(pe, s, "oh", gi + 1)
                    if kind != "sum":
                        wait(pe, s, "msg", gi + 1)
                    if kind != "att":
                        wait(pe, s, "gath", (it * 2 + u // 2 + 1) * (16 * S4), u % 2)
                    wait(pe, s, "acc", gi * S4)
                    for j in range(S4):
                        oh = OH[:, u % 4, j, :]
                        dst = R[2][:, j * 256:j * 256 + w]
                        if kind == "att":
                            ins = nc.tensor.matmul(dst, oh, M[:, u % 2, j, :], start=True, stop=True)
                        else:
                            ins = nc.tensor.matmul(dst, oh, G[:, u % 2, j, 0:w], start=True, stop=True)
                        if kind == "diff":
                            nc.tensor.matmul(R[2][:, j * 256 + D:j * 256 + 2 * D], oh, M[:, u % 2, j, 0:D],
                                             start=True, stop=True)
                            ins = nc.tensor.matmul(R[3][:, j:j + 1], oh, ONES[:, 0:1], start=True, stop=True)
                    ins.then_inc(s["agg"], 1)

                def body(it, u):
                    gi = it * 4 + u
                    if kind != "sum":
                        if exists(gi + 2):
                            transpose(it if u < 2 else it + 1, (u + 2) % 4)
                        if exists(gi + 1):
                            expand(it if u < 3 else it + 1, (u + 1) % 4)
                    summed(it, u)

                if kind != "sum":
                    transpose(0, 0)
                    transpose(0, 1)
                    expand(0, 0)
                per_group(pe, body)
                end_phase(pe, "pe")

            edge_pass("diff", 0)

            pe.sem_inc(dB["fresh"])
            with pe.Fori(0, NG) as g:
                wait(pe, dB, "cp", g + 1)
                transposes(R[0], lambda j: KV[:, j, 0:D], None)
                transposes(R[1], lambda j: KV[:, j, D:2 * D], None)
                transposes(R[2], lambda j: XP[:, j, :], dB["t"])
                wait(pe, dB, "tc", g + 1)
                products(Rt[3], [(tile_of(T1), mat["We1"]), (tile_of(T2), mat["We2"])], dB["mm"])
                wait(pe, dB, "s", g + 1)
                transposes(R[0], lambda j: XN[:, j, :], dB["zt"])
                wait(pe, dB, "ztc", g + 1)
                products(Rt[1], [(tile_of(T3), mat["Wl1"]), (tile_of(T1), mat["Wl2"])], dB["z"])
                wait(pe, dB, "steps", (g + 1) * CHAIN["b"])
                pe.sem_inc(dB["fresh"])
            pe.wait_ge(deg_sum, 1)
            nc.tensor.matmul(R[0][:, 0:1], ONES[:, :], SMALL[:, 0:1], start=True, stop=True).then_inc(deg_tot, 1)
            end_phase(pe, "pe")

            for l in range(2):
                s = dD[l]
                pe.wait_ge(w_l1, 16 * (len(L1MATS) + len(L1ROWS) + 3) * (l + 1))
                with pe.Fori(0, NG) as g:
                    wait(pe, s, "xn", g + 1)
                    transposes(R[0], lambda j: XN[:, j, :], s["xt"])
                    wait(pe, s, "xtc", g + 1)
                    products(Rt[1], [(tile_of(T1), l1mat["Wpos"])], s["pos"])
                    wait(pe, s, "xp", g + 1)
                    transposes(R[0], lambda j: XP[:, j, :], s["pt"])
                    wait(pe, s, "ptc", g + 1)
                    products(Rt[1], [(tile_of(T1), l1mat["Wq"])], None)
                    products(Rt[2], [(tile_of(T1), l1mat["Wk"])], None)
                    products(Rt[3], [(tile_of(T1), l1mat["Wv"])], s["qkv"])
                end_phase(pe, "pe")
                edge_pass(f"att{l}", 1)
                s = dE[l]
                with pe.Fori(0, NG) as g:
                    wait(pe, s, "ag", g + 1)
                    transposes(R[0], lambda j: XN[:, j, :], s["at"])
                    wait(pe, s, "atc", g + 1)
                    products(Rt[1], [(tile_of(T1), l1mat["Wo"])], s["o"])
                    wait(pe, s, "xn", g + 1)
                    transposes(R[0], lambda j: XN[:, j, :], s["xt"])
                    wait(pe, s, "xtc", g + 1)
                    half = TG * P // 2
                    for c in range(FF // P):
                        if c >= 2:
                            wait(pe, s, "gelu", g * (FF // P) + (c - 1))
                        for k in range(2):
                            ins = nc.tensor.matmul(R[2 + c % 2][:, k * 512:k * 512 + half],
                                                   WF1[:, c * P:(c + 1) * P], T1[:, k * half:(k + 1) * half],
                                                   start=True, stop=True)
                        ins.then_inc(s["hid"], 1)
                    wait(pe, s, "gelu", (g + 1) * (FF // P))
                    products(Rt[0], [((lambda j, c=c: HT[:, c, j * P:(j + 1) * P]), WF2[:, c, :])
                                     for c in range(FF // P)], s["o2"])
                end_phase(pe, "pe")
            edge_pass("conv", 1)
            with pe.Fori(0, NG) as g:
                wait(pe, dF, "ag", g + 1)
                transposes(R[0], lambda j: XN[:, j, :], dF["at"])
                wait(pe, dF, "atc", g + 1)
                products(Rt[1], [(tile_of(T1), mat["Wg"])], dF["o"])
                wait(pe, dF, "h", g + 1)
                transposes(R[0], lambda j: XN[:, j, :], dF["ht"])
                wait(pe, dF, "htc", g + 1)
                products(Rt[1], [(tile_of(T1), mat["W31"])], dF["mm"])
            end_phase(pe, "pe")
            edge_pass("gcn1", 1)
            with pe.Fori(0, NG) as g:
                wait(pe, dG, "h", g + 1)
                transposes(R[0], lambda j: XN[:, j, :], dG["ht"])
                wait(pe, dG, "htc", g + 1)
                products(R[1][:, 0:TG * DZ].rearrange("p (t d) -> p t d", t=TG),
                         [(tile_of(T1), mat["W32"][:, 0:DZ])], dG["mm"])
            end_phase(pe, "pe")
            edge_pass("gcn2", 1)
            with pe.Fori(0, NG) as g:
                wait(pe, dH, "z", g + 1)
                gated(pe, passed)
                transposes(R[0], lambda j: Z64[:, j, :], dH["zt"], DZ)
                wait(pe, dH, "ztc", g + 1)
                products(Rt[1], [(tile_of(T1, DZ), mat["Wd"][0:DZ, :])], dH["mm"])
            end_phase(pe, "pe")

        @block.scalar
        def _(act):
            for n in MATS:
                v = a[n]
                act.dma_start(mat[n][0:v.shape[0], 0:v.shape[1]], v).then_inc(w_in, 16)
            for n in BIASES:
                v = a[n]
                act.dma_start(bias[n][:, 0:v.shape[0]], v.partition_broadcast(P)).then_inc(w_in, 16)
            end_phase(act, "act")

            def copied(dst, src, s, ready, done, g, k=P):
                wait(act, s, ready, g + 1)
                nc.scalar.activation(dst[0:k, :], src[0:k, 0:TG * D], ACT.Copy).then_inc(s[done], 1)

            def deviation(s, g, of=1, k=0):
                wait(act, s, "mv", g * of + (k + 1))
                nc.scalar.activation(SD[:, :], MV[:, :, 1], ACT.Sqrt, bias=EPS[:, 0:1]).then_inc(s["sd"], 1)

            with act.Fori(0, NG) as g:
                deviation(dA, g)
                copied(T1, R[0], dA, "t", "tc", g)
            end_phase(act, "act")

            def edge_pass(name):
                s, kind = ps[name], kind_of(name)

                def copy(it, u):
                    gi = it * 4 + u
                    wait(act, s, "tr", gi + 1)
                    wait(act, s, "exp", gi - 1)
                    nc.scalar.activation(OHT[:, u % 2, :, :].rearrange("p s w -> p (s w)"),
                                         R[0][:, (u % 2) * 512:(u % 2) * 512 + 512], ACT.Copy).then_inc(s["oht"], 1)

                def body(it, u):
                    gi = it * 4 + u
                    if exists(gi + 2):
                        copy(it if u < 2 else it + 1, (u + 2) % 4)
                    wait(act, s, "att", gi + 1)
                    if kind == "att":
                        wait(act, s, "agg", gi - 1)
                        nc.scalar.activation(M[:, u % 2, :, D:D + HEADS], EATT[:, :, :], ACT.Exp)\
                            .then_inc(s["ex"], 1)
                    else:
                        nc.scalar.activation(M[:, u % 2, :, 0:D], PROD[:, :, :], ACT.Abs).then_inc(s["msg"], 1)

                if kind != "sum":
                    copy(0, 0)
                    copy(0, 1)
                    per_group(act, body)
                end_phase(act, "act")

            edge_pass("diff")
            with act.Fori(0, NG) as g:
                wait(act, dB, "t", g + 1)
                nc.scalar.activation(T1, R[0][:, 0:TG * D], ACT.Copy)
                nc.scalar.activation(T2, R[1][:, 0:TG * D], ACT.Copy)
                nc.scalar.activation(T3, R[2][:, 0:TG * D], ACT.Copy).then_inc(dB["tc"], 1)
                copied(T1, R[0], dB, "zt", "ztc", g)
                deviation(dB, g)
            act.wait_ge(root_in, 1)
            nc.scalar.activation(SMALL[:, 1:2], R[0][:, 0:1], ACT.Sqrt, scale=1.0 / (N - 1)).then_inc(root_out, 1)
            act.wait_ge(root_in, 2)
            nc.scalar.activation(RO, RO, ACT.Sqrt).then_inc(root_out, 1)
            end_phase(act, "act")
            for l in range(2):
                s = dD[l]
                with act.Fori(0, NG) as g:
                    deviation(s, g)
                    copied(T1, R[0], s, "xt", "xtc", g)
                    copied(T1, R[0], s, "pt", "ptc", g)
                    wait(act, s, "att", g + 1)
                    nc.scalar.activation(EX[:, :, :], ATT[:, :, :], ACT.Exp).then_inc(s["ex"], 1)
                end_phase(act, "act")
                edge_pass(f"att{l}")
                if l == 0:
                    act.wait_ge(root_in, 3)
                    nc.scalar.activation(NODE[:, 4:6, :], NODE[:, 4:6, :], ACT.Sqrt).then_inc(root_out, 1)
                s = dE[l]
                with act.Fori(0, NG) as g:
                    copied(T1, R[0], s, "at", "atc", g)
                    deviation(s, g, 1 + l)
                    copied(T1, R[0], s, "xt", "xtc", g)
                    half = TG * P // 2
                    for c in range(FF // P):
                        wait(act, s, "hid", g * (FF // P) + (c + 1))
                        nc.scalar.activation(HT[:, c, :].rearrange("p (k n) -> p k n", k=2),
                                             R[2 + c % 2][:, :].rearrange("p (k n) -> p k n", k=2)[:, :, 0:half],
                                             ACT.Gelu, bias=B1T[:, c:c + 1]).then_inc(s["gelu"], 1)
                    if l == 1:
                        deviation(s, g, 2, 1)
                end_phase(act, "act")
            edge_pass("conv")
            with act.Fori(0, NG) as g:
                copied(T1, R[0], dF, "at", "atc", g)
                deviation(dF, g)
                copied(T1, R[0], dF, "ht", "htc", g)
            end_phase(act, "act")
            edge_pass("gcn1")
            with act.Fori(0, NG) as g:
                copied(T1, R[0], dG, "ht", "htc", g)
            end_phase(act, "act")
            edge_pass("gcn2")
            with act.Fori(0, NG) as g:
                copied(T1, R[0], dH, "zt", "ztc", g, DZ)
                wait(act, dH, "y", g + 1)
                nc.scalar.activation(XP[:, :, :], XN[:, :, :], ACT.Sigmoid).then_inc(dH["sg"], 1)
            end_phase(act, "act")

        @block.vector
        def _(dve):
            V = nc.vector

            def copied(dst, src):
                return V.tensor_scalar(dst, src, 0.0, None, ALU.add)

            V.memset(SRCI, NT * P)
            V.memset(DSTI, NT * P).then_inc(ids_cleared, 1)
            for o in range(2):
                V.memset(EL[o][:, :, 0], 0)
                ins = V.memset(EL[o][:, :, 1], -1)
            ins.then_inc(clear_ready, 1)
            V.memset(X[:, NT - 1, :], 0.0).then_inc(x_pad, 1)
            dve.wait_ge(const_ready, 1)
            dve.wait_ge(edges_in, 64)

            for o, (key, val) in enumerate(((SRCI, DSTI), (DSTI, SRCI))):
                s = sort[o]
                m = Chain(dve, s["misc"], 100)
                m.turn(0)
                V.tensor_copy(PAIR[o][:, :, 0], val)
                V.tensor_single_scalar(PAIR[o][:, :, 1], key, P - 1, ALU.bitwise_and)
                m.link(V.tensor_single_scalar(HII, key, P.bit_length() - 1, ALU.logical_shift_right))
                V.tensor_copy(HI, HII)
                m.link(V.memset(RANK, 0.0))
                c = Chain(dve, s["step"], 5)
                with dve.Fori(0, NT) as h:
                    c.turn(h)
                    c.link(V.tensor_scalar(EQ, HI, IOTA[:, bass.ds(h, 1)], None, ALU.is_equal))
                    c.link(V.tensor_tensor_scan(CUM, ONESC, EQ, 0.0, ALU.mult, ALU.add))
                    c.link(V.tensor_tensor(EQ, EQ, CUM, ALU.mult))
                    c.link(V.tensor_tensor(RANK, RANK, EQ, ALU.add))
                    c.link(copied(CNT[:, bass.ds(h, 1)], CUM[:, EC - 1:EC]))
                    c.end()
                V.memset(STARTP, 1e9).then_inc(s["counts"], 1)
                dve.wait_ge(s["sums"], 1)
                m.link(V.tensor_scalar(NSTI, R[0][:, 512:512 + NT], float(P - 1), None, ALU.add))
                m.link(V.tensor_single_scalar(NSTI, NSTI, P.bit_length() - 1, ALU.logical_shift_right))
                m.link(V.tensor_copy(NST, NSTI))
                m.link(V.tensor_tensor_scan(INCL, ONESC[:, 0:NT], NST, 0.0, ALU.mult, ALU.add))
                m.link(V.tensor_tensor(STARTS, INCL, NST, ALU.subtract))
                V.tensor_copy(STARTP[:, 0:NT], STARTS).then_inc(s["startp"], 1)
                m.link(V.scalar_tensor_tensor(BASE, STARTS, float(P), R[0][:, 0:NT], ALU.mult, ALU.add))
                dve.wait_ge(s["startt"], 1)
                m.link(V.tensor_copy(STARTT, R[1][:, 0:1]))
                V.tensor_scalar(GE, IOTAS, STARTT, None, ALU.is_ge).then_inc(s["ge"], 1)
                c = Chain(dve, s["step2"], 2)
                with dve.Fori(0, NT) as h:
                    c.turn(h)
                    c.link(V.tensor_scalar(EQ, HI, IOTA[:, bass.ds(h, 1)], BASE[:, bass.ds(h, 1)],
                                           ALU.is_equal, ALU.mult))
                    c.link(V.tensor_tensor(RANK, RANK, EQ, ALU.add))
                    c.end()
                dve.wait_ge(s["tiles"], 1)
                half = STEPS // 2
                for k in range(2):
                    m.link(V.tensor_scalar(TILE[o][0:1, k * half:(k + 1) * half], R[2][0:1, k * 512:k * 512 + half],
                                           -1.0, None, ALU.add))
                m.link(V.tensor_scalar(HII, RANK, -1.0, None, ALU.add))
                V.tensor_single_scalar(POSA, HII, P - 1, ALU.bitwise_and)
                m.link(V.tensor_single_scalar(POSB, HII, P.bit_length() - 1, ALU.arith_shift_right))
                m.link(V.tensor_scalar(EQ, HI, float(NT), float(OUT_OF_RANGE), ALU.is_equal, ALU.mult))
                m.link(V.scalar_tensor_tensor(CUM, POSA, float(STEPS), POSB, ALU.mult, ALU.add))
                V.tensor_tensor(SLOT[o], CUM, EQ, ALU.add).then_inc(s["slots"], 1)
                dve.wait_ge(s["slots"], 1)
            for o in range(2):
                dve.wait_ge(sort[o]["listed"], 16)
                V.tensor_copy(LO[o][:, :], EL[o][:, :, 1])
            end_phase(dve, "dve")

            def layer_norm(c, s, g, src, dst, of=1, k=0):
                gated(dve, passed)
                for j in range(TG):
                    ins = V.bn_stats(ST[:, j, :], src(j))
                c.link(ins)
                gated(dve, passed)
                for j in range(TG):
                    ins = V.bn_aggr(MV[:, j, :], ST[:, j, :])
                ins.then_inc(s["mv"], 1)
                wait(dve, s, "sd", g * of + (k + 1))
                c.link(V.reciprocal(RSTD[:, :], SD[:, :]))
                for j in range(TG):
                    ins = V.tensor_scalar(dst[:, j, :], src(j), MV[:, j, 0:1], RSTD[:, j:j + 1],
                                          ALU.subtract, ALU.mult)
                c.link(ins)

            def turn_of(t, g):
                return t[:, bass.ds(g * TG, TG), :]

            def tile_in(t, g):
                return lambda j: t[:, bass.ds(g * TG + j, 1), :].rearrange("p t d -> p (t d)")

            def signal(ins, s, what, g):
                ins.then_inc(s[what], 1)
                wait(dve, s, what, g + 1)

            dve.wait_ge(x_in, 32)
            dve.wait_ge(w_in, 16 * (len(MATS) + len(BIASES)))
            c = Chain(dve, dA["steps"], CHAIN["a"], dA.base["steps"])
            with dve.Fori(0, NG) as g:
                c.turn(g)
                layer_norm(c, dA, g, tile_in(X, g), XN)
                signal(V.tensor_scalar(XN[:, :, :], XN[:, :, :], 0.0, None, ALU.max), dA, "h", g)
                c.link(copied(turn_of(Y, g), XN[:, :, :]))
                wait(dve, dA, "mm", g + 1)
                wait(dve, dA, "free", g + 1)
                signal(V.tensor_tensor(HS[:, :, :], Rt[1], over_tiles(bias["bn"]), ALU.add), dA, "hp", g)
                c.link(copied(turn_of(Q, g), HS[:, :, :]))
                c.end()
            V.memset(ACC[:, :], 0.0)
            V.memset(OUTD, 0.0)
            end_phase(dve, "dve")

            def edge_pass(name, o):
                s, kind = ps[name], kind_of(name)
                w = {"att": L1W, "diff": AW}.get(kind, TABLE[name][1])
                per = S4 * (2 if kind == "diff" else 1)

                def onehot(it, u):
                    gi = it * 4 + u
                    V.tensor_tensor(OH[:, u % 4, :, :], over_tiles(IOTA[:, :], S4),
                                    over_features(LO[o][:, bass.ds(gi * S4, S4)]), ALU.is_equal)\
                        .then_inc(s["oh"], 1)

                def add(it, u):
                    gi = it * 4 + u
                    tiles = step_tiles(dve, o, gi)
                    wait(dve, s, "agg", gi + 1)
                    for j in range(S4):
                        wait(dve, s, "acc", gi * S4 + j)
                        dst = ACC[:, bass.ds(tiles[j] * w, w)]
                        if kind == "diff":
                            d2 = OUTD[:, bass.ds(tiles[j], 1)]
                            wait(dve, s, "red", gi * S4 + j)
                            V.tensor_tensor(d2, d2, R[3][:, j:j + 1], ALU.add).then_inc(s["red"], 1)
                        V.tensor_tensor(dst, dst, R[2][:, j * 256:j * 256 + w], ALU.add).then_inc(s["acc"], 1)

                def before(it, u):
                    return (it, u - 1) if u else (it - 1, 3)

                def body(it, u):
                    gi = it * 4 + u
                    if kind != "sum":
                        wait(dve, s, "exp", gi + 1)
                        wait(dve, s, "gath", (it * 2 + u // 2 + 1) * (16 * S4), u % 2)
                    if kind == "diff":
                        wait(dve, s, "msg", gi)
                        V.tensor_tensor(PROD[:, :, :], R[1][:, (u % 2) * 512:(u % 2) * 512 + 512]
                                        .rearrange("p (s w) -> p s w", s=S4), G[:, u % 2, :, 0:D], ALU.subtract)\
                            .then_inc(s["att"], 1)
                    if kind == "att":
                        V.tensor_tensor(PROD[:, :, :], R[1][:, (u % 2) * 512:(u % 2) * 512 + 512]
                                        .rearrange("p (s w) -> p s w", s=S4), G[:, u % 2, :, 0:D], ALU.mult)\
                            .then_inc(s["prod"], 1)
                        wait(dve, s, "prod", gi + 1)
                        wait(dve, s, "ex", gi)
                        V.tensor_reduce(EATT[:, :, :], heads(PROD[:, :, :]), AX.X, ALU.add).then_inc(s["red"], 1)
                        wait(dve, s, "red", gi + 1)
                        V.tensor_scalar(EATT[:, :, :], EATT[:, :, :], -50.0, 50.0, ALU.max, ALU.min)\
                            .then_inc(s["att"], 1)
                    if not (isinstance(gi, int) and gi == 0):
                        add(*before(it, u))
                    if kind == "att":
                        wait(dve, s, "ex", gi + 1)
                        V.tensor_tensor(heads(M[:, u % 2, :, 0:D]), heads(G[:, u % 2, :, D:2 * D]),
                                        over_heads(M[:, u % 2, :, D:D + HEADS]), ALU.mult).then_inc(s["msg"], 1)
                    if exists(gi + 3):
                        onehot(it if u < 1 else it + 1, (u + 3) % 4)

                if kind == "att":
                    V.memset(M[:, :, :, D + HEADS:L1W], 1.0)
                for u in range(3):
                    onehot(0, u)
                per_group(dve, body)
                add(GROUPS // 4 - 1, 3)
                end_phase(dve, "dve")

            edge_pass("diff", 0)

            c = Chain(dve, dB["steps"], CHAIN["b"], dB.base["steps"])
            with dve.Fori(0, NG) as g:
                c.turn(g)
                copied(CT[:, 0, :], OUTD[:, bass.ds(g * TG, TG)])
                c.link(V.tensor_scalar(CT[:, 1, :], OUTD[:, bass.ds(g * TG, TG)], 1.0, None, ALU.max))
                c.link(V.reciprocal(CT[:, 1, :], CT[:, 1, :]))
                wait(dve, dB, "mm", g + 1)
                for j in range(TG):
                    ins = V.scalar_tensor_tensor(XN[:, j, :], bias["be"], CT[:, 0, j:j + 1], Rt[3][:, j, :],
                                                 ALU.mult, ALU.add)
                c.link(ins)
                c.link(V.tensor_tensor(XN[:, :, :], XN[:, :, :], turn_of(Q, g), ALU.add))
                signal(V.tensor_tensor(XN[:, :, :], XN[:, :, :], over_features(CT[:, 1, :]), ALU.mult), dB, "s", g)
                wait(dve, dB, "z", g + 1)
                c.link(V.tensor_tensor(XN[:, :, :], Rt[1], over_tiles(bias["bl"]), ALU.add))
                c.link(V.tensor_tensor(turn_of(X, g), turn_of(X, g), XN[:, :, :], ALU.add))
                layer_norm(c, dB, g, tile_in(X, g), XN)
                c.link(V.tensor_scalar(turn_of(Y, g), XN[:, :, :], 0.0, None, ALU.max))
                c.end()
            mean = (E + N) / N
            c = Chain(dve, deg_step, 100)
            c.turn(0)
            c.link(V.tensor_scalar(DEGN, OUTD, 1.0, -mean, ALU.add, ALU.add))
            c.link(V.tensor_tensor(TMPN, DEGN, MASK, ALU.mult))
            c.link(V.tensor_tensor(TMPN, TMPN, TMPN, ALU.mult))
            V.tensor_reduce(SMALL[:, 0:1], TMPN, AX.X, ALU.add).then_inc(deg_sum, 1)
            dve.wait_ge(deg_tot, 1)
            V.tensor_scalar(RO, OUTD, 1.0, None, ALU.max).then_inc(root_in, 2)
            dve.wait_ge(root_out, 2)
            c.link(V.tensor_scalar(SMALL[:, 2:3], SMALL[:, 1:2], 1e-6, None, ALU.add))
            c.link(V.reciprocal(SMALL[:, 3:4], SMALL[:, 2:3]))
            c.link(V.tensor_scalar(DEGN, DEGN, SMALL[:, 3:4], None, ALU.mult))
            c.link(V.reciprocal(RO, RO))
            end_phase(dve, "dve")

            for l in range(2):
                s = dD[l]
                dve.wait_ge(w_l1, 16 * (len(L1MATS) + len(L1ROWS) + 3) * (l + 1))
                c = Chain(dve, dD_pre[l], 2)
                c.turn(0)
                c.link(V.tensor_tensor(row["bpos"], row["bpos"], row["bdeg"], ALU.add))
                c.link(V.tensor_scalar(row["bq"], row["bq"], float(HD) ** -0.5, None, ALU.mult))
                c = Chain(dve, s["steps"], CHAIN[f"d{l}"], s.base["steps"])
                with dve.Fori(0, NG) as g:
                    c.turn(g)
                    layer_norm(c, s, g, tile_in(Y, g), XN)
                    c.link(V.tensor_tensor(XN[:, :, :], XN[:, :, :], over_tiles(row["ln1_g"]), ALU.mult))
                    signal(V.tensor_tensor(XN[:, :, :], XN[:, :, :], over_tiles(row["ln1_b"]), ALU.add), s, "xn", g)
                    copied(CT[:, 0, :], DEGN[:, bass.ds(g * TG, TG)])
                    wait(dve, s, "pos", g + 1)
                    c.link(V.tensor_tensor(XP[:, :, :], Rt[1], over_tiles(row["bpos"]), ALU.add))
                    for j in range(TG):
                        ins = V.scalar_tensor_tensor(XP[:, j, :], row["Wdeg"], CT[:, 0, j:j + 1], XP[:, j, :],
                                                     ALU.mult, ALU.add)
                    c.link(ins)
                    signal(V.tensor_tensor(XP[:, :, :], XP[:, :, :], XN[:, :, :], ALU.add), s, "xp", g)
                    wait(dve, s, "qkv", g + 1)
                    c.link(V.scalar_tensor_tensor(turn_of(Q, g), Rt[1], float(HD) ** -0.5, over_tiles(row["bq"]),
                                                  ALU.mult, ALU.add))
                    wait(dve, s, "free", g + 1)
                    c.link(V.tensor_tensor(KV[:, :, 0:D], Rt[2], over_tiles(row["bk"]), ALU.add))
                    signal(V.tensor_tensor(KV[:, :, D:2 * D], Rt[3], over_tiles(row["bv"]), ALU.add), s, "kv", g)
                    c.link(V.tensor_tensor(XP[:, :, :], turn_of(Q, g), KV[:, :, 0:D], ALU.mult))
                    c.link(V.tensor_reduce(ATT[:, :, :], heads(XP[:, :, :]), AX.X, ALU.add))
                    signal(V.tensor_scalar(ATT[:, :, :], ATT[:, :, :], -50.0, 50.0, ALU.max, ALU.min), s, "att", g)
                    wait(dve, s, "ex", g + 1)
                    acc = turn_of(accv[L1W], g)
                    c.link(V.tensor_tensor(heads(acc[:, :, 0:D]), heads(KV[:, :, D:2 * D]), over_heads(EX[:, :, :]),
                                           ALU.mult))
                    c.link(copied(acc[:, :, D:D + HEADS], EX[:, :, :]))
                    c.link(copied(acc[:, :, D + HEADS:L1W], ZERO[:, 0:TG].unsqueeze(2)))
                    c.end()
                end_phase(dve, "dve")
                edge_pass(f"att{l}", 1)
                if l == 0:
                    c = Chain(dve, ind_step, 5)
                    c.turn(0)
                    c.link(V.tensor_copy(IND, accv[L1W][:, :, D + HEADS]))
                    c.link(V.tensor_scalar(RI, IND, 1.0, None, ALU.max))
                    V.tensor_scalar(DI, IND, 1.0, None, ALU.add).then_inc(root_in, 1)
                    dve.wait_ge(root_out, 3)
                    c.link(V.reciprocal(NODE[:, 4:6, :], NODE[:, 4:6, :]))
                s = dE[l]
                c = Chain(dve, s["steps"], CHAIN[f"e{l}"], s.base["steps"])
                with dve.Fori(0, NG) as g:
                    c.turn(g)
                    acc = turn_of(accv[L1W], g)
                    c.link(V.reciprocal(RSUM[:, :, :], acc[:, :, D:D + HEADS]))
                    signal(V.tensor_tensor(heads(XN[:, :, :]), heads(acc[:, :, 0:D]), over_heads(RSUM[:, :, :]),
                                           ALU.mult), s, "ag", g)
                    wait(dve, s, "o", g + 1)
                    c.link(V.tensor_tensor(XN[:, :, :], Rt[1], over_tiles(row["bo"]), ALU.add))
                    c.link(V.tensor_tensor(turn_of(Y, g), turn_of(Y, g), XN[:, :, :], ALU.add))
                    layer_norm(c, s, g, tile_in(Y, g), XN, 1 + l)
                    c.link(V.tensor_tensor(XN[:, :, :], XN[:, :, :], over_tiles(row["ln2_g"]), ALU.mult))
                    signal(V.tensor_tensor(XN[:, :, :], XN[:, :, :], over_tiles(row["ln2_b"]), ALU.add), s, "xn", g)
                    wait(dve, s, "o2", g + 1)
                    c.link(V.tensor_tensor(XN[:, :, :], Rt[0], over_tiles(row["b2"]), ALU.add))
                    c.link(V.tensor_tensor(turn_of(Y, g), turn_of(Y, g), XN[:, :, :], ALU.add))
                    if l == 1:
                        c.link(V.tensor_tensor(turn_of(X, g), turn_of(X, g), turn_of(Y, g), ALU.add))
                        layer_norm(c, s, g, tile_in(X, g), XN, 2, 1)
                        c.link(V.tensor_scalar(XN[:, :, :], XN[:, :, :], 0.0, None, ALU.max))
                        wait(dve, s, "free", g + 1)
                        signal(V.tensor_tensor(XP[:, :, :], XN[:, :, :], over_features(RO[:, bass.ds(g * TG, TG)]),
                                               ALU.mult), s, "hs", g)
                    c.end()
                if l == 1:
                    V.memset(ACC[:, 0:NT * D], 0.0)
                end_phase(dve, "dve")

            edge_pass("conv", 1)
            c = Chain(dve, dF["steps"], CHAIN["f"], dF.base["steps"])
            with dve.Fori(0, NG) as g:
                c.turn(g)
                signal(V.tensor_tensor(XN[:, :, :], turn_of(accv[D], g), over_features(RI[:, bass.ds(g * TG, TG)]),
                                       ALU.mult), dF, "ag", g)
                wait(dve, dF, "o", g + 1)
                c.link(V.tensor_tensor(XN[:, :, :], Rt[1], over_tiles(bias["bg"]), ALU.add))
                c.link(V.tensor_scalar(XN[:, :, :], XN[:, :, :], 0.0, None, ALU.max))
                c.link(V.tensor_tensor(turn_of(X, g), turn_of(X, g), XN[:, :, :], ALU.add))
                layer_norm(c, dF, g, tile_in(X, g), XN)
                signal(V.tensor_scalar(XN[:, :, :], XN[:, :, :], 0.0, None, ALU.max), dF, "h", g)
                wait(dve, dF, "mm", g + 1)
                wait(dve, dF, "free", g + 1)
                signal(V.tensor_tensor(HS[:, :, :], Rt[1], over_features(DI[:, bass.ds(g * TG, TG)]), ALU.mult),
                       dF, "hs", g)
                c.link(copied(turn_of(accv[D], g), HS[:, :, :]))
                c.end()
            end_phase(dve, "dve")
            edge_pass("gcn1", 1)
            c = Chain(dve, dG["steps"], CHAIN["g"], dG.base["steps"])
            with dve.Fori(0, NG) as g:
                c.turn(g)
                c.link(V.tensor_tensor(XN[:, :, :], turn_of(accv[D], g), over_features(DI[:, bass.ds(g * TG, TG)]),
                                       ALU.mult))
                c.link(V.tensor_tensor(XN[:, :, :], XN[:, :, :], over_tiles(bias["b31"]), ALU.add))
                signal(V.tensor_scalar(XN[:, :, :], XN[:, :, :], 0.0, None, ALU.max), dG, "h", g)
                wait(dve, dG, "mm", g + 1)
                wait(dve, dG, "free", g + 1)
                signal(V.tensor_tensor(HS64[:, :, :], R[1][:, 0:TG * DZ].rearrange("p (t d) -> p t d", t=TG),
                                       over_features(DI[:, bass.ds(g * TG, TG)], DZ), ALU.mult), dG, "hs", g)
                c.link(copied(turn_of(accv[DZ], g), HS64[:, :, :]))
                c.end()
            end_phase(dve, "dve")
            edge_pass("gcn2", 1)
            c = Chain(dve, dH["steps"], CHAIN["h"], dH.base["steps"])
            with dve.Fori(0, NG) as g:
                c.turn(g)
                c.link(V.tensor_tensor(Z64[:, :, :], turn_of(accv[DZ], g),
                                       over_features(DI[:, bass.ds(g * TG, TG)], DZ), ALU.mult))
                signal(V.tensor_tensor(Z64[:, :, :], Z64[:, :, :], over_tiles(bias["b32"][:, 0:DZ]), ALU.add),
                       dH, "z", g)
                wait(dve, dH, "mm", g + 1)
                signal(V.tensor_tensor(XN[:, :, :], Rt[1], over_tiles(bias["bd"]), ALU.add), dH, "y", g)
                wait(dve, dH, "sg", g + 1)
                c.link(V.tensor_tensor(turn_of(X, g), turn_of(X, g), XP[:, :, :], ALU.add))
                c.end()
            end_phase(dve, "dve")


def kernel(**inputs):
    import numpy as np
    import concourse.bacc as bacc
    from concourse.bass_utils import run_bass_kernel_spmd as run

    i = {k: np.asarray(v) for k, v in inputs.items()}
    t = np.ascontiguousarray
    host = {"x": i["x"], "src": i["src"], "dst": i["dst"]}
    host["Wn"] = t(i["L0_gnn_W_neigh"].T)
    host["We1"], host["We2"] = t(i["L0_gnn_W_edge"].T[:D]), t(i["L0_gnn_W_edge"].T[D:])
    host["Wl1"], host["Wl2"] = t(i["L0_gnn_W_lin"].T[:D]), t(i["L0_gnn_W_lin"].T[D:])
    host["bn"], host["be"], host["bl"] = i["L0_gnn_b_neigh"], i["L0_gnn_b_edge"], i["L0_gnn_b_lin"]
    for n in ("Wpos", "Wq", "Wk", "Wv", "Wo", "bpos", "bdeg", "Wdeg", "bq", "bk", "bv", "bo", "ln1_g", "ln1_b",
              "ln2_g", "ln2_b", "b2", "W1", "W2"):
        host[n] = i["L1_gnn_" + n]
    host["b1t"] = t(i["L1_gnn_b1"].reshape(2, FF // P, P).transpose(0, 2, 1))
    host["Wg"], host["bg"] = i["L2_gnn_weight"], i["L2_gnn_bias"]
    host["W31"], host["b31"], host["W32"], host["b32"] = (i["L3_gnn_" + n] for n in ("W1", "b1", "W2", "b2"))
    host["Wd"], host["bd"] = i["L3_gnn_Wd"], i["L3_gnn_bd"]

    nc = bacc.Bacc("TRN2", target_bir_lowering=False, num_devices=1)
    a, arrays = {}, {}
    for n, v in host.items():
        arrays["in_" + n] = t(v)
        a[n] = nc.dram_tensor("in_" + n, v.shape, mybir.dt.from_np(v.dtype), kind="ExternalInput").ap()
    out = nc.dram_tensor("out_x", (N, D), F32, kind="ExternalOutput").ap()
    build(nc, a, out)
    return run(nc, [arrays], core_ids=[0]).results[0]["out_x"]
```

```python
import concourse.bass as bass
from concourse import mybir
from contextlib import ExitStack

F32 = mybir.dt.float32
I32 = mybir.dt.int32
ALU = mybir.AluOpType
ACT = mybir.ActivationFunctionType
AX = mybir.AxisListType

P = 128
N, E, D = 6250, 100000, 128
HEADS, HD, FF, DZ = 8, 16, 512, 64
NT = -(-N // P)
LAST = N - (NT - 1) * P
TG = 7
NG = NT // TG
assert NG * TG == NT
SB = 28
EC = -(-E // (P * 2 * SB)) * 2 * SB
EFULL, EREST = E // EC, E % EC
S4 = 4
PB = 16
STEPS = -(-((E - NT) // P + NT) // (2 * PB)) * 2 * PB
GROUPS = STEPS // S4
AW = 2 * D + 1
L1W = D + HEADS + 1
OUT_OF_RANGE = 1 << 20
ENGINES = 5
CHAIN = {"a": 5, "b": 10, "d0": 13, "e0": 9, "d1": 13, "e1": 14, "f": 7, "g": 3, "h": 2}


class Events(dict):
    pass


def wait(eng, s, what, value, slot=None):
    if isinstance(value, int) and value <= 0:
        return
    eng.wait_ge(s[what] if slot is None else s[what][slot], value + s.base[what])


def gated(eng, passed):
    eng.sem_inc(passed)


class Chain:

    def __init__(self, eng, sem, per, base=0):
        self.eng, self.sem, self.per, self.base = eng, sem, per, base

    def turn(self, g):
        self.start, self.k = g * self.per + self.base, 0

    def link(self, ins):
        self.k += 1
        ins.then_inc(self.sem, 1)
        self.eng.wait_ge(self.sem, self.start + self.k)

    def end(self):
        assert self.k == self.per, (self.base, self.k, self.per)


def build(nc, a, out, debug=None):
    with ExitStack() as ctx:
        def sb(name, shape, dt=F32):
            return ctx.enter_context(nc.sbuf_tensor(name, shape, dt))

        def sem(name):
            return ctx.enter_context(nc.semaphore(name))

        tab_h = nc.dram_tensor("tab_h", (NT * P, D), F32, kind="Internal").ap()
        tab_kv = nc.dram_tensor("tab_kv", (NT * P, 2 * D), F32, kind="Internal").ap()
        tab_z = nc.dram_tensor("tab_z", (NT * P, DZ), F32, kind="Internal").ap()
        lists = [nc.dram_tensor(f"list{o}", (P * STEPS, 2), I32, kind="Internal").ap() for o in range(2)]

        X = sb("X", [P, NT, D])
        Y = sb("Y", [P, NT, D])
        Q = sb("Q", [P, NT, D])
        ACC = sb("ACC", [P, NT * AW])
        accv = {w: ACC[:, 0:NT * w].rearrange("p (t w) -> p t w", w=w) for w in (AW, L1W, D, DZ)}
        LO = [sb(f"LO{o}", [P, STEPS]) for o in range(2)]
        TILE = [sb(f"TILE{o}", [1, STEPS], I32) for o in range(2)]
        RECS = sb("RECS", [P, 3, EC], I32)
        SCR = sb("SCR", [P, 7296])
        IOTA = sb("IOTA", [P, P])
        IDENT = sb("IDENT", [P, P])
        ONES = sb("ONES", [P, P])
        ZERO = sb("ZERO", [P, D])
        STAGE = sb("STAGE", [P, 4, PB, 2], I32)
        SLOTS = sb("SLOTS", [P, 2, SB], I32)
        PAIRS = sb("PAIRS", [P, 2, SB, 2], I32)
        WMAT = sb("WMAT", [P, 11, D])
        WL1 = sb("WL1", [P, 5, D])
        WF1 = sb("WF1", [P, FF])
        WF2 = sb("WF2", [P, FF // P, D])
        B1T = sb("B1T", [P, FF // P])
        BL1 = sb("BL1", [P, 12, D])
        BIAS = sb("BIAS", [P, 7, D])
        NODE = sb("NODE", [P, 8, NT])
        OUTD, IND, DEGN, RO, RI, DI, TMPN, MASK = (NODE[:, i, :] for i in range(8))
        ST = sb("ST", [P, TG, 6])
        MV = sb("MV", [P, TG, 2])
        RSTD = sb("RSTD", [P, TG])
        SD = sb("SD", [P, TG])
        EPS = sb("EPS", [P, 1])
        CT = sb("CT", [P, 2, TG])
        SMALL = sb("SMALL", [P, 8])
        RSUM = sb("RSUM", [P, TG, HEADS])
        EX = sb("EX", [P, TG, HEADS])
        ATT = sb("ATT", [P, TG, HEADS])

        Gn = SCR[:, 0:4 * S4 * D].rearrange("p (r s w) -> p r s w", r=4, s=S4)
        Gw = ACC[:, NT * L1W:NT * L1W + 8 * S4 * D].rearrange("p (r s w) -> p r s w", r=4, s=S4)
        OH = SCR[:, 2048:4096].rearrange("p (r s w) -> p r s w", r=4, s=S4)
        OHT = SCR[:, 4096:5120].rearrange("p (r s w) -> p r s w", r=2, s=S4)
        M = SCR[:, 5120:5120 + 2 * S4 * L1W].rearrange("p (r s w) -> p r s w", r=2, s=S4)
        PROD = SCR[:, 6656:7168].rearrange("p (s w) -> p s w", s=S4)
        EATT = SCR[:, 7168:7168 + S4 * HEADS].rearrange("p (s h) -> p s h", s=S4)
        def tmp(i, w=1):
            return SCR[:, i * TG * D:(i + w) * TG * D]
        XN = tmp(0).rearrange("p (t d) -> p t d", t=TG)
        XP = tmp(1).rearrange("p (t d) -> p t d", t=TG)
        T1, T2, T3 = tmp(2), tmp(3), tmp(4)
        KV = tmp(5, 2).rearrange("p (t d) -> p t d", t=TG)
        HT = tmp(3, 4).rearrange("p (c n) -> p c n", c=FF // P)
        HS = tmp(5).rearrange("p (t d) -> p t d", t=TG)
        HS64 = tmp(5)[:, 0:TG * DZ].rearrange("p (t d) -> p t d", t=TG)
        Z64 = tmp(6)[:, 0:TG * DZ].rearrange("p (t d) -> p t d", t=TG)
        LIST = SCR[:, 5376:5376 + 2 * STEPS].bitcast(I32).rearrange("p (s two) -> p s two", two=2)
        col = [ACC[:, i * EC:(i + 1) * EC] for i in range(16)]
        SRCI, DSTI = col[0].bitcast(I32), col[1].bitcast(I32)
        HII, HI, EQ, CUM, RANK = col[2].bitcast(I32), col[3], col[4], col[5], col[6]
        SLOT, VAL, LOC = ([col[i].bitcast(I32), RECS[:, k, :]] for k, i in enumerate((7, 8, 9)))
        POSA, POSB = col[13].bitcast(I32), col[14].bitcast(I32)
        Qf = Q[:, :, :].rearrange("p t d -> p (t d)")
        GE, ONESC = ACC[:, 13 * EC:13 * EC + STEPS], col[15]
        small = tmp(3, 2)
        IOTAS = small[:, 0:STEPS]
        BEFORE = small[:, STEPS:STEPS + P]
        STARTP = small[:, STEPS + P:STEPS + 2 * P]
        CNT, NST, INCL, STARTS, BASE, NSTI, STARTT = (
            small[:, STEPS + 2 * P + i * 64:STEPS + 2 * P + i * 64 + NT] for i in range(7))
        NSTI, STARTT = NSTI.bitcast(I32), STARTT[:, 0:1]

        R = [ctx.enter_context(nc.psum_tensor(f"R{i}", [P, 1024], F32)) for i in range(2)]
        SUMS = ctx.enter_context(nc.psum_tensor("SUMS", [P, 2048], F32))
        R += [SUMS[:, 0:1024], SUMS[:, 1024:2048]]
        Rt = [r[:, 0:TG * D].rearrange("p (t d) -> p t d", t=TG) for r in R]

        phase_done, dense_done, passed = sem("phase_done"), sem("dense_done"), sem("passed")
        phase = {}

        def end_phase(eng, key):
            n = phase[key] = phase.get(key, 0) + 1
            eng.drain().then_inc(phase_done, 1)
            eng.wait_ge(phase_done, ENGINES * n)

        def end_dense(eng):
            eng.drain().then_inc(dense_done, 1)
            eng.wait_ge(dense_done, ENGINES - 1)

        MATS = ["Wn", "We1", "We2", "Wl1", "Wl2", "Wg", "W31", "W32", "Wd"]
        mat = {n: WMAT[:, i, :] for i, n in enumerate(MATS)}
        BIASES = ["bn", "be", "bl", "bg", "b31", "b32", "bd"]
        bias = {n: BIAS[:, i, :] for i, n in enumerate(BIASES)}
        L1MATS = ["Wpos", "Wq", "Wk", "Wv", "Wo"]
        l1mat = {n: WL1[:, i, :] for i, n in enumerate(L1MATS)}
        L1ROWS = ["bpos", "bdeg", "Wdeg", "bq", "bk", "bv", "bo", "ln1_g", "ln1_b", "ln2_g", "ln2_b", "b2"]
        row = {n: BL1[:, i, :] for i, n in enumerate(L1ROWS)}

        def over_tiles(b, n=TG):
            return b.unsqueeze(1).broadcast_to([P, n, b.shape[1]])

        def over_features(s, w=D):
            return s.unsqueeze(2).broadcast_to([P, s.shape[1], w])

        def over_heads(s):
            return s.unsqueeze(3).broadcast_to([P, s.shape[1], HEADS, HD])

        def heads(ap):
            return ap.rearrange("p t (h d) -> p t h d", h=HEADS)

        edges_in, x_in, w_in, w_l1, x_pad = sem("edges_in"), sem("x_in"), sem("w_in"), sem("w_l1"), sem("x_pad")
        const_ready, const_step = sem("const_ready"), sem("const_step")
        taken = sem("node_numbers_taken")
        ids_cleared, list_cleared, clear_ready = sem("ids_cleared"), sem("list_cleared"), sem("clear_ready")
        sort = [dict(step=sem(f"rank_step{o}"), step2=sem(f"base_step{o}"), misc=sem(f"sort_step{o}"),
                     counts=sem(f"counts_ready{o}"), sums=sem(f"bucket_sums{o}"), startp=sem(f"starts_ready{o}"),
                     startt=sem(f"starts_transposed{o}"), ge=sem(f"reached_ready{o}"), tiles=sem(f"tiles_summed{o}"),
                     slots=sem(f"slots_ready{o}"), staged=sem(f"scatter_staged{o}"),
                     sent=[sem(f"scattered{o}_{u}") for u in range(2)], listed=sem(f"list_loaded{o}"))
                for o in range(2)]
        PASSES = ["diff", "att0", "att1", "conv", "gcn1", "gcn2"]
        once = ("oh", "tr", "oht", "exp", "prod", "att", "ex", "msg", "agg")
        names = dict(oh="onehot_built", tr="onehot_transposed", oht="onehot_t_copied",
                     exp="rows_expanded", prod="products_ready", red="products_reduced", att="scores_ready",
                     ex="exp_ready", msg="messages_ready", agg="edges_summed", acc="sums_added")
        sems = {k: sem(v) for k, v in names.items()}
        sems["staged"] = [sem(f"indices_staged{u}") for u in range(4)]
        sems["gath"] = [sem(f"gathered{u}") for u in range(4)]

        def kind_of(n):
            return "att" if n.startswith("att") else "diff" if n == "diff" else "sum"

        def counts_of(n):
            c = {k: GROUPS for k in once}
            c.update(staged=16 * STEPS // PB // 4, gath=16 * S4 * GROUPS // 4, acc=S4 * GROUPS, red=GROUPS)
            unused = {"att": (), "diff": ("prod", "ex", "red"), "sum": ("tr", "oht", "exp", "prod", "red", "att", "ex", "msg")}
            c.update({k: 0 for k in unused[kind_of(n)]})
            return c

        ps, base = {}, dict.fromkeys(list(sems), 0)
        for n in PASSES:
            ps[n] = Events(sems)
            ps[n].base = dict(base)
            base = {k: base[k] + v for k, v in counts_of(n).items()}

        STAGES = {
            "a": "mv sd h t tc mm hp st free", "b": "mv sd cp fresh s t tc mm zt ztc z",
            "d0": "mv sd xn xt xtc pos xp pt ptc qkv kv st free att ex", "e0": "mv sd ag at atc o xn xt xtc hid gelu o2",
            "d1": "mv sd xn xt xtc pos xp pt ptc qkv kv st free att ex", "e1": "mv sd mv2 sd2 ag at atc o xn xt xtc hid gelu o2 hs st free",
            "f": "mv sd ag at atc o h ht htc mm hs st free", "g": "h ht htc mm hs st free", "h": "z zt ztc mm y sg",
        }
        meaning = dict(mv="variance_ready", sd="deviation_ready", h="h_ready", t="transposed", tc="transposed_copied", mm="product_ready", hp="table_rows",
                       st="rows_stored", free="rows_free", cp="copies_ready", fresh="copies_free", s="mean_ready",
                       zt="z_transposed", ztc="z_t_copied", z="z_ready", xn="normed_ready", xt="normed_transposed",
                       xtc="normed_t_copied", pos="pos_ready", xp="xp_ready", pt="xp_transposed", ptc="xp_t_copied",
                       qkv="qkv_ready", kv="kv_rows", att="self_scores", ex="self_exp", ag="aggregate_ready",
                       at="aggregate_transposed", atc="aggregate_t_copied", o="projected", hid="hidden_ready",
                       gelu="gelu_ready", o2="ffn_ready", hs="scaled_rows", ht="h_transposed", htc="h_t_copied",
                       y="logits_ready", sg="sigmoid_ready", steps="vector_steps")
        stage_sems = {k: sem(v) for k, v in meaning.items()}
        per_turn = dict(st=16, hid=FF // P, gelu=FF // P)
        dense, base = {}, dict.fromkeys(stage_sems, 0)
        for n, events in STAGES.items():
            dense[n] = Events(stage_sems)
            dense[n].base = dict(base)
            for k in events.split():
                base[k.rstrip("2") if k in ("mv2", "sd2") else k] += \
                    NG * per_turn.get(k, 1) + (k in ("free", "fresh"))
            base["steps"] += NG * CHAIN[n]
        dA, dB, dF, dG, dH = (dense[n] for n in "abfgh")
        dD, dE = [dense["d0"], dense["d1"]], [dense["e0"], dense["e1"]]
        deg_step, deg_sum, deg_tot = sem("deg_step"), sem("deg_sum"), sem("deg_tot")
        out_done = sem("out_done")
        dD_pre = [sem(f"bias_step{l}") for l in range(2)]
        root_in, root_out = sem("root_operand_ready"), sem("root_ready")
        ind_step = sem("indegree_step")

        block = ctx.enter_context(nc.Block())

        def per_group(eng, body):
            n = GROUPS // 4
            for u in range(4):
                body(0, u)
            with eng.Fori(1, n - 1) as it:
                for u in range(4):
                    body(it, u)
            for u in range(4):
                body(n - 1, u)

        def exists(gi):
            return not isinstance(gi, int) or gi < GROUPS

        def step_tiles(eng, o, gi):
            _, tiles = nc.values_load_multi_w_load_instructions(
                TILE[o][0:1, bass.ds(gi * S4, S4)], engines=(eng.engine,), min_val=0, max_val=NT - 1,
                skip_runtime_bounds_check_because="a count of the NT buckets that start by the step, less one")
            return tiles

        TABLE = {"diff": (tab_h, D), "att0": (tab_kv, 2 * D), "att1": (tab_kv, 2 * D), "conv": (tab_h, D),
                 "gcn1": (tab_h, D), "gcn2": (tab_z, DZ)}

        @block.sync
        def _(sp):
            sp.wait_ge(ids_cleared, 1)
            for ids, dst in ((a["src"], SRCI), (a["dst"], DSTI)):
                sp.dma_start(dst[0:EFULL, :], ids[0:EFULL * EC].rearrange("(p c) -> p c", c=EC)).then_inc(edges_in, 16)
                sp.dma_start(dst[EFULL:EFULL + 1, 0:EREST],
                             ids[EFULL * EC:E].rearrange("(p c) -> p c", c=EREST)).then_inc(edges_in, 16)
            sp.wait_ge(clear_ready, 1)
            for o in range(2):
                sp.dma_start(lists[o].rearrange("(p s) two -> p s two", s=STEPS), LIST).then_inc(list_cleared, 16)
            sp.wait_ge(x_pad, 1)
            sp.dma_start(X[:, 0:NT - 1, :], a["x"][0:(NT - 1) * P, :].rearrange("(t p) d -> p t d", p=P))\
                .then_inc(x_in, 16)
            sp.dma_start(X[0:LAST, NT - 1, :], a["x"][(NT - 1) * P:N, :]).then_inc(x_in, 16)

            def store(table, src, s, ready):
                view = table.rearrange("(t p) d -> p t d", p=P)
                sp.sem_inc(s["free"])
                with sp.Fori(0, NG) as g:
                    wait(sp, s, ready, g + 1)
                    sp.dma_start(view[:, bass.ds(g * TG, TG), :], src).then_inc(s["st"], 16)
                    wait(sp, s, "st", (g + 1) * 16)
                    sp.sem_inc(s["free"])

            def load_l1(l):
                for n in L1MATS:
                    sp.dma_start(l1mat[n], a[n][l]).then_inc(w_l1, 16)
                for n in L1ROWS:
                    v = a[n][l, 0] if n == "Wdeg" else a[n][l]
                    sp.dma_start(row[n], v.partition_broadcast(P)).then_inc(w_l1, 16)
                sp.dma_start(WF1[:, :], a["W1"][l]).then_inc(w_l1, 16)
                sp.dma_start(WF2[:, :, :], a["W2"][l].rearrange("(c k) d -> k c d", k=P)).then_inc(w_l1, 16)
                sp.dma_start(B1T[:, :], a["b1t"][l]).then_inc(w_l1, 16)

            def stage_indices(name, o):
                s = ps[name]
                freed = "msg" if kind_of(name) == "att" else "agg"
                entries = lists[o].rearrange("(p s) two -> p s two", s=STEPS)

                def load(it, u, first):
                    b = it * 4 + u
                    if not first:
                        wait(sp, s, freed, b * (PB // S4) - 3 * (PB // S4))
                    sp.dma_start(STAGE[:, u, :, :], entries[:, bass.ds(b * PB, PB), :]).then_inc(s["staged"][u], 16)

                for u in range(4):
                    load(0, u, True)
                with sp.Fori(1, STEPS // PB // 4) as it:
                    for u in range(4):
                        load(it, u, False)
                end_phase(sp, "sp")

            def load_list(o):
                for u in range(2):
                    sp.wait_ge(sort[o]["sent"][u], 16 * EC // 2)
                sp.dma_start(LIST, lists[o].rearrange("(p s) two -> p s two", s=STEPS)).then_inc(sort[o]["listed"], 16)

            load_l1(0)
            store(tab_h, HS[:, :, :], dA, "hp")
            load_list(0)
            end_phase(sp, "sp")
            stage_indices("diff", 0)
            end_dense(sp)
            for l in range(2):
                store(tab_kv, KV[:, :, :], dD[l], "kv")
                end_phase(sp, "sp")
                if l == 0:
                    load_list(1)
                stage_indices(f"att{l}", 1)
                if l == 1:
                    store(tab_h, XP[:, :, :], dE[l], "hs")
                end_phase(sp, "sp")
                if l == 0:
                    load_l1(1)
            stage_indices("conv", 1)
            store(tab_h, HS[:, :, :], dF, "hs")
            end_phase(sp, "sp")
            stage_indices("gcn1", 1)
            store(tab_z, HS64[:, :, :], dG, "hs")
            end_phase(sp, "sp")
            stage_indices("gcn2", 1)
            end_phase(sp, "sp")
            sp.dma_start(out[0:(NT - 1) * P, :].rearrange("(t p) d -> p t d", p=P), X[:, 0:NT - 1, :])\
                .then_inc(out_done, 16)
            sp.dma_start(out[(NT - 1) * P:N, :], X[0:LAST, NT - 1, :]).then_inc(out_done, 16)
            sp.wait_ge(out_done, 32)

        @block.gpsimd
        def _(pool):
            n = [0]

            def step(ins):
                n[0] += 1
                ins.then_inc(const_step, 1)
                pool.wait_ge(const_step, n[0])

            nc.gpsimd.memset(IDENT[:, :], 0.0)
            nc.gpsimd.memset(ONES[:, :], 1.0)
            nc.gpsimd.memset(ZERO[:, :], 0.0)
            nc.gpsimd.memset(EPS[:, :], 1e-5)
            nc.gpsimd.memset(ONESC, 1.0)
            nc.gpsimd.memset(MASK, 1.0)
            step(nc.gpsimd.memset(BEFORE, 1.0))
            step(nc.gpsimd.iota(IOTA[:, :], [[1, P]], base=0, channel_multiplier=0,
                                allow_small_or_imprecise_dtypes=True))
            step(nc.gpsimd.iota(IOTAS, [[1, STEPS]], base=0, channel_multiplier=0,
                                allow_small_or_imprecise_dtypes=True))
            step(nc.gpsimd.affine_select(out=IDENT[:, :], in_=IDENT[:, :], compare_op=ALU.not_equal, fill=1.0,
                                         base=0, pattern=[[-1, P]], channel_multiplier=1))
            step(nc.gpsimd.affine_select(out=BEFORE, in_=BEFORE, compare_op=ALU.is_gt, fill=0.0,
                                         base=0, pattern=[[1, P]], channel_multiplier=-1))
            nc.gpsimd.affine_select(out=MASK, in_=MASK, compare_op=ALU.is_gt, fill=0.0,
                                    base=N, pattern=[[-P, NT]], channel_multiplier=-1).then_inc(const_ready, 1)

            pool.wait_ge(list_cleared, 32)
            def scatters(o):
                s = sort[o]
                pool.wait_ge(s["slots"], 1)

                def scatter(b, it, u, first):
                    if not first:
                        pool.wait_ge(s["sent"][u], it * (16 * SB))
                        gated(pool, passed)
                    elif o == 1:
                        pool.wait_ge(sort[0]["sent"][u], 16 * EC // 2)
                    nc.gpsimd.tensor_copy(PAIRS[:, u, :, 0], VAL[o][:, bass.ds(b * SB, SB)])
                    nc.gpsimd.tensor_copy(PAIRS[:, u, :, 1], LOC[o][:, bass.ds(b * SB, SB)])
                    nc.gpsimd.tensor_copy(SLOTS[:, u, :], SLOT[o][:, bass.ds(b * SB, SB)]).then_inc(s["staged"], 1)
                    pool.wait_ge(s["staged"], b + 1)
                    gated(pool, passed)
                    for j in range(SB):
                        nc.gpsimd.indirect_dma_start(
                            lists[o], bass.IndirectOffsetOnAxis(SLOTS[:, u, j:j + 1], 0), PAIRS[:, u, j, :], None,
                            bounds_check=P * STEPS - 1, oob_is_err=False).then_inc(s["sent"][u], 16)

                for u in range(2):
                    scatter(u, 0, u, True)
                with pool.Fori(1, EC // SB // 2) as it:
                    for u in range(2):
                        scatter(it * 2 + u, it, u, False)

            scatters(0)
            end_phase(pool, "pool")

            def gathers(name, o):
                s, kind = ps[name], kind_of(name)
                table, w = TABLE[name]
                freed = "msg" if kind == "att" else "agg"

                G = Gw if kind == "att" else Gn

                def block_of(it, u, first):
                    b = it * 4 + u
                    wait(pool, s, "staged", (it + 1) * 16, u)
                    gated(pool, passed)
                    for q in range(PB // S4):
                        if not (first and u == 0):
                            wait(pool, s, freed, b * (PB // S4) + (q - 3))
                            gated(pool, passed)
                        for j in range(S4):
                            nc.gpsimd.indirect_dma_start(
                                G[:, q, j, 0:w], None, table,
                                bass.IndirectOffsetOnAxis(STAGE[:, u, q * S4 + j, 0:1], 0))\
                                .then_inc(s["gath"][q], 16)

                for u in range(4):
                    block_of(0, u, True)
                with pool.Fori(1, STEPS // PB // 4) as it:
                    for u in range(4):
                        block_of(it, u, False)
                end_phase(pool, "pool")

            gathers("diff", 0)
            scatters(1)
            for l in range(2):
                end_phase(pool, "pool")
                gathers(f"att{l}", 1)
                end_phase(pool, "pool")
            gathers("conv", 1)
            end_phase(pool, "pool")
            gathers("gcn1", 1)
            end_phase(pool, "pool")
            gathers("gcn2", 1)
            end_phase(pool, "pool")

        @block.tensor
        def _(pe):
            pe.wait_ge(const_ready, 1)
            def bucket_sums(o):
                s = sort[o]
                pe.wait_ge(s["counts"], 1)
                nc.tensor.matmul(R[0][:, 0:NT], BEFORE, CNT, start=True, stop=True)
                nc.tensor.matmul(R[0][:, 512:512 + NT], ONES[:, :], CNT, start=True, stop=True).then_inc(s["sums"], 1)
                pe.wait_ge(s["startp"], 1)
                nc.tensor.transpose(R[1][:, 0:P], STARTP, IDENT[:, :]).then_inc(s["startt"], 1)
                pe.wait_ge(s["ge"], 1)
                h = STEPS // 2
                nc.tensor.matmul(R[2][:, 0:h], ONES[:, :], GE[:, 0:h], start=True, stop=True)
                nc.tensor.matmul(R[2][:, 512:512 + h], ONES[:, :], GE[:, h:STEPS], start=True, stop=True)\
                    .then_inc(s["tiles"], 1)

            def transposes(dst, src, sig, w=D):
                for j in range(TG):
                    ins = nc.tensor.transpose(dst[0:w, j * P:(j + 1) * P], src(j), IDENT[:, :])
                if sig is not None:
                    ins.then_inc(sig, 1)

            def products(dst, pairs, sig):
                for j in range(TG):
                    for k, (t, w) in enumerate(pairs):
                        ins = nc.tensor.matmul(dst[:, j, :], t(j), w, start=k == 0, stop=k == len(pairs) - 1)
                if sig is not None:
                    ins.then_inc(sig, 1)

            def tile_of(t, k=P):
                return lambda j: t[0:k, j * P:(j + 1) * P]

            bucket_sums(0)
            pe.wait_ge(w_in, 16 * (len(MATS) + len(BIASES)))
            with pe.Fori(0, NG) as g:
                wait(pe, dA, "h", g + 1)
                transposes(R[0], lambda j: XN[:, j, :], dA["t"])
                wait(pe, dA, "tc", g + 1)
                products(Rt[1], [(tile_of(T1), mat["Wn"])], dA["mm"])
            bucket_sums(1)
            end_phase(pe, "pe")

            def edge_pass(name, o):
                s, kind = ps[name], kind_of(name)
                w = {"att": L1W, "diff": D}.get(kind, TABLE[name][1])
                G = Gn

                def transpose(it, u):
                    gi = it * 4 + u
                    wait(pe, s, "oh", gi + 1)
                    wait(pe, s, "oht", gi - 1)
                    for j in range(S4):
                        ins = nc.tensor.transpose(R[0][:, (u % 2) * 512 + j * P:(u % 2) * 512 + (j + 1) * P],
                                                  OH[:, u % 4, j, :], IDENT[:, :])
                    ins.then_inc(s["tr"], 1)

                def expand(it, u):
                    gi = it * 4 + u
                    tiles = step_tiles(pe, o, gi)
                    wait(pe, s, "oht", gi + 1)
                    wait(pe, s, "att", gi - 1)
                    for j in range(S4):
                        ins = nc.tensor.matmul(R[1][:, (u % 2) * 512 + j * P:(u % 2) * 512 + (j + 1) * P],
                                               OHT[:, u % 2, j, :], Qf[:, bass.ds(tiles[j] * D, D)],
                                               start=True, stop=True)
                    ins.then_inc(s["exp"], 1)

                def summed(it, u):
                    gi = it * 4 + u
                    wait(pe, s, "oh", gi + 1)
                    if kind != "sum":
                        wait(pe, s, "msg", gi + 1)
                    if kind != "att":
                        wait(pe, s, "gath", (it + 1) * (16 * S4), u)
                    wait(pe, s, "acc", gi * S4 if kind == "diff" else gi * S4 - S4)
                    for j in range(S4):
                        oh = OH[:, u % 4, j, :]
                        at = j * 512 if kind == "diff" else u % 2 * 1024 + j * 256
                        dst = SUMS[:, at:at + w]
                        if kind == "att":
                            ins = nc.tensor.matmul(dst, oh, M[:, u % 2, j, :], start=True, stop=True)
                        else:
                            ins = nc.tensor.matmul(dst, oh, G[:, u, j, 0:w], start=True, stop=True)
                        if kind == "diff":
                            ins = nc.tensor.matmul(SUMS[:, at + D:at + AW], oh, M[:, u % 2, j, 0:D + 1],
                                                   start=True, stop=True)
                    ins.then_inc(s["agg"], 1)

                def body(it, u):
                    gi = it * 4 + u
                    if kind != "sum":
                        if exists(gi + 2):
                            transpose(it if u < 2 else it + 1, (u + 2) % 4)
                        if exists(gi + 1):
                            expand(it if u < 3 else it + 1, (u + 1) % 4)
                    summed(it, u)

                if kind != "sum":
                    transpose(0, 0)
                    transpose(0, 1)
                    expand(0, 0)
                per_group(pe, body)
                end_phase(pe, "pe")

            edge_pass("diff", 0)

            pe.sem_inc(dB["fresh"])
            with pe.Fori(0, NG) as g:
                wait(pe, dB, "cp", g + 1)
                transposes(R[0], lambda j: KV[:, j, 0:D], None)
                transposes(R[1], lambda j: KV[:, j, D:2 * D], None)
                transposes(R[2], lambda j: XP[:, j, :], dB["t"])
                wait(pe, dB, "tc", g + 1)
                products(Rt[3], [(tile_of(T1), mat["We1"]), (tile_of(T2), mat["We2"])], dB["mm"])
                wait(pe, dB, "s", g + 1)
                transposes(R[0], lambda j: XN[:, j, :], dB["zt"])
                wait(pe, dB, "ztc", g + 1)
                products(Rt[1], [(tile_of(T3), mat["Wl1"]), (tile_of(T1), mat["Wl2"])], dB["z"])
                wait(pe, dB, "steps", (g + 1) * CHAIN["b"])
                pe.sem_inc(dB["fresh"])
            pe.wait_ge(deg_sum, 1)
            nc.tensor.matmul(R[0][:, 0:1], ONES[:, :], SMALL[:, 0:1], start=True, stop=True).then_inc(deg_tot, 1)
            end_dense(pe)

            for l in range(2):
                s = dD[l]
                pe.wait_ge(w_l1, 16 * (len(L1MATS) + len(L1ROWS) + 3) * (l + 1))
                with pe.Fori(0, NG) as g:
                    wait(pe, s, "xn", g + 1)
                    transposes(R[0], lambda j: XN[:, j, :], s["xt"])
                    wait(pe, s, "xtc", g + 1)
                    products(Rt[1], [(tile_of(T1), l1mat["Wpos"])], s["pos"])
                    wait(pe, s, "xp", g + 1)
                    transposes(R[0], lambda j: XP[:, j, :], s["pt"])
                    wait(pe, s, "ptc", g + 1)
                    products(Rt[1], [(tile_of(T1), l1mat["Wq"])], None)
                    products(Rt[2], [(tile_of(T1), l1mat["Wk"])], None)
                    products(Rt[3], [(tile_of(T1), l1mat["Wv"])], s["qkv"])
                end_phase(pe, "pe")
                edge_pass(f"att{l}", 1)
                s = dE[l]
                with pe.Fori(0, NG) as g:
                    wait(pe, s, "ag", g + 1)
                    transposes(R[0], lambda j: XN[:, j, :], s["at"])
                    wait(pe, s, "atc", g + 1)
                    products(Rt[1], [(tile_of(T1), l1mat["Wo"])], s["o"])
                    wait(pe, s, "xn", g + 1)
                    transposes(R[0], lambda j: XN[:, j, :], s["xt"])
                    wait(pe, s, "xtc", g + 1)
                    half = TG * P // 2
                    for c in range(FF // P):
                        if c >= 2:
                            wait(pe, s, "gelu", g * (FF // P) + (c - 1))
                        for k in range(2):
                            ins = nc.tensor.matmul(R[2 + c % 2][:, k * 512:k * 512 + half],
                                                   WF1[:, c * P:(c + 1) * P], T1[:, k * half:(k + 1) * half],
                                                   start=True, stop=True)
                        ins.then_inc(s["hid"], 1)
                    wait(pe, s, "gelu", (g + 1) * (FF // P))
                    products(Rt[0], [((lambda j, c=c: HT[:, c, j * P:(j + 1) * P]), WF2[:, c, :])
                                     for c in range(FF // P)], s["o2"])
                end_phase(pe, "pe")
            edge_pass("conv", 1)
            with pe.Fori(0, NG) as g:
                wait(pe, dF, "ag", g + 1)
                transposes(R[0], lambda j: XN[:, j, :], dF["at"])
                wait(pe, dF, "atc", g + 1)
                products(Rt[1], [(tile_of(T1), mat["Wg"])], dF["o"])
                wait(pe, dF, "h", g + 1)
                transposes(R[0], lambda j: XN[:, j, :], dF["ht"])
                wait(pe, dF, "htc", g + 1)
                products(Rt[1], [(tile_of(T1), mat["W31"])], dF["mm"])
            end_phase(pe, "pe")
            edge_pass("gcn1", 1)
            with pe.Fori(0, NG) as g:
                wait(pe, dG, "h", g + 1)
                transposes(R[0], lambda j: XN[:, j, :], dG["ht"])
                wait(pe, dG, "htc", g + 1)
                products(R[1][:, 0:TG * DZ].rearrange("p (t d) -> p t d", t=TG),
                         [(tile_of(T1), mat["W32"][:, 0:DZ])], dG["mm"])
            end_phase(pe, "pe")
            edge_pass("gcn2", 1)
            with pe.Fori(0, NG) as g:
                wait(pe, dH, "z", g + 1)
                gated(pe, passed)
                transposes(R[0], lambda j: Z64[:, j, :], dH["zt"], DZ)
                wait(pe, dH, "ztc", g + 1)
                products(Rt[1], [(tile_of(T1, DZ), mat["Wd"][0:DZ, :])], dH["mm"])
            end_phase(pe, "pe")

        @block.scalar
        def _(act):
            for n in MATS:
                v = a[n]
                act.dma_start(mat[n][0:v.shape[0], 0:v.shape[1]], v).then_inc(w_in, 16)
            for n in BIASES:
                v = a[n]
                act.dma_start(bias[n][:, 0:v.shape[0]], v.partition_broadcast(P)).then_inc(w_in, 16)

            def copied(dst, src, s, ready, done, g, k=P):
                wait(act, s, ready, g + 1)
                nc.scalar.activation(dst[0:k, :], src[0:k, 0:TG * D], ACT.Copy).then_inc(s[done], 1)

            def deviation(s, g, of=1, k=0):
                wait(act, s, "mv", g * of + (k + 1))
                nc.scalar.activation(SD[:, :], MV[:, :, 1], ACT.Sqrt, bias=EPS[:, 0:1]).then_inc(s["sd"], 1)

            with act.Fori(0, NG) as g:
                deviation(dA, g)
                copied(T1, R[0], dA, "t", "tc", g)
            end_phase(act, "act")

            def edge_pass(name):
                s, kind = ps[name], kind_of(name)

                def copy(it, u):
                    gi = it * 4 + u
                    wait(act, s, "tr", gi + 1)
                    wait(act, s, "exp", gi - 1)
                    nc.scalar.activation(OHT[:, u % 2, :, :].rearrange("p s w -> p (s w)"),
                                         R[0][:, (u % 2) * 512:(u % 2) * 512 + 512], ACT.Copy).then_inc(s["oht"], 1)

                def body(it, u):
                    gi = it * 4 + u
                    if exists(gi + 2):
                        copy(it if u < 2 else it + 1, (u + 2) % 4)
                    wait(act, s, "att", gi + 1)
                    if kind == "att":
                        wait(act, s, "agg", gi - 1)
                        nc.scalar.activation(M[:, u % 2, :, D:D + HEADS], EATT[:, :, :], ACT.Exp)\
                            .then_inc(s["ex"], 1)
                    else:
                        nc.scalar.activation(M[:, u % 2, :, 0:D], PROD[:, :, :], ACT.Abs).then_inc(s["msg"], 1)

                if kind != "sum":
                    copy(0, 0)
                    copy(0, 1)
                    per_group(act, body)
                end_phase(act, "act")

            edge_pass("diff")
            with act.Fori(0, NG) as g:
                wait(act, dB, "fresh", g + 1)
                gated(act, passed)
                nc.scalar.activation(KV[:, :, :], accv[AW][:, bass.ds(g * TG, TG), 0:2 * D], ACT.Copy)
                nc.scalar.activation(XP[:, :, :], Y[:, bass.ds(g * TG, TG), :], ACT.Copy).then_inc(dB["cp"], 1)
                wait(act, dB, "t", g + 1)
                nc.scalar.activation(T1, R[0][:, 0:TG * D], ACT.Copy)
                nc.scalar.activation(T2, R[1][:, 0:TG * D], ACT.Copy)
                nc.scalar.activation(T3, R[2][:, 0:TG * D], ACT.Copy).then_inc(dB["tc"], 1)
                copied(T1, R[0], dB, "zt", "ztc", g)
                deviation(dB, g)
            act.wait_ge(root_in, 1)
            nc.scalar.activation(SMALL[:, 1:2], R[0][:, 0:1], ACT.Sqrt, scale=1.0 / (N - 1)).then_inc(root_out, 1)
            act.wait_ge(root_in, 2)
            nc.scalar.activation(RO, RO, ACT.Sqrt).then_inc(root_out, 1)
            end_dense(act)
            for l in range(2):
                s = dD[l]
                with act.Fori(0, NG) as g:
                    deviation(s, g)
                    copied(T1, R[0], s, "xt", "xtc", g)
                    copied(T1, R[0], s, "pt", "ptc", g)
                    wait(act, s, "att", g + 1)
                    nc.scalar.activation(EX[:, :, :], ATT[:, :, :], ACT.Exp).then_inc(s["ex"], 1)
                end_phase(act, "act")
                edge_pass(f"att{l}")
                if l == 0:
                    act.wait_ge(root_in, 3)
                    nc.scalar.activation(NODE[:, 4:6, :], NODE[:, 4:6, :], ACT.Sqrt).then_inc(root_out, 1)
                s = dE[l]
                with act.Fori(0, NG) as g:
                    copied(T1, R[0], s, "at", "atc", g)
                    deviation(s, g, 1 + l)
                    copied(T1, R[0], s, "xt", "xtc", g)
                    half = TG * P // 2
                    for c in range(FF // P):
                        wait(act, s, "hid", g * (FF // P) + (c + 1))
                        nc.scalar.activation(HT[:, c, :].rearrange("p (k n) -> p k n", k=2),
                                             R[2 + c % 2][:, :].rearrange("p (k n) -> p k n", k=2)[:, :, 0:half],
                                             ACT.Gelu, bias=B1T[:, c:c + 1]).then_inc(s["gelu"], 1)
                    if l == 1:
                        deviation(s, g, 2, 1)
                end_phase(act, "act")
            edge_pass("conv")
            with act.Fori(0, NG) as g:
                copied(T1, R[0], dF, "at", "atc", g)
                deviation(dF, g)
                copied(T1, R[0], dF, "ht", "htc", g)
            end_phase(act, "act")
            edge_pass("gcn1")
            with act.Fori(0, NG) as g:
                copied(T1, R[0], dG, "ht", "htc", g)
            end_phase(act, "act")
            edge_pass("gcn2")
            with act.Fori(0, NG) as g:
                copied(T1, R[0], dH, "zt", "ztc", g, DZ)
                wait(act, dH, "y", g + 1)
                nc.scalar.activation(XP[:, :, :], XN[:, :, :], ACT.Sigmoid).then_inc(dH["sg"], 1)
            end_phase(act, "act")

        @block.vector
        def _(dve):
            V = nc.vector

            def copied(dst, src):
                return V.tensor_scalar(dst, src, 0.0, None, ALU.add)

            V.memset(SRCI, NT * P)
            V.memset(DSTI, NT * P).then_inc(ids_cleared, 1)
            V.memset(LIST[:, :, 0], 0)
            V.memset(LIST[:, :, 1], -1).then_inc(clear_ready, 1)
            V.memset(X[:, NT - 1, :], 0.0).then_inc(x_pad, 1)
            dve.wait_ge(const_ready, 1)
            dve.wait_ge(edges_in, 64)

            def bucket(o, key, val):
                s = sort[o]
                m = Chain(dve, s["misc"], 100)
                m.turn(0)
                V.tensor_copy(VAL[o], val)
                V.tensor_single_scalar(LOC[o], key, P - 1, ALU.bitwise_and)
                m.link(V.tensor_single_scalar(HII, key, P.bit_length() - 1, ALU.logical_shift_right))
                V.tensor_copy(HI, HII)
                m.link(V.memset(RANK, 0.0))
                c = Chain(dve, s["step"], 5)
                with dve.Fori(0, NT) as h:
                    c.turn(h)
                    c.link(V.tensor_scalar(EQ, HI, IOTA[:, bass.ds(h, 1)], None, ALU.is_equal))
                    c.link(V.tensor_tensor_scan(CUM, ONESC, EQ, 0.0, ALU.mult, ALU.add))
                    c.link(V.tensor_tensor(EQ, EQ, CUM, ALU.mult))
                    c.link(V.tensor_tensor(RANK, RANK, EQ, ALU.add))
                    c.link(copied(CNT[:, bass.ds(h, 1)], CUM[:, EC - 1:EC]))
                    c.end()
                V.memset(STARTP, 1e9).then_inc(s["counts"], 1)
                dve.wait_ge(s["sums"], 1)
                m.link(V.tensor_scalar(NSTI, R[0][:, 512:512 + NT], float(P - 1), None, ALU.add))
                m.link(V.tensor_single_scalar(NSTI, NSTI, P.bit_length() - 1, ALU.logical_shift_right))
                m.link(V.tensor_copy(NST, NSTI))
                m.link(V.tensor_tensor_scan(INCL, ONESC[:, 0:NT], NST, 0.0, ALU.mult, ALU.add))
                m.link(V.tensor_tensor(STARTS, INCL, NST, ALU.subtract))
                V.tensor_copy(STARTP[:, 0:NT], STARTS).then_inc(s["startp"], 1)
                m.link(V.scalar_tensor_tensor(BASE, STARTS, float(P), R[0][:, 0:NT], ALU.mult, ALU.add))
                dve.wait_ge(s["startt"], 1)
                m.link(V.tensor_copy(STARTT, R[1][:, 0:1]))
                V.tensor_scalar(GE, IOTAS, STARTT, None, ALU.is_ge).then_inc(s["ge"], 1)
                c = Chain(dve, s["step2"], 2)
                with dve.Fori(0, NT) as h:
                    c.turn(h)
                    c.link(V.tensor_scalar(EQ, HI, IOTA[:, bass.ds(h, 1)], BASE[:, bass.ds(h, 1)],
                                           ALU.is_equal, ALU.mult))
                    c.link(V.tensor_tensor(RANK, RANK, EQ, ALU.add))
                    c.end()
                dve.wait_ge(s["tiles"], 1)
                half = STEPS // 2
                for k in range(2):
                    m.link(V.tensor_scalar(TILE[o][0:1, k * half:(k + 1) * half], R[2][0:1, k * 512:k * 512 + half],
                                           -1.0, None, ALU.add))
                m.link(V.tensor_scalar(HII, RANK, -1.0, None, ALU.add))
                V.tensor_single_scalar(POSA, HII, P - 1, ALU.bitwise_and)
                m.link(V.tensor_single_scalar(POSB, HII, P.bit_length() - 1, ALU.arith_shift_right))
                m.link(V.tensor_scalar(EQ, HI, float(NT), float(OUT_OF_RANGE), ALU.is_equal, ALU.mult))
                m.link(V.scalar_tensor_tensor(CUM, POSA, float(STEPS), POSB, ALU.mult, ALU.add))
                V.tensor_tensor(SLOT[o], CUM, EQ, ALU.add).then_inc(s["slots"], 1)
                dve.wait_ge(s["slots"], 1)

            bucket(0, SRCI, DSTI)


            def layer_norm(c, s, g, src, dst, of=1, k=0):
                gated(dve, passed)
                for j in range(TG):
                    ins = V.bn_stats(ST[:, j, :], src(j))
                c.link(ins)
                gated(dve, passed)
                for j in range(TG):
                    ins = V.bn_aggr(MV[:, j, :], ST[:, j, :])
                ins.then_inc(s["mv"], 1)
                wait(dve, s, "sd", g * of + (k + 1))
                c.link(V.reciprocal(RSTD[:, :], SD[:, :]))
                for j in range(TG):
                    ins = V.tensor_scalar(dst[:, j, :], src(j), MV[:, j, 0:1], RSTD[:, j:j + 1],
                                          ALU.subtract, ALU.mult)
                c.link(ins)

            def turn_of(t, g):
                return t[:, bass.ds(g * TG, TG), :]

            def tile_in(t, g):
                return lambda j: t[:, bass.ds(g * TG + j, 1), :].rearrange("p t d -> p (t d)")

            def signal(ins, s, what, g):
                ins.then_inc(s[what], 1)
                wait(dve, s, what, g + 1)

            dve.wait_ge(x_in, 32)
            dve.wait_ge(w_in, 16 * (len(MATS) + len(BIASES)))
            c = Chain(dve, dA["steps"], CHAIN["a"], dA.base["steps"])
            with dve.Fori(0, NG) as g:
                c.turn(g)
                layer_norm(c, dA, g, tile_in(X, g), XN)
                signal(V.tensor_scalar(XN[:, :, :], XN[:, :, :], 0.0, None, ALU.max), dA, "h", g)
                c.link(copied(turn_of(Y, g), XN[:, :, :]))
                wait(dve, dA, "mm", g + 1)
                wait(dve, dA, "free", g + 1)
                signal(V.tensor_tensor(HS[:, :, :], Rt[1], over_tiles(bias["bn"]), ALU.add), dA, "hp", g)
                c.link(copied(turn_of(Q, g), HS[:, :, :]))
                c.end()
            bucket(1, DSTI, SRCI)
            def take_list(o):
                dve.wait_ge(sort[o]["listed"], 16)
                V.tensor_copy(LO[o][:, :], LIST[:, :, 1]).then_inc(taken, 1)
                dve.wait_ge(taken, o + 1)

            take_list(0)
            V.memset(ACC[:, :], 0.0)
            V.memset(OUTD, 0.0)
            end_phase(dve, "dve")

            def edge_pass(name, o):
                s, kind = ps[name], kind_of(name)
                w = {"att": L1W, "diff": AW}.get(kind, TABLE[name][1])
                G = Gw if kind == "att" else Gn

                def onehot(it, u):
                    gi = it * 4 + u
                    V.tensor_tensor(OH[:, u % 4, :, :], over_tiles(IOTA[:, :], S4),
                                    over_features(LO[o][:, bass.ds(gi * S4, S4)]), ALU.is_equal)\
                        .then_inc(s["oh"], 1)

                def add(it, u, tiles, j):
                    gi = it * 4 + u
                    if j == 0:
                        wait(dve, s, "agg", gi + 1)
                    wait(dve, s, "acc", gi * S4 + j)
                    at = j * 512 if kind == "diff" else u % 2 * 1024 + j * 256
                    dst = ACC[:, bass.ds(tiles[j] * w, w)]
                    V.tensor_tensor(dst, dst, SUMS[:, at:at + w], ALU.add).then_inc(s["acc"], 1)

                def body(it, u):
                    gi = it * 4 + u
                    later = (it if u < 1 else it + 1, (u + 3) % 4)
                    before = (it, u - 1) if u else (it - 1, 3)
                    tiles = None
                    if not (isinstance(gi, int) and gi == 0):
                        tiles = step_tiles(dve, o, before[0] * 4 + before[1])

                    def sums(*js):
                        for j in js if tiles else ():
                            add(*before, tiles, j)

                    if kind != "sum":
                        wait(dve, s, "exp", gi + 1)
                        wait(dve, s, "gath", (it + 1) * (16 * S4), u)
                        rows = R[1][:, (u % 2) * 512:(u % 2) * 512 + 512].rearrange("p (s w) -> p s w", s=S4)
                    if kind == "diff":
                        wait(dve, s, "msg", gi)
                        V.tensor_tensor(PROD[:, :, :], rows, G[:, u, :, 0:D], ALU.subtract).then_inc(s["att"], 1)
                        sums(0)
                        if exists(gi + 3):
                            onehot(*later)
                        sums(1, 2, 3)
                    elif kind == "sum":
                        sums(0)
                        if exists(gi + 3):
                            onehot(*later)
                        sums(1, 2, 3)
                    else:
                        V.tensor_tensor(PROD[:, :, :], rows, G[:, u, :, 0:D], ALU.mult).then_inc(s["prod"], 1)
                        wait(dve, s, "prod", gi + 1)
                        wait(dve, s, "ex", gi)
                        V.tensor_reduce(EATT[:, :, :], heads(PROD[:, :, :]), AX.X, ALU.add).then_inc(s["red"], 1)
                        sums(0)
                        wait(dve, s, "red", gi + 1)
                        V.tensor_scalar(EATT[:, :, :], EATT[:, :, :], -50.0, 50.0, ALU.max, ALU.min)\
                            .then_inc(s["att"], 1)
                        if exists(gi + 3):
                            onehot(*later)
                        sums(1)
                        wait(dve, s, "ex", gi + 1)
                        V.tensor_tensor(heads(M[:, u % 2, :, 0:D]), heads(G[:, u, :, D:2 * D]),
                                        over_heads(M[:, u % 2, :, D:D + HEADS]), ALU.mult).then_inc(s["msg"], 1)
                        sums(2, 3)

                if kind == "att":
                    V.memset(M[:, :, :, D + HEADS:L1W], 1.0)
                if kind == "diff":
                    V.memset(M[:, :, :, D:D + 1], 1.0)
                for u in range(3):
                    onehot(0, u)
                per_group(dve, body)
                tiles = step_tiles(dve, o, GROUPS - 1)
                for j in range(S4):
                    add(GROUPS // 4 - 1, 3, tiles, j)
                if kind == "diff":
                    wait(dve, s, "acc", S4 * GROUPS)
                    V.tensor_copy(OUTD, accv[AW][:, :, 2 * D])
                end_phase(dve, "dve")

            edge_pass("diff", 0)

            c = Chain(dve, dB["steps"], CHAIN["b"], dB.base["steps"])
            with dve.Fori(0, NG) as g:
                c.turn(g)
                copied(CT[:, 0, :], OUTD[:, bass.ds(g * TG, TG)])
                c.link(V.tensor_scalar(CT[:, 1, :], OUTD[:, bass.ds(g * TG, TG)], 1.0, None, ALU.max))
                c.link(V.reciprocal(CT[:, 1, :], CT[:, 1, :]))
                wait(dve, dB, "mm", g + 1)
                for j in range(TG):
                    ins = V.scalar_tensor_tensor(XN[:, j, :], bias["be"], CT[:, 0, j:j + 1], Rt[3][:, j, :],
                                                 ALU.mult, ALU.add)
                c.link(ins)
                c.link(V.tensor_tensor(XN[:, :, :], XN[:, :, :], turn_of(Q, g), ALU.add))
                signal(V.tensor_tensor(XN[:, :, :], XN[:, :, :], over_features(CT[:, 1, :]), ALU.mult), dB, "s", g)
                wait(dve, dB, "z", g + 1)
                c.link(V.tensor_tensor(XN[:, :, :], Rt[1], over_tiles(bias["bl"]), ALU.add))
                c.link(V.tensor_tensor(turn_of(X, g), turn_of(X, g), XN[:, :, :], ALU.add))
                layer_norm(c, dB, g, tile_in(X, g), XN)
                c.link(V.tensor_scalar(turn_of(Y, g), XN[:, :, :], 0.0, None, ALU.max))
                c.end()
            mean = (E + N) / N
            c = Chain(dve, deg_step, 100)
            c.turn(0)
            c.link(V.tensor_scalar(DEGN, OUTD, 1.0, -mean, ALU.add, ALU.add))
            c.link(V.tensor_tensor(TMPN, DEGN, MASK, ALU.mult))
            c.link(V.tensor_tensor(TMPN, TMPN, TMPN, ALU.mult))
            V.tensor_reduce(SMALL[:, 0:1], TMPN, AX.X, ALU.add).then_inc(deg_sum, 1)
            dve.wait_ge(deg_tot, 1)
            V.tensor_scalar(RO, OUTD, 1.0, None, ALU.max).then_inc(root_in, 2)
            dve.wait_ge(root_out, 2)
            c.link(V.tensor_scalar(SMALL[:, 2:3], SMALL[:, 1:2], 1e-6, None, ALU.add))
            c.link(V.reciprocal(SMALL[:, 3:4], SMALL[:, 2:3]))
            c.link(V.tensor_scalar(DEGN, DEGN, SMALL[:, 3:4], None, ALU.mult))
            c.link(V.reciprocal(RO, RO))
            end_dense(dve)

            for l in range(2):
                s = dD[l]
                dve.wait_ge(w_l1, 16 * (len(L1MATS) + len(L1ROWS) + 3) * (l + 1))
                c = Chain(dve, dD_pre[l], 2)
                c.turn(0)
                c.link(V.tensor_tensor(row["bpos"], row["bpos"], row["bdeg"], ALU.add))
                c.link(V.tensor_scalar(row["bq"], row["bq"], float(HD) ** -0.5, None, ALU.mult))
                c = Chain(dve, s["steps"], CHAIN[f"d{l}"], s.base["steps"])
                with dve.Fori(0, NG) as g:
                    c.turn(g)
                    layer_norm(c, s, g, tile_in(Y, g), XN)
                    c.link(V.tensor_tensor(XN[:, :, :], XN[:, :, :], over_tiles(row["ln1_g"]), ALU.mult))
                    signal(V.tensor_tensor(XN[:, :, :], XN[:, :, :], over_tiles(row["ln1_b"]), ALU.add), s, "xn", g)
                    copied(CT[:, 0, :], DEGN[:, bass.ds(g * TG, TG)])
                    wait(dve, s, "pos", g + 1)
                    c.link(V.tensor_tensor(XP[:, :, :], Rt[1], over_tiles(row["bpos"]), ALU.add))
                    for j in range(TG):
                        ins = V.scalar_tensor_tensor(XP[:, j, :], row["Wdeg"], CT[:, 0, j:j + 1], XP[:, j, :],
                                                     ALU.mult, ALU.add)
                    c.link(ins)
                    signal(V.tensor_tensor(XP[:, :, :], XP[:, :, :], XN[:, :, :], ALU.add), s, "xp", g)
                    wait(dve, s, "qkv", g + 1)
                    c.link(V.scalar_tensor_tensor(turn_of(Q, g), Rt[1], float(HD) ** -0.5, over_tiles(row["bq"]),
                                                  ALU.mult, ALU.add))
                    wait(dve, s, "free", g + 1)
                    c.link(V.tensor_tensor(KV[:, :, 0:D], Rt[2], over_tiles(row["bk"]), ALU.add))
                    signal(V.tensor_tensor(KV[:, :, D:2 * D], Rt[3], over_tiles(row["bv"]), ALU.add), s, "kv", g)
                    c.link(V.tensor_tensor(XP[:, :, :], turn_of(Q, g), KV[:, :, 0:D], ALU.mult))
                    c.link(V.tensor_reduce(ATT[:, :, :], heads(XP[:, :, :]), AX.X, ALU.add))
                    signal(V.tensor_scalar(ATT[:, :, :], ATT[:, :, :], -50.0, 50.0, ALU.max, ALU.min), s, "att", g)
                    wait(dve, s, "ex", g + 1)
                    acc = turn_of(accv[L1W], g)
                    c.link(V.tensor_tensor(heads(acc[:, :, 0:D]), heads(KV[:, :, D:2 * D]), over_heads(EX[:, :, :]),
                                           ALU.mult))
                    c.link(copied(acc[:, :, D:D + HEADS], EX[:, :, :]))
                    c.link(copied(acc[:, :, D + HEADS:L1W], ZERO[:, 0:TG].unsqueeze(2)))
                    c.end()
                end_phase(dve, "dve")
                if l == 0:
                    take_list(1)
                edge_pass(f"att{l}", 1)
                if l == 0:
                    c = Chain(dve, ind_step, 5)
                    c.turn(0)
                    c.link(V.tensor_copy(IND, accv[L1W][:, :, D + HEADS]))
                    c.link(V.tensor_scalar(RI, IND, 1.0, None, ALU.max))
                    V.tensor_scalar(DI, IND, 1.0, None, ALU.add).then_inc(root_in, 1)
                    dve.wait_ge(root_out, 3)
                    c.link(V.reciprocal(NODE[:, 4:6, :], NODE[:, 4:6, :]))
                s = dE[l]
                c = Chain(dve, s["steps"], CHAIN[f"e{l}"], s.base["steps"])
                with dve.Fori(0, NG) as g:
                    c.turn(g)
                    acc = turn_of(accv[L1W], g)
                    c.link(V.reciprocal(RSUM[:, :, :], acc[:, :, D:D + HEADS]))
                    signal(V.tensor_tensor(heads(XN[:, :, :]), heads(acc[:, :, 0:D]), over_heads(RSUM[:, :, :]),
                                           ALU.mult), s, "ag", g)
                    wait(dve, s, "o", g + 1)
                    c.link(V.tensor_tensor(XN[:, :, :], Rt[1], over_tiles(row["bo"]), ALU.add))
                    c.link(V.tensor_tensor(turn_of(Y, g), turn_of(Y, g), XN[:, :, :], ALU.add))
                    layer_norm(c, s, g, tile_in(Y, g), XN, 1 + l)
                    c.link(V.tensor_tensor(XN[:, :, :], XN[:, :, :], over_tiles(row["ln2_g"]), ALU.mult))
                    signal(V.tensor_tensor(XN[:, :, :], XN[:, :, :], over_tiles(row["ln2_b"]), ALU.add), s, "xn", g)
                    wait(dve, s, "o2", g + 1)
                    c.link(V.tensor_tensor(XN[:, :, :], Rt[0], over_tiles(row["b2"]), ALU.add))
                    c.link(V.tensor_tensor(turn_of(Y, g), turn_of(Y, g), XN[:, :, :], ALU.add))
                    if l == 1:
                        c.link(V.tensor_tensor(turn_of(X, g), turn_of(X, g), turn_of(Y, g), ALU.add))
                        layer_norm(c, s, g, tile_in(X, g), XN, 2, 1)
                        c.link(V.tensor_scalar(XN[:, :, :], XN[:, :, :], 0.0, None, ALU.max))
                        wait(dve, s, "free", g + 1)
                        signal(V.tensor_tensor(XP[:, :, :], XN[:, :, :], over_features(RO[:, bass.ds(g * TG, TG)]),
                                               ALU.mult), s, "hs", g)
                    c.end()
                if l == 1:
                    V.memset(ACC[:, 0:NT * D], 0.0)
                end_phase(dve, "dve")

            edge_pass("conv", 1)
            c = Chain(dve, dF["steps"], CHAIN["f"], dF.base["steps"])
            with dve.Fori(0, NG) as g:
                c.turn(g)
                signal(V.tensor_tensor(XN[:, :, :], turn_of(accv[D], g), over_features(RI[:, bass.ds(g * TG, TG)]),
                                       ALU.mult), dF, "ag", g)
                wait(dve, dF, "o", g + 1)
                c.link(V.tensor_tensor(XN[:, :, :], Rt[1], over_tiles(bias["bg"]), ALU.add))
                c.link(V.tensor_scalar(XN[:, :, :], XN[:, :, :], 0.0, None, ALU.max))
                c.link(V.tensor_tensor(turn_of(X, g), turn_of(X, g), XN[:, :, :], ALU.add))
                layer_norm(c, dF, g, tile_in(X, g), XN)
                signal(V.tensor_scalar(XN[:, :, :], XN[:, :, :], 0.0, None, ALU.max), dF, "h", g)
                wait(dve, dF, "mm", g + 1)
                wait(dve, dF, "free", g + 1)
                signal(V.tensor_tensor(HS[:, :, :], Rt[1], over_features(DI[:, bass.ds(g * TG, TG)]), ALU.mult),
                       dF, "hs", g)
                c.link(copied(turn_of(accv[D], g), HS[:, :, :]))
                c.end()
            end_phase(dve, "dve")
            edge_pass("gcn1", 1)
            c = Chain(dve, dG["steps"], CHAIN["g"], dG.base["steps"])
            with dve.Fori(0, NG) as g:
                c.turn(g)
                c.link(V.tensor_tensor(XN[:, :, :], turn_of(accv[D], g), over_features(DI[:, bass.ds(g * TG, TG)]),
                                       ALU.mult))
                c.link(V.tensor_tensor(XN[:, :, :], XN[:, :, :], over_tiles(bias["b31"]), ALU.add))
                signal(V.tensor_scalar(XN[:, :, :], XN[:, :, :], 0.0, None, ALU.max), dG, "h", g)
                wait(dve, dG, "mm", g + 1)
                wait(dve, dG, "free", g + 1)
                signal(V.tensor_tensor(HS64[:, :, :], R[1][:, 0:TG * DZ].rearrange("p (t d) -> p t d", t=TG),
                                       over_features(DI[:, bass.ds(g * TG, TG)], DZ), ALU.mult), dG, "hs", g)
                c.link(copied(turn_of(accv[DZ], g), HS64[:, :, :]))
                c.end()
            end_phase(dve, "dve")
            edge_pass("gcn2", 1)
            c = Chain(dve, dH["steps"], CHAIN["h"], dH.base["steps"])
            with dve.Fori(0, NG) as g:
                c.turn(g)
                c.link(V.tensor_tensor(Z64[:, :, :], turn_of(accv[DZ], g),
                                       over_features(DI[:, bass.ds(g * TG, TG)], DZ), ALU.mult))
                signal(V.tensor_tensor(Z64[:, :, :], Z64[:, :, :], over_tiles(bias["b32"][:, 0:DZ]), ALU.add),
                       dH, "z", g)
                wait(dve, dH, "mm", g + 1)
                signal(V.tensor_tensor(XN[:, :, :], Rt[1], over_tiles(bias["bd"]), ALU.add), dH, "y", g)
                wait(dve, dH, "sg", g + 1)
                c.link(V.tensor_tensor(turn_of(X, g), turn_of(X, g), XP[:, :, :], ALU.add))
                c.end()
            end_phase(dve, "dve")


def kernel(**inputs):
    import numpy as np
    import concourse.bacc as bacc
    from concourse.bass_utils import run_bass_kernel_spmd as run

    i = {k: np.asarray(v) for k, v in inputs.items()}
    t = np.ascontiguousarray
    host = {"x": i["x"], "src": i["src"], "dst": i["dst"]}
    host["Wn"] = t(i["L0_gnn_W_neigh"].T)
    host["We1"], host["We2"] = t(i["L0_gnn_W_edge"].T[:D]), t(i["L0_gnn_W_edge"].T[D:])
    host["Wl1"], host["Wl2"] = t(i["L0_gnn_W_lin"].T[:D]), t(i["L0_gnn_W_lin"].T[D:])
    host["bn"], host["be"], host["bl"] = i["L0_gnn_b_neigh"], i["L0_gnn_b_edge"], i["L0_gnn_b_lin"]
    for n in ("Wpos", "Wq", "Wk", "Wv", "Wo", "bpos", "bdeg", "Wdeg", "bq", "bk", "bv", "bo", "ln1_g", "ln1_b",
              "ln2_g", "ln2_b", "b2", "W1", "W2"):
        host[n] = i["L1_gnn_" + n]
    host["b1t"] = t(i["L1_gnn_b1"].reshape(2, FF // P, P).transpose(0, 2, 1))
    host["Wg"], host["bg"] = i["L2_gnn_weight"], i["L2_gnn_bias"]
    host["W31"], host["b31"], host["W32"], host["b32"] = (i["L3_gnn_" + n] for n in ("W1", "b1", "W2", "b2"))
    host["Wd"], host["bd"] = i["L3_gnn_Wd"], i["L3_gnn_bd"]

    nc = bacc.Bacc("TRN2", target_bir_lowering=False, num_devices=1)
    a, arrays = {}, {}
    for n, v in host.items():
        arrays["in_" + n] = t(v)
        a[n] = nc.dram_tensor("in_" + n, v.shape, mybir.dt.from_np(v.dtype), kind="ExternalInput").ap()
    out = nc.dram_tensor("out_x", (N, D), F32, kind="ExternalOutput").ap()
    build(nc, a, out)
    return run(nc, [arrays], core_ids=[0]).results[0]["out_x"]
```

```python
import concourse.bass as bass
from concourse import mybir
from contextlib import ExitStack

F32 = mybir.dt.float32
I32 = mybir.dt.int32
ALU = mybir.AluOpType
ACT = mybir.ActivationFunctionType
AX = mybir.AxisListType

P = 128
N, E, D = 6250, 100000, 128
HEADS, HD, FF, DZ = 8, 16, 512, 64
NT = -(-N // P)
LAST = N - (NT - 1) * P
TG = 7
NG = NT // TG
assert NG * TG == NT
SB = 28
EC = -(-E // (P * 2 * SB)) * 2 * SB
EFULL, EREST = E // EC, E % EC
RB = 7
assert NT % RB == 0
PARTS = (0, 2, 7, EC // (2 * SB))
EARLY = 14
S4 = 4
PB = 16
STEPS = -(-((E - NT) // P + NT) // (2 * PB)) * 2 * PB
GROUPS = STEPS // S4
GTURNS = STEPS // PB // 4
TURNS = [EC // (2 * SB), (EC - EARLY * (GTURNS - 1)) // (2 * SB)]
assert TURNS[1] * 2 * SB + EARLY * (GTURNS - 1) == EC
AW = 2 * D + 1
L1W = D + HEADS + 1
OUT_OF_RANGE = 1 << 20
ENGINES = 5
CHAIN = {"a": 5, "b": 10, "d0": 3, "e0": 4, "d1": 3, "e1": 4, "f": 4, "g": 0, "h": 0}


TAIL = {"d0": 7, "e0": 2, "d1": 7, "e1": 6, "f": 1, "g": 1, "h": 1}


class Events(dict):
    pass


def wait(eng, s, what, value, slot=None):
    if isinstance(value, int) and value <= 0:
        return
    eng.wait_ge(s[what] if slot is None else s[what][slot], value + s.base[what])


def gated(eng, passed):
    eng.sem_inc(passed)


class Chain:

    def __init__(self, eng, sem, per, base=0):
        self.eng, self.sem, self.per, self.base = eng, sem, per, base

    def turn(self, g):
        self.start, self.k = g * self.per + self.base, 0

    def link(self, ins):
        self.k += 1
        ins.then_inc(self.sem, 1)
        self.eng.wait_ge(self.sem, self.start + self.k)

    def end(self):
        assert self.k == self.per, (self.base, self.k, self.per)


def build(nc, a, out):
    with ExitStack() as ctx:
        def sb(name, shape, dt=F32):
            return ctx.enter_context(nc.sbuf_tensor(name, shape, dt))

        def sem(name):
            return ctx.enter_context(nc.semaphore(name))

        tab_h = nc.dram_tensor("tab_h", (NT * P, D), F32, kind="Internal").ap()
        tab_kv = nc.dram_tensor("tab_kv", (NT * P, 2 * D), F32, kind="Internal").ap()
        tab_z = nc.dram_tensor("tab_z", (NT * P, DZ), F32, kind="Internal").ap()
        lists = [nc.dram_tensor(f"list{o}", (P * STEPS, 2), I32, kind="Internal").ap() for o in range(2)]

        X = sb("X", [P, NT, D])
        Y = sb("Y", [P, NT, D])
        Q = sb("Q", [P, NT, D])
        ACC = sb("ACC", [P, NT * AW])
        accv = {w: ACC[:, 0:NT * w].rearrange("p (t w) -> p t w", w=w) for w in (AW, L1W, D, DZ)}
        LO = [sb(f"LO{o}", [P, STEPS]) for o in range(2)]
        TILE = [sb(f"TILE{o}", [1, STEPS], I32) for o in range(2)]
        RECS = sb("RECS", [P, 3, EC], I32)
        SCR = sb("SCR", [P, 7296])
        IOTA = sb("IOTA", [P, P])
        IDENT = sb("IDENT", [P, P])
        ONES = sb("ONES", [P, P])
        ZERO = sb("ZERO", [P, D])
        STAGE = sb("STAGE", [P, 4, PB, 2], I32)
        SLOTS = sb("SLOTS", [P, 2, SB], I32)
        PAIRS = sb("PAIRS", [P, 2, SB, 2], I32)
        WMAT = sb("WMAT", [P, 11, D])
        WL1 = sb("WL1", [P, 5, D])
        WF1 = sb("WF1", [P, FF])
        WF2 = sb("WF2", [P, FF // P, D])
        B1T = sb("B1T", [P, FF // P])
        BL1 = sb("BL1", [P, 10, D])
        BIAS = sb("BIAS", [P, 5, D])
        COLUMNS = sb("COLUMNS", [P, 6])
        NODE = sb("NODE", [P, 8, NT])
        OUTD, IND, DEGN, RO, RI, DI, TMPN, MASK = (NODE[:, i, :] for i in range(8))
        ST = sb("ST", [P, TG, 6])
        MV = sb("MV", [P, TG, 2])
        RSTD = sb("RSTD", [P, TG])
        SD = sb("SD", [P, TG])
        EPS = sb("EPS", [P, 1])
        CT = sb("CT", [P, 2, TG])
        SMALL = sb("SMALL", [P, 8])
        RSUM = sb("RSUM", [P, TG, HEADS])
        EX = sb("EX", [P, TG, HEADS])
        ATT = sb("ATT", [P, TG, HEADS])

        Gn = SCR[:, 0:4 * S4 * D].rearrange("p (r s w) -> p r s w", r=4, s=S4)
        Gw = ACC[:, NT * L1W:NT * L1W + 8 * S4 * D].rearrange("p (r s w) -> p r s w", r=4, s=S4)
        OH = SCR[:, 2048:4096].rearrange("p (r s w) -> p r s w", r=4, s=S4)
        OHT = SCR[:, 4096:5120].rearrange("p (r s w) -> p r s w", r=2, s=S4)
        M = SCR[:, 5120:5120 + 2 * S4 * L1W].rearrange("p (r s w) -> p r s w", r=2, s=S4)
        PROD = SCR[:, 6656:7168].rearrange("p (s w) -> p s w", s=S4)
        EATT = SCR[:, 7168:7168 + S4 * HEADS].rearrange("p (s h) -> p s h", s=S4)
        def tmp(i, w=1):
            return SCR[:, i * TG * D:(i + w) * TG * D]
        XN = tmp(0).rearrange("p (t d) -> p t d", t=TG)
        XP = tmp(1).rearrange("p (t d) -> p t d", t=TG)
        T1, T2, T3 = tmp(2), tmp(3), tmp(4)
        KV = tmp(5, 2).rearrange("p (t d) -> p t d", t=TG)
        HT = tmp(3, 4).rearrange("p (c n) -> p c n", c=FF // P)
        T4 = tmp(7)
        XB = ACC[:, NT * L1W:NT * L1W + TG * D].rearrange("p (t d) -> p t d", t=TG)
        XG = ACC[:, NT * L1W + TG * D:NT * L1W + 2 * TG * D].rearrange("p (t d) -> p t d", t=TG)
        HS = tmp(5).rearrange("p (t d) -> p t d", t=TG)
        HS64 = tmp(5)[:, 0:TG * DZ].rearrange("p (t d) -> p t d", t=TG)
        Z64 = tmp(6)[:, 0:TG * DZ].rearrange("p (t d) -> p t d", t=TG)
        LIST = SCR[:, 5376:5376 + 2 * STEPS].bitcast(I32).rearrange("p (s two) -> p s two", two=2)
        col = [ACC[:, i * EC:(i + 1) * EC] for i in range(16)]
        SRCI, DSTI = col[0].bitcast(I32), col[1].bitcast(I32)
        HII, HI, RANK = col[2].bitcast(I32), col[3], col[6]
        EQS, CUMS = (col[4], col[13]), (col[5], col[14])
        SLOT, VAL, LOC = ([col[i].bitcast(I32), RECS[:, k, :]] for k, i in enumerate((7, 8, 9)))
        POSA, POSB = col[13].bitcast(I32), col[14].bitcast(I32)
        Qf = Q[:, :, :].rearrange("p t d -> p (t d)")
        GE, ONESC = ACC[:, 13 * EC:13 * EC + STEPS], col[15]
        small = tmp(3, 2)
        IOTAS = small[:, 0:STEPS]
        BEFORE = small[:, STEPS:STEPS + P]
        STARTP = small[:, STEPS + P:STEPS + 2 * P]
        CNT, NST, INCL, STARTS, BASE, NSTI, STARTT = (
            small[:, STEPS + 2 * P + i * 64:STEPS + 2 * P + i * 64 + NT] for i in range(7))
        NSTI, STARTT = NSTI.bitcast(I32), STARTT[:, 0:1]

        R = [ctx.enter_context(nc.psum_tensor(f"R{i}", [P, 1024], F32)) for i in range(2)]
        SUMS = ctx.enter_context(nc.psum_tensor("SUMS", [P, 2048], F32))
        R += [SUMS[:, 0:1024], SUMS[:, 1024:2048]]
        Rt = [r[:, 0:TG * D].rearrange("p (t d) -> p t d", t=TG) for r in R]

        phase_done, dense_done, passed = sem("phase_done"), sem("dense_done"), sem("passed")
        phase = {}

        def end_phase(eng, key):
            n = phase[key] = phase.get(key, 0) + 1
            eng.drain().then_inc(phase_done, 1)
            eng.wait_ge(phase_done, ENGINES * n)

        def end_dense(eng):
            eng.drain().then_inc(dense_done, 1)
            eng.wait_ge(dense_done, ENGINES - 1)

        MATS = ["Wn", "We1", "We2", "Wl1", "Wl2", "Wg", "W31", "W32", "Wd"]
        mat = {n: WMAT[:, i, :] for i, n in enumerate(MATS)}
        BIASES = ["bn", "be", "bl", "bg", "bd"]
        bias = {n: BIAS[:, i, :] for i, n in enumerate(BIASES)}
        L1MATS = ["Wpos", "Wq", "Wk", "Wv", "Wo"]
        l1mat = {n: WL1[:, i, :] for i, n in enumerate(L1MATS)}
        L1ROWS = ["bpos", "bdeg", "Wdeg", "bq", "bk", "bv", "bo", "ln1_g", "ln1_b", "b2"]
        row = {n: BL1[:, i, :] for i, n in enumerate(L1ROWS)}
        L1COLUMNS = ["ln1_g", "ln1_b", "ln2_g", "ln2_b"]
        column = {n: COLUMNS[:, i:i + 1] for i, n in enumerate(L1COLUMNS + ["b31", "b32"])}
        LOADS = len(MATS) + len(BIASES) + 2
        L1LOADS = len(L1MATS) + len(L1ROWS) + len(L1COLUMNS) + 3

        def over_tiles(b, n=TG):
            return b.unsqueeze(1).broadcast_to([P, n, b.shape[1]])

        def over_features(s, w=D):
            return s.unsqueeze(2).broadcast_to([P, s.shape[1], w])

        def over_heads(s):
            return s.unsqueeze(3).broadcast_to([P, s.shape[1], HEADS, HD])

        def heads(ap):
            return ap.rearrange("p t (h d) -> p t h d", h=HEADS)

        edges_in, x_in, w_in, w_l1, x_pad = sem("edges_in"), sem("x_in"), sem("w_in"), sem("w_l1"), sem("x_pad")
        const_ready, const_step = sem("const_ready"), sem("const_step")
        early_staged, early_sent = sem("early_staged"), sem("early_scattered")
        taken = sem("node_numbers_taken")
        ids_cleared, list_cleared, clear_ready = sem("ids_cleared"), sem("list_cleared"), sem("clear_ready")
        sort = [dict(step=sem(f"rank_step{o}"), counted=sem(f"bucket_counted{o}"), misc=sem(f"sort_step{o}"),
                     counts=sem(f"counts_ready{o}"), sums=sem(f"bucket_sums{o}"), startp=sem(f"starts_ready{o}"),
                     startt=sem(f"starts_transposed{o}"), ge=sem(f"reached_ready{o}"), tiles=sem(f"tiles_summed{o}"),
                     slots=sem(f"slots_ready{o}"), staged=sem(f"scatter_staged{o}"),
                     sent=[sem(f"scattered{o}_{u}") for u in range(2)], listed=sem(f"list_loaded{o}"))
                for o in range(2)]
        PASSES = ["diff", "att0", "att1", "conv", "gcn1", "gcn2"]
        once = ("oh", "tr", "oht", "exp", "prod", "att", "ex", "msg", "agg")
        names = dict(oh="onehot_built", tr="onehot_transposed", oht="onehot_t_copied",
                     exp="rows_expanded", prod="products_ready", red="products_reduced", att="scores_ready",
                     ex="exp_ready", msg="messages_ready", agg="edges_summed", acc="sums_added")
        sems = {k: sem(v) for k, v in names.items()}
        sems["staged"] = [sem(f"indices_staged{u}") for u in range(4)]
        sems["gath"] = [sem(f"gathered{u}") for u in range(4)]

        def kind_of(n):
            return "att" if n.startswith("att") else "diff" if n == "diff" else "sum"

        def counts_of(n):
            c = {k: GROUPS for k in once}
            c.update(staged=16 * STEPS // PB // 4, gath=16 * S4 * GROUPS // 4, acc=S4 * GROUPS, red=GROUPS)
            unused = {"att": (), "diff": ("prod", "ex", "red"), "sum": ("tr", "oht", "exp", "prod", "red", "att", "ex", "msg")}
            c.update({k: 0 for k in unused[kind_of(n)]})
            return c

        ps, base = {}, dict.fromkeys(list(sems), 0)
        for n in PASSES:
            ps[n] = Events(sems)
            ps[n].base = dict(base)
            base = {k: base[k] + v for k, v in counts_of(n).items()}

        STAGES = {
            "a": "mv sd h t tc mm hp st free", "b": "mv sd cp fresh s t tc mm zt ztc z",
            "d0": "mv sd xn xt xtc pos xp pt ptc qkv kv st free att ex", "e0": "mv sd ag at atc o xn xt xtc hid gelu o2 agg_steps",
            "d1": "mv sd xn xt xtc pos xp pt ptc qkv kv st free att ex", "e1": "mv sd mv2 sd2 ag at atc o xn xt xtc hid gelu o2 hs st free agg_steps",
            "f": "mv sd ag at atc o h ht htc mm hs st free", "g": "h ht htc mm hs st free", "h": "z zt ztc mm y sg",
        }
        meaning = dict(mv="variance_ready", sd="deviation_ready", h="h_ready", t="transposed", tc="transposed_copied", mm="product_ready", hp="table_rows",
                       st="rows_stored", free="rows_free", cp="copies_ready", fresh="copies_free", s="mean_ready",
                       zt="z_transposed", ztc="z_t_copied", z="z_ready", xn="normed_ready", xt="normed_transposed",
                       xtc="normed_t_copied", pos="pos_ready", xp="xp_ready", pt="xp_transposed", ptc="xp_t_copied",
                       qkv="qkv_ready", kv="kv_rows", att="self_scores", ex="self_exp", ag="aggregate_ready",
                       at="aggregate_transposed", atc="aggregate_t_copied", o="projected", hid="hidden_ready",
                       gelu="gelu_ready", o2="ffn_ready", hs="scaled_rows", ht="h_transposed", htc="h_t_copied",
                       agg_steps="aggregate_steps", tail="tail_steps", y="logits_ready", sg="sigmoid_ready", steps="vector_steps")
        stage_sems = {k: sem(v) for k, v in meaning.items()}
        per_turn = dict(st=16, hid=FF // P, gelu=FF // P)
        dense, base = {}, dict.fromkeys(stage_sems, 0)
        for n, events in STAGES.items():
            dense[n] = Events(stage_sems)
            dense[n].base = dict(base)
            for k in events.split():
                base[k.rstrip("2") if k in ("mv2", "sd2") else k] += \
                    NG * per_turn.get(k, 1) + (k in ("free", "fresh"))
            base["steps"] += NG * CHAIN[n]
            if n[0] == "d":
                base["agg_steps"] += 2 * NG
            base["tail"] += NG * TAIL.get(n, 0)
        dA, dB, dF, dG, dH = (dense[n] for n in "abfgh")
        dD, dE = [dense["d0"], dense["d1"]], [dense["e0"], dense["e1"]]
        deg_step, deg_sum, deg_tot = sem("deg_step"), sem("deg_sum"), sem("deg_tot")
        out_done = sem("out_done")
        dD_pre = [sem(f"bias_step{l}") for l in range(2)]
        root_in, root_out = sem("root_operand_ready"), sem("root_ready")
        ind_step = sem("indegree_step")

        block = ctx.enter_context(nc.Block())

        def per_group(eng, body):
            n = GROUPS // 4
            for u in range(4):
                body(0, u)
            with eng.Fori(1, n - 1) as it:
                for u in range(4):
                    body(it, u)
            for u in range(4):
                body(n - 1, u)

        def exists(gi):
            return not isinstance(gi, int) or gi < GROUPS

        def step_tiles(eng, o, gi):
            _, tiles = nc.values_load_multi_w_load_instructions(
                TILE[o][0:1, bass.ds(gi * S4, S4)], engines=(eng.engine,), min_val=0, max_val=NT - 1,
                skip_runtime_bounds_check_because="a count of the NT buckets that start by the step, less one")
            return tiles

        TABLE = {"diff": (tab_h, D), "att0": (tab_kv, 2 * D), "att1": (tab_kv, 2 * D), "conv": (tab_h, D),
                 "gcn1": (tab_h, D), "gcn2": (tab_z, DZ)}

        @block.sync
        def _(sp):
            sp.wait_ge(ids_cleared, 1)
            for ids, dst in ((a["src"], SRCI), (a["dst"], DSTI)):
                sp.dma_start(dst[0:EFULL, :], ids[0:EFULL * EC].rearrange("(p c) -> p c", c=EC)).then_inc(edges_in, 16)
                sp.dma_start(dst[EFULL:EFULL + 1, 0:EREST],
                             ids[EFULL * EC:E].rearrange("(p c) -> p c", c=EREST)).then_inc(edges_in, 16)
            sp.wait_ge(clear_ready, 1)
            for o in range(2):
                sp.dma_start(lists[o].rearrange("(p s) two -> p s two", s=STEPS), LIST).then_inc(list_cleared, 16)
            sp.wait_ge(x_pad, 1)
            sp.dma_start(X[:, 0:NT - 1, :], a["x"][0:(NT - 1) * P, :].rearrange("(t p) d -> p t d", p=P))\
                .then_inc(x_in, 16)
            sp.dma_start(X[0:LAST, NT - 1, :], a["x"][(NT - 1) * P:N, :]).then_inc(x_in, 16)

            def store(table, src, s, ready):
                view = table.rearrange("(t p) d -> p t d", p=P)
                sp.sem_inc(s["free"])
                with sp.Fori(0, NG) as g:
                    wait(sp, s, ready, g + 1)
                    sp.dma_start(view[:, bass.ds(g * TG, TG), :], src).then_inc(s["st"], 16)
                    wait(sp, s, "st", (g + 1) * 16)
                    sp.sem_inc(s["free"])

            def load_l1(l):
                for n in L1MATS:
                    sp.dma_start(l1mat[n], a[n][l]).then_inc(w_l1, 16)
                for n in L1ROWS:
                    v = a[n][l, 0] if n == "Wdeg" else a[n][l]
                    sp.dma_start(row[n], v.partition_broadcast(P)).then_inc(w_l1, 16)
                for n in L1COLUMNS:
                    sp.dma_start(column[n], a[n][l].rearrange("(k one) -> k one", one=1)).then_inc(w_l1, 16)
                sp.dma_start(WF1[:, :], a["W1"][l]).then_inc(w_l1, 16)
                sp.dma_start(WF2[:, :, :], a["W2"][l].rearrange("(c k) d -> k c d", k=P)).then_inc(w_l1, 16)
                sp.dma_start(B1T[:, :], a["b1t"][l]).then_inc(w_l1, 16)

            def stage_indices(name, o):
                s = ps[name]
                freed = "msg" if kind_of(name) == "att" else "agg"
                entries = lists[o].rearrange("(p s) two -> p s two", s=STEPS)

                def load(it, u, first):
                    b = it * 4 + u
                    if not first:
                        wait(sp, s, freed, b * (PB // S4) - 3 * (PB // S4))
                    sp.dma_start(STAGE[:, u, :, :], entries[:, bass.ds(b * PB, PB), :]).then_inc(s["staged"][u], 16)

                for u in range(4):
                    load(0, u, True)
                with sp.Fori(1, GTURNS) as it:
                    for u in range(4):
                        load(it, u, False)
                end_phase(sp, "sp")

            def load_list(o):
                for u in range(2):
                    sp.wait_ge(sort[o]["sent"][u], 16 * SB * TURNS[o])
                if o == 1:
                    sp.wait_ge(early_sent, 16 * EARLY * (GTURNS - 1))
                sp.dma_start(LIST, lists[o].rearrange("(p s) two -> p s two", s=STEPS)).then_inc(sort[o]["listed"], 16)

            load_l1(0)
            store(tab_h, HS[:, :, :], dA, "hp")
            load_list(0)
            end_phase(sp, "sp")
            stage_indices("diff", 0)
            end_dense(sp)
            for l in range(2):
                store(tab_kv, KV[:, :, :], dD[l], "kv")
                end_phase(sp, "sp")
                if l == 0:
                    load_list(1)
                stage_indices(f"att{l}", 1)
                if l == 1:
                    store(tab_h, XP[:, :, :], dE[l], "hs")
                end_phase(sp, "sp")
                if l == 0:
                    load_l1(1)
            stage_indices("conv", 1)
            store(tab_h, HS[:, :, :], dF, "hs")
            end_phase(sp, "sp")
            stage_indices("gcn1", 1)
            store(tab_z, HS64[:, :, :], dG, "hs")
            end_phase(sp, "sp")
            stage_indices("gcn2", 1)
            end_phase(sp, "sp")
            sp.dma_start(out[0:(NT - 1) * P, :].rearrange("(t p) d -> p t d", p=P), X[:, 0:NT - 1, :])\
                .then_inc(out_done, 16)
            sp.dma_start(out[(NT - 1) * P:N, :], X[0:LAST, NT - 1, :]).then_inc(out_done, 16)
            sp.wait_ge(out_done, 32)

        @block.gpsimd
        def _(pool):
            n = [0]

            def step(ins):
                n[0] += 1
                ins.then_inc(const_step, 1)
                pool.wait_ge(const_step, n[0])

            nc.gpsimd.memset(IDENT[:, :], 0.0)
            nc.gpsimd.memset(ONES[:, :], 1.0)
            nc.gpsimd.memset(ZERO[:, :], 0.0)
            nc.gpsimd.memset(EPS[:, :], 1e-5)
            nc.gpsimd.memset(ONESC, 1.0)
            nc.gpsimd.memset(MASK, 1.0)
            step(nc.gpsimd.memset(BEFORE, 1.0))
            step(nc.gpsimd.iota(IOTA[:, :], [[1, P]], base=0, channel_multiplier=0,
                                allow_small_or_imprecise_dtypes=True))
            step(nc.gpsimd.iota(IOTAS, [[1, STEPS]], base=0, channel_multiplier=0,
                                allow_small_or_imprecise_dtypes=True))
            step(nc.gpsimd.affine_select(out=IDENT[:, :], in_=IDENT[:, :], compare_op=ALU.not_equal, fill=1.0,
                                         base=0, pattern=[[-1, P]], channel_multiplier=1))
            step(nc.gpsimd.affine_select(out=BEFORE, in_=BEFORE, compare_op=ALU.is_gt, fill=0.0,
                                         base=0, pattern=[[1, P]], channel_multiplier=-1))
            nc.gpsimd.affine_select(out=MASK, in_=MASK, compare_op=ALU.is_gt, fill=0.0,
                                    base=N, pattern=[[-P, NT]], channel_multiplier=-1).then_inc(const_ready, 1)

            pool.wait_ge(list_cleared, 32)
            def scatters(o):
                s = sort[o]
                pool.wait_ge(s["slots"], 1)

                def scatter(b, it, u, first):
                    if not first:
                        pool.wait_ge(s["sent"][u], it * (16 * SB))
                        gated(pool, passed)
                    elif o == 1:
                        if u == 0:
                            pool.wait_ge(early_sent, 16 * EARLY * (GTURNS - 1))
                        pool.wait_ge(sort[0]["sent"][u], 16 * SB * TURNS[0])
                    nc.gpsimd.tensor_copy(PAIRS[:, u, :, 0], VAL[o][:, bass.ds(b * SB, SB)])
                    nc.gpsimd.tensor_copy(PAIRS[:, u, :, 1], LOC[o][:, bass.ds(b * SB, SB)])
                    nc.gpsimd.tensor_copy(SLOTS[:, u, :], SLOT[o][:, bass.ds(b * SB, SB)]).then_inc(s["staged"], 1)
                    pool.wait_ge(s["staged"], b + 1)
                    gated(pool, passed)
                    for j in range(SB):
                        nc.gpsimd.indirect_dma_start(
                            lists[o], bass.IndirectOffsetOnAxis(SLOTS[:, u, j:j + 1], 0), PAIRS[:, u, j, :], None,
                            bounds_check=P * STEPS - 1, oob_is_err=False).then_inc(s["sent"][u], 16)

                for u in range(2):
                    scatter(u, 0, u, True)
                for part, (first, last) in enumerate(zip(PARTS[:-1], PARTS[1:])):
                    first, last = max(first, 1), min(last, TURNS[o])
                    pool.wait_ge(s["slots"], part + 1)
                    with pool.Fori(first, last) as it:
                        for u in range(2):
                            scatter(it * 2 + u, it, u, False)

            scatters(0)
            end_phase(pool, "pool")

            def gathers(name, o):
                s, kind = ps[name], kind_of(name)
                table, w = TABLE[name]
                freed = "msg" if kind == "att" else "agg"

                G = Gw if kind == "att" else Gn

                def stage_early(it):
                    first = it * EARLY - EARLY + TURNS[1] * 2 * SB
                    for k in range(2):
                        nc.gpsimd.tensor_copy(PAIRS[:, 0, 0:EARLY, k], RECS[:, k + 1, bass.ds(first, EARLY)])
                    nc.gpsimd.tensor_copy(SLOTS[:, 0, 0:EARLY], RECS[:, 0, bass.ds(first, EARLY)])\
                        .then_inc(early_staged, 1)
                    pool.wait_ge(early_staged, it)
                    gated(pool, passed)

                def scatter_early(u):
                    for j in range(EARLY * u // 3, EARLY * (u + 1) // 3):
                        nc.gpsimd.indirect_dma_start(
                            lists[1], bass.IndirectOffsetOnAxis(SLOTS[:, 0, j:j + 1], 0), PAIRS[:, 0, j, :], None,
                            bounds_check=P * STEPS - 1, oob_is_err=False).then_inc(early_sent, 16)

                def block_of(it, u, first):
                    b = it * 4 + u
                    wait(pool, s, "staged", (it + 1) * 16, u)
                    gated(pool, passed)
                    for q in range(PB // S4):
                        if not (first and u == 0):
                            wait(pool, s, freed, b * (PB // S4) + (q - 3))
                            gated(pool, passed)
                        for j in range(S4):
                            nc.gpsimd.indirect_dma_start(
                                G[:, q, j, 0:w], None, table,
                                bass.IndirectOffsetOnAxis(STAGE[:, u, q * S4 + j, 0:1], 0))\
                                .then_inc(s["gath"][q], 16)
                for u in range(4):
                    block_of(0, u, True)
                if kind == "diff":
                    pool.wait_ge(sort[0]["sent"][0], 16 * SB * TURNS[0])
                    gated(pool, passed)
                with pool.Fori(1, GTURNS) as it:
                    if kind == "diff":
                        stage_early(it)
                    for u in range(4):
                        block_of(it, u, False)
                        if kind == "diff" and u < 3:
                            scatter_early(u)
                    if kind == "diff":
                        pool.wait_ge(early_sent, it * (16 * EARLY))
                        gated(pool, passed)
                end_phase(pool, "pool")

            gathers("diff", 0)
            scatters(1)
            for l in range(2):
                end_phase(pool, "pool")
                gathers(f"att{l}", 1)
                end_phase(pool, "pool")
            gathers("conv", 1)
            end_phase(pool, "pool")
            gathers("gcn1", 1)
            end_phase(pool, "pool")
            gathers("gcn2", 1)
            end_phase(pool, "pool")

        @block.tensor
        def _(pe):
            pe.wait_ge(const_ready, 1)
            def bucket_sums(o):
                s = sort[o]
                pe.wait_ge(s["counts"], 1)
                nc.tensor.matmul(R[0][:, 0:NT], BEFORE, CNT, start=True, stop=True)
                nc.tensor.matmul(R[0][:, 512:512 + NT], ONES[:, :], CNT, start=True, stop=True).then_inc(s["sums"], 1)
                pe.wait_ge(s["startp"], 1)
                nc.tensor.transpose(R[1][:, 0:P], STARTP, IDENT[:, :]).then_inc(s["startt"], 1)
                pe.wait_ge(s["ge"], 1)
                h = STEPS // 2
                nc.tensor.matmul(R[2][:, 0:h], ONES[:, :], GE[:, 0:h], start=True, stop=True)
                nc.tensor.matmul(R[2][:, 512:512 + h], ONES[:, :], GE[:, h:STEPS], start=True, stop=True)\
                    .then_inc(s["tiles"], 1)

            def transposes(dst, src, sig, w=D):
                for j in range(TG):
                    ins = nc.tensor.transpose(dst[0:w, j * P:(j + 1) * P], src(j), IDENT[:, :])
                if sig is not None:
                    ins.then_inc(sig, 1)

            def products(dst, pairs, sig):
                for j in range(TG):
                    for k, (t, w) in enumerate(pairs):
                        ins = nc.tensor.matmul(dst[:, j, :], t(j), w, start=k == 0, stop=k == len(pairs) - 1)
                if sig is not None:
                    ins.then_inc(sig, 1)

            def tile_of(t, k=P):
                return lambda j: t[0:k, j * P:(j + 1) * P]

            bucket_sums(0)
            pe.wait_ge(w_in, 16 * LOADS)
            with pe.Fori(0, NG) as g:
                wait(pe, dA, "h", g + 1)
                transposes(R[0], lambda j: XN[:, j, :], dA["t"])
                wait(pe, dA, "tc", g + 1)
                products(Rt[1], [(tile_of(T1), mat["Wn"])], dA["mm"])
            bucket_sums(1)
            end_phase(pe, "pe")

            def edge_pass(name, o):
                s, kind = ps[name], kind_of(name)
                w = {"att": L1W, "diff": D}.get(kind, TABLE[name][1])
                G = Gn

                def transpose(it, u):
                    gi = it * 4 + u
                    wait(pe, s, "oh", gi + 1)
                    wait(pe, s, "oht", gi - 1)
                    for j in range(S4):
                        ins = nc.tensor.transpose(R[0][:, (u % 2) * 512 + j * P:(u % 2) * 512 + (j + 1) * P],
                                                  OH[:, u % 4, j, :], IDENT[:, :])
                    ins.then_inc(s["tr"], 1)

                def expand(it, u):
                    gi = it * 4 + u
                    tiles = step_tiles(pe, o, gi)
                    wait(pe, s, "oht", gi + 1)
                    wait(pe, s, "att", gi - 1)
                    for j in range(S4):
                        ins = nc.tensor.matmul(R[1][:, (u % 2) * 512 + j * P:(u % 2) * 512 + (j + 1) * P],
                                               OHT[:, u % 2, j, :], Qf[:, bass.ds(tiles[j] * D, D)],
                                               start=True, stop=True)
                    ins.then_inc(s["exp"], 1)

                def summed(it, u):
                    gi = it * 4 + u
                    wait(pe, s, "oh", gi + 1)
                    if kind != "sum":
                        wait(pe, s, "msg", gi + 1)
                    if kind != "att":
                        wait(pe, s, "gath", (it + 1) * (16 * S4), u)
                    wait(pe, s, "acc", gi * S4 if kind == "diff" else gi * S4 - S4)
                    for j in range(S4):
                        oh = OH[:, u % 4, j, :]
                        at = j * 512 if kind == "diff" else u % 2 * 1024 + j * 256
                        dst = SUMS[:, at:at + w]
                        if kind == "att":
                            ins = nc.tensor.matmul(dst, oh, M[:, u % 2, j, :], start=True, stop=True)
                        else:
                            ins = nc.tensor.matmul(dst, oh, G[:, u, j, 0:w], start=True, stop=True)
                        if kind == "diff":
                            ins = nc.tensor.matmul(SUMS[:, at + D:at + AW], oh, M[:, u % 2, j, 0:D + 1],
                                                   start=True, stop=True)
                    ins.then_inc(s["agg"], 1)

                def body(it, u):
                    gi = it * 4 + u
                    if kind != "sum":
                        if exists(gi + 2):
                            transpose(it if u < 2 else it + 1, (u + 2) % 4)
                        if exists(gi + 1):
                            expand(it if u < 3 else it + 1, (u + 1) % 4)
                    summed(it, u)

                if kind != "sum":
                    transpose(0, 0)
                    transpose(0, 1)
                    expand(0, 0)
                per_group(pe, body)
                end_phase(pe, "pe")

            edge_pass("diff", 0)

            pe.sem_inc(dB["fresh"])
            with pe.Fori(0, NG) as g:
                wait(pe, dB, "cp", g + 1)
                transposes(R[0], lambda j: KV[:, j, 0:D], None)
                transposes(R[1], lambda j: KV[:, j, D:2 * D], None)
                transposes(R[2], lambda j: XP[:, j, :], dB["t"])
                wait(pe, dB, "tc", g + 1)
                products(Rt[3], [(tile_of(T1), mat["We1"]), (tile_of(T2), mat["We2"])], dB["mm"])
                wait(pe, dB, "s", g + 1)
                transposes(R[0], lambda j: XN[:, j, :], dB["zt"])
                wait(pe, dB, "ztc", g + 1)
                products(Rt[1], [(tile_of(T3), mat["Wl1"]), (tile_of(T1), mat["Wl2"])], dB["z"])
                wait(pe, dB, "steps", (g + 1) * CHAIN["b"])
                pe.sem_inc(dB["fresh"])
            pe.wait_ge(deg_sum, 1)
            nc.tensor.matmul(R[0][:, 0:1], ONES[:, :], SMALL[:, 0:1], start=True, stop=True).then_inc(deg_tot, 1)
            end_dense(pe)

            for l in range(2):
                s = dD[l]
                pe.wait_ge(w_l1, 16 * L1LOADS * (l + 1))
                def normed(g):
                    wait(pe, s, "xn", g + 1)
                    transposes(R[0], lambda j: XN[:, j, :], s["xt"])

                def position(g):
                    wait(pe, s, "xtc", g + 1)
                    products(Rt[0], [(tile_of(T1), l1mat["Wpos"])], s["pos"])

                def placed(g):
                    wait(pe, s, "xp", g + 1)
                    transposes(R[0], lambda j: XP[:, j, :], s["pt"])

                def turn(g, first=False, last=False):
                    wait(pe, s, "ptc", g + 1)
                    if not last:
                        normed(g + 1)
                    if not first:
                        wait(pe, s, "kv", g)
                    products(Rt[1], [(tile_of(T4), l1mat["Wq"])], None)
                    if not last:
                        position(g + 1)
                    products(Rt[2], [(tile_of(T4), l1mat["Wk"])], None)
                    products(Rt[3], [(tile_of(T4), l1mat["Wv"])], s["qkv"])
                    if not last:
                        placed(g + 1)

                normed(0)
                position(0)
                placed(0)
                turn(0, first=True)
                with pe.Fori(1, NG - 1) as g:
                    turn(g)
                turn(NG - 1, last=True)
                end_phase(pe, "pe")
                edge_pass(f"att{l}", 1)
                s = dE[l]
                def aggregate(g):
                    wait(pe, s, "ag", g + 1)
                    transposes(R[0], lambda j: XN[:, j, :], s["at"])

                def project(g):
                    wait(pe, s, "atc", g + 1)
                    products(Rt[1], [(tile_of(T1), l1mat["Wo"])], s["o"])

                def normed(g):
                    wait(pe, s, "xn", g + 1)
                    transposes(R[0], lambda j: XN[:, j, :], s["xt"])

                def hidden(g, *cs):
                    half = TG * P // 2
                    for c in cs:
                        if c >= 2:
                            wait(pe, s, "gelu", g * (FF // P) + (c - 1))
                        for k in range(2):
                            ins = nc.tensor.matmul(R[2 + c % 2][:, k * 512:k * 512 + half],
                                                   WF1[:, c * P:(c + 1) * P], T4[:, k * half:(k + 1) * half],
                                                   start=True, stop=True)
                        ins.then_inc(s["hid"], 1)

                def turn(g, first=False, last=False):
                    wait(pe, s, "xtc", g + 1)
                    if not last:
                        aggregate(g + 1)
                    hidden(g, 0, 1)
                    if not last:
                        if not first:
                            wait(pe, s, "tail", (g - 1) * TAIL[f"e{l}"] + 1)
                        project(g + 1)
                    hidden(g, 2, 3)
                    if not last:
                        normed(g + 1)
                    wait(pe, s, "gelu", (g + 1) * (FF // P))
                    if last:
                        wait(pe, s, "tail", (g - 1) * TAIL[f"e{l}"] + 1)
                    products(Rt[1], [((lambda j, c=c: HT[:, c, j * P:(j + 1) * P]), WF2[:, c, :])
                                     for c in range(FF // P)], s["o2"])

                aggregate(0)
                project(0)
                normed(0)
                turn(0, first=True)
                with pe.Fori(1, NG - 1) as g:
                    turn(g)
                turn(NG - 1, last=True)
                end_phase(pe, "pe")
            edge_pass("conv", 1)
            def conv_out(g):
                wait(pe, dF, "atc", g + 1)
                products(Rt[1], [(tile_of(T1), mat["Wg"])], dF["o"])
                wait(pe, dF, "h", g + 1)
                transposes(R[2], lambda j: XN[:, j, :], dF["ht"])

            def sums_in(g):
                wait(pe, dF, "ag", g + 1)
                transposes(R[0], lambda j: XN[:, j, :], dF["at"])

            def turn(g, first=False, last=False):
                wait(pe, dF, "htc", g + 1)
                if not last:
                    sums_in(g + 1)
                if not first:
                    wait(pe, dF, "hs", g)
                products(Rt[3], [(tile_of(T4), mat["W31"])], dF["mm"])
                if not last:
                    conv_out(g + 1)

            sums_in(0)
            conv_out(0)
            turn(0, first=True)
            with pe.Fori(1, NG - 1) as g:
                turn(g)
            turn(NG - 1, last=True)
            end_phase(pe, "pe")
            edge_pass("gcn1", 1)
            def beside(eng, first_step, second_step):
                first_step(0)
                second_step(0)
                first_step(1)
                with eng.Fori(1, NG - 1) as g:
                    second_step(g)
                    first_step(g + 1)
                second_step(NG - 1)

            def rows_in(g):
                wait(pe, dG, "h", g + 1)
                transposes(R[0], lambda j: XN[:, j, :], dG["ht"])

            def product(g):
                wait(pe, dG, "htc", g + 1)
                wait(pe, dG, "hs", g)
                products(R[1][:, 0:TG * DZ].rearrange("p (t d) -> p t d", t=TG),
                         [(tile_of(T1), mat["W32"][:, 0:DZ])], dG["mm"])

            beside(pe, rows_in, product)
            end_phase(pe, "pe")
            edge_pass("gcn2", 1)

            def z_in(g):
                wait(pe, dH, "z", g + 1)
                gated(pe, passed)
                transposes(R[0], lambda j: Z64[:, j, :], dH["zt"], DZ)

            def logits(g):
                wait(pe, dH, "ztc", g + 1)
                wait(pe, dH, "y", g)
                products(Rt[1], [(tile_of(T1, DZ), mat["Wd"][0:DZ, :])], dH["mm"])

            beside(pe, z_in, logits)
            end_phase(pe, "pe")

        @block.scalar
        def _(act):
            for n in MATS:
                v = a[n]
                act.dma_start(mat[n][0:v.shape[0], 0:v.shape[1]], v).then_inc(w_in, 16)
            for n in BIASES:
                v = a[n]
                act.dma_start(bias[n][:, 0:v.shape[0]], v.partition_broadcast(P)).then_inc(w_in, 16)

            def copied(dst, src, s, ready, done, g, k=P, how=ACT.Copy, **operands):
                wait(act, s, ready, g + 1)
                nc.scalar.activation(dst[0:k, :], src[0:k, 0:TG * D], how, **operands).then_inc(s[done], 1)

            def deviation(s, n):
                wait(act, s, "mv", n + 1)
                nc.scalar.activation(SD[:, :], MV[:, :, 1], ACT.Sqrt, bias=EPS[:, 0:1]).then_inc(s["sd"], 1)

            for n in ("b31", "b32"):
                v = a[n]
                act.dma_start(column[n][0:v.shape[0]], v.rearrange("(k one) -> k one", one=1)).then_inc(w_in, 16)
            act.wait_ge(w_in, 16 * LOADS)
            with act.Fori(0, NG) as g:
                deviation(dA, g)
                copied(T1, R[0], dA, "t", "tc", g)
            end_phase(act, "act")

            def edge_pass(name):
                s, kind = ps[name], kind_of(name)

                def copy(it, u):
                    gi = it * 4 + u
                    wait(act, s, "tr", gi + 1)
                    wait(act, s, "exp", gi - 1)
                    nc.scalar.activation(OHT[:, u % 2, :, :].rearrange("p s w -> p (s w)"),
                                         R[0][:, (u % 2) * 512:(u % 2) * 512 + 512], ACT.Copy).then_inc(s["oht"], 1)

                def body(it, u):
                    gi = it * 4 + u
                    if exists(gi + 2):
                        copy(it if u < 2 else it + 1, (u + 2) % 4)
                    wait(act, s, "att", gi + 1)
                    if kind == "att":
                        wait(act, s, "agg", gi - 1)
                        nc.scalar.activation(M[:, u % 2, :, D:D + HEADS], EATT[:, :, :], ACT.Exp)\
                            .then_inc(s["ex"], 1)
                    else:
                        nc.scalar.activation(M[:, u % 2, :, 0:D], PROD[:, :, :], ACT.Abs).then_inc(s["msg"], 1)

                if kind != "sum":
                    copy(0, 0)
                    copy(0, 1)
                    per_group(act, body)
                end_phase(act, "act")

            edge_pass("diff")
            with act.Fori(0, NG) as g:
                wait(act, dB, "fresh", g + 1)
                gated(act, passed)
                nc.scalar.activation(KV[:, :, :], accv[AW][:, bass.ds(g * TG, TG), 0:2 * D], ACT.Copy)
                nc.scalar.activation(XP[:, :, :], Y[:, bass.ds(g * TG, TG), :], ACT.Copy).then_inc(dB["cp"], 1)
                wait(act, dB, "t", g + 1)
                nc.scalar.activation(T1, R[0][:, 0:TG * D], ACT.Copy)
                nc.scalar.activation(T2, R[1][:, 0:TG * D], ACT.Copy)
                nc.scalar.activation(T3, R[2][:, 0:TG * D], ACT.Copy).then_inc(dB["tc"], 1)
                copied(T1, R[0], dB, "zt", "ztc", g)
                deviation(dB, g)
            act.wait_ge(root_in, 1)
            nc.scalar.activation(SMALL[:, 1:2], R[0][:, 0:1], ACT.Sqrt, scale=1.0 / (N - 1)).then_inc(root_out, 1)
            act.wait_ge(root_in, 2)
            nc.scalar.activation(RO, RO, ACT.Sqrt).then_inc(root_out, 1)
            end_dense(act)
            for l in range(2):
                s = dD[l]
                norm1 = dict(how=ACT.Identity, scale=column["ln1_g"], bias=column["ln1_b"])
                norm2 = dict(how=ACT.Identity, scale=column["ln2_g"], bias=column["ln2_b"])
                act.wait_ge(w_l1, 16 * L1LOADS * (l + 1))

                def self_exp(g):
                    wait(act, s, "att", g + 1)
                    nc.scalar.activation(EX[:, :, :], ATT[:, :, :], ACT.Exp).then_inc(s["ex"], 1)

                deviation(s, 0)
                copied(T1, R[0], s, "xt", "xtc", 0, **norm1)
                copied(T4, R[0], s, "pt", "ptc", 0)
                deviation(s, 1)
                with act.Fori(0, NG - 2) as g:
                    copied(T1, R[0], s, "xt", "xtc", g + 1, **norm1)
                    copied(T4, R[0], s, "pt", "ptc", g + 1)
                    deviation(s, g + 2)
                    self_exp(g)
                copied(T1, R[0], s, "xt", "xtc", NG - 1, **norm1)
                copied(T4, R[0], s, "pt", "ptc", NG - 1)
                self_exp(NG - 2)
                self_exp(NG - 1)
                end_phase(act, "act")
                edge_pass(f"att{l}")
                if l == 0:
                    act.wait_ge(root_in, 3)
                    nc.scalar.activation(NODE[:, 4:6, :], NODE[:, 4:6, :], ACT.Sqrt).then_inc(root_out, 1)
                s = dE[l]
                def gelu(g, *cs):
                    half = TG * P // 2
                    for c in cs:
                        wait(act, s, "hid", g * (FF // P) + (c + 1))
                        nc.scalar.activation(HT[:, c, :].rearrange("p (k n) -> p k n", k=2),
                                             R[2 + c % 2][:, :].rearrange("p (k n) -> p k n", k=2)[:, :, 0:half],
                                             ACT.Gelu, bias=B1T[:, c:c + 1]).then_inc(s["gelu"], 1)

                def turn(g, last=False):
                    if not last:
                        copied(T1, R[0], s, "at", "atc", g + 1)
                    gelu(g, 0, 1)
                    if not last:
                        deviation(s, (g + 1) * (1 + l) - l)
                    gelu(g, 2, 3)
                    if not last:
                        copied(T4, R[0], s, "xt", "xtc", g + 1, **norm2)
                    if l == 1:
                        deviation(s, 2 * g + (1 if last else 2))

                copied(T1, R[0], s, "at", "atc", 0)
                deviation(s, 0)
                copied(T4, R[0], s, "xt", "xtc", 0, **norm2)
                with act.Fori(0, NG - 1) as g:
                    turn(g)
                turn(NG - 1, last=True)
                end_phase(act, "act")
            edge_pass("conv")
            with act.Fori(0, NG) as g:
                copied(T1, R[0], dF, "at", "atc", g)
                deviation(dF, g)
                copied(T4, R[2], dF, "ht", "htc", g, how=ACT.Relu)
            end_phase(act, "act")
            edge_pass("gcn1")
            with act.Fori(0, NG) as g:
                copied(T1, R[0], dG, "ht", "htc", g, how=ACT.Relu, bias=column["b31"])
            end_phase(act, "act")
            edge_pass("gcn2")
            offset = dict(how=ACT.Identity, bias=column["b32"][0:DZ])

            def sigmoid(g):
                wait(act, dH, "y", g + 1)
                nc.scalar.activation(XP[:, :, :], XN[:, :, :], ACT.Sigmoid).then_inc(dH["sg"], 1)

            copied(T1, R[0], dH, "zt", "ztc", 0, DZ, **offset)
            with act.Fori(0, NG - 1) as g:
                copied(T1, R[0], dH, "zt", "ztc", g + 1, DZ, **offset)
                sigmoid(g)
            sigmoid(NG - 1)
            end_phase(act, "act")

        @block.vector
        def _(dve):
            V = nc.vector

            def copied(dst, src):
                return V.tensor_scalar(dst, src, 0.0, None, ALU.add)

            V.memset(SRCI, NT * P)
            V.memset(DSTI, NT * P).then_inc(ids_cleared, 1)
            V.memset(LIST[:, :, 0], 0)
            V.memset(LIST[:, :, 1], -1).then_inc(clear_ready, 1)
            V.memset(X[:, NT - 1, :], 0.0).then_inc(x_pad, 1)
            dve.wait_ge(const_ready, 1)
            dve.wait_ge(edges_in, 64)

            def bucket(o, key, val):
                s = sort[o]
                m = Chain(dve, s["misc"], 100)
                m.turn(0)
                V.tensor_copy(VAL[o], val)
                V.tensor_single_scalar(LOC[o], key, P - 1, ALU.bitwise_and)
                m.link(V.tensor_single_scalar(HII, key, P.bit_length() - 1, ALU.logical_shift_right))
                V.tensor_copy(HI, HII)
                m.link(V.memset(RANK, 0.0))
                with dve.Fori(0, NT // RB) as it:
                    for k in range(RB):
                        if k >= 2:
                            dve.wait_ge(s["counted"], it * RB + (k - 1))
                        h = bass.ds(it * RB + k, 1)
                        V.tensor_scalar(EQS[k % 2], HI, IOTA[:, h], 0.0, ALU.is_equal, ALU.add,
                                        accum_out=CNT[:, h]).then_inc(s["counted"], 1)
                    dve.wait_ge(s["counted"], it * RB + RB)
                V.memset(STARTP, 1e9).then_inc(s["counts"], 1)
                dve.wait_ge(s["sums"], 1)
                m.link(V.tensor_scalar(NSTI, R[0][:, 512:512 + NT], float(P - 1), None, ALU.add))
                m.link(V.tensor_single_scalar(NSTI, NSTI, P.bit_length() - 1, ALU.logical_shift_right))
                m.link(V.tensor_copy(NST, NSTI))
                m.link(V.tensor_tensor_scan(INCL, ONESC[:, 0:NT], NST, 0.0, ALU.mult, ALU.add))
                m.link(V.tensor_tensor(STARTS, INCL, NST, ALU.subtract))
                V.tensor_copy(STARTP[:, 0:NT], STARTS).then_inc(s["startp"], 1)
                m.link(V.scalar_tensor_tensor(BASE, STARTS, float(P), R[0][:, 0:NT], ALU.mult, ALU.add))
                dve.wait_ge(s["startt"], 1)
                m.link(V.tensor_copy(STARTT, R[1][:, 0:1]))
                V.tensor_scalar(GE, IOTAS, STARTT, None, ALU.is_ge).then_inc(s["ge"], 1)
                dve.wait_ge(s["tiles"], 1)
                half = STEPS // 2
                for k in range(2):
                    m.link(V.tensor_scalar(TILE[o][0:1, k * half:(k + 1) * half], R[2][0:1, k * 512:k * 512 + half],
                                           -1.0, None, ALU.add))

                done = 0
                for part in range(len(PARTS) - 1):
                    cols = slice(PARTS[part] * 2 * SB, PARTS[part + 1] * 2 * SB)
                    carries = part < len(PARTS) - 2
                    steps = []
                    for k in range(RB + 1):
                        if k < RB:
                            steps += ([("equal", k)] if k == 0 else []) + [("count", k)]
                        if k >= 1:
                            steps += [("add", k - 1)]
                        if k + 1 < RB:
                            steps += [("equal", k + 1)]
                        if k < RB:
                            steps += ([("carry", k)] if carries else []) + [("pick", k)]
                    needs = dict(equal=None, count="equal", carry="count", pick="carry" if carries else "count", add="pick")
                    if part:
                        dve.wait_ge(s["step"], done)
                    with dve.Fori(0, NT // RB) as it:
                        start = it * len(steps) + done
                        for what, k in steps:
                            h, eq, cum = bass.ds(it * RB + k, 1), EQS[k % 2][:, cols], CUMS[k % 2][:, cols]
                            if needs[what]:
                                dve.wait_ge(s["step"], start + steps.index((needs[what], k)) + 1)
                            if what == "equal":
                                ins = V.tensor_scalar(eq, HI[:, cols], IOTA[:, h], None, ALU.is_equal)
                            elif what == "count":
                                ins = V.tensor_tensor_scan(cum, ONESC[:, cols], eq, BASE[:, h], ALU.mult, ALU.add)
                            elif what == "carry":
                                ins = copied(BASE[:, h], CUMS[k % 2][:, cols.stop - 1:cols.stop])
                            elif what == "pick":
                                ins = V.tensor_tensor(cum, eq, cum, ALU.mult)
                            else:
                                ins = V.tensor_tensor(RANK[:, cols], RANK[:, cols], cum, ALU.add)
                            ins.then_inc(s["step"], 1)
                    done += len(steps) * (NT // RB)
                    dve.wait_ge(s["step"], done)
                    eq, cum, low, high = (v[:, cols] for v in (EQS[0], CUMS[0], POSA, POSB))
                    m.link(V.tensor_scalar(HII[:, cols], RANK[:, cols], -1.0, None, ALU.add))
                    V.tensor_single_scalar(low, HII[:, cols], P - 1, ALU.bitwise_and)
                    m.link(V.tensor_single_scalar(high, HII[:, cols], P.bit_length() - 1, ALU.arith_shift_right))
                    m.link(V.tensor_scalar(eq, HI[:, cols], float(NT), float(OUT_OF_RANGE), ALU.is_equal, ALU.mult))
                    m.link(V.scalar_tensor_tensor(cum, low, float(STEPS), high, ALU.mult, ALU.add))
                    V.tensor_tensor(SLOT[o][:, cols], cum, eq, ALU.add).then_inc(s["slots"], 1)
                    dve.wait_ge(s["slots"], part + 1)

            bucket(0, SRCI, DSTI)


            def layer_norm(c, s, n, src, dst, what=None, g=None):
                gated(dve, passed)
                for j in range(TG):
                    ins = V.bn_stats(ST[:, j, :], src(j))
                c.link(ins)
                gated(dve, passed)
                for j in range(TG):
                    ins = V.bn_aggr(MV[:, j, :], ST[:, j, :])
                ins.then_inc(s["mv"], 1)
                wait(dve, s, "sd", n + 1)
                c.link(V.reciprocal(RSTD[:, :], SD[:, :]))
                for j in range(TG):
                    ins = V.tensor_scalar(dst[:, j, :], src(j), MV[:, j, 0:1], RSTD[:, j:j + 1],
                                          ALU.subtract, ALU.mult)
                if what:
                    signal(ins, s, what, g)
                else:
                    c.link(ins)

            def turn_of(t, g):
                return t[:, bass.ds(g * TG, TG), :]

            def tile_in(t, g):
                return lambda j: t[:, bass.ds(g * TG + j, 1), :].rearrange("p t d -> p (t d)")

            def signal(ins, s, what, g):
                ins.then_inc(s[what], 1)
                wait(dve, s, what, g + 1)

            dve.wait_ge(x_in, 32)
            dve.wait_ge(w_in, 16 * LOADS)
            c = Chain(dve, dA["steps"], CHAIN["a"], dA.base["steps"])
            with dve.Fori(0, NG) as g:
                c.turn(g)
                layer_norm(c, dA, g, tile_in(X, g), XN)
                signal(V.tensor_scalar(XN[:, :, :], XN[:, :, :], 0.0, None, ALU.max), dA, "h", g)
                c.link(copied(turn_of(Y, g), XN[:, :, :]))
                wait(dve, dA, "mm", g + 1)
                wait(dve, dA, "free", g + 1)
                signal(V.tensor_tensor(HS[:, :, :], Rt[1], over_tiles(bias["bn"]), ALU.add), dA, "hp", g)
                c.link(copied(turn_of(Q, g), HS[:, :, :]))
                c.end()
            bucket(1, DSTI, SRCI)
            def take_list(o):
                dve.wait_ge(sort[o]["listed"], 16)
                V.tensor_copy(LO[o][:, :], LIST[:, :, 1]).then_inc(taken, 1)
                dve.wait_ge(taken, o + 1)

            take_list(0)
            V.memset(ACC[:, :], 0.0)
            V.memset(OUTD, 0.0)
            end_phase(dve, "dve")

            def edge_pass(name, o):
                s, kind = ps[name], kind_of(name)
                w = {"att": L1W, "diff": AW}.get(kind, TABLE[name][1])
                G = Gw if kind == "att" else Gn

                def onehot(it, u):
                    gi = it * 4 + u
                    V.tensor_tensor(OH[:, u % 4, :, :], over_tiles(IOTA[:, :], S4),
                                    over_features(LO[o][:, bass.ds(gi * S4, S4)]), ALU.is_equal)\
                        .then_inc(s["oh"], 1)

                def add(it, u, tiles, j):
                    gi = it * 4 + u
                    if j == 0:
                        wait(dve, s, "agg", gi + 1)
                    wait(dve, s, "acc", gi * S4 + j)
                    at = j * 512 if kind == "diff" else u % 2 * 1024 + j * 256
                    dst = ACC[:, bass.ds(tiles[j] * w, w)]
                    V.tensor_tensor(dst, dst, SUMS[:, at:at + w], ALU.add).then_inc(s["acc"], 1)

                def body(it, u):
                    gi = it * 4 + u
                    later = (it if u < 1 else it + 1, (u + 3) % 4)
                    before = (it, u - 1) if u else (it - 1, 3)
                    tiles = None
                    if not (isinstance(gi, int) and gi == 0):
                        tiles = step_tiles(dve, o, before[0] * 4 + before[1])

                    def sums(*js):
                        for j in js if tiles else ():
                            add(*before, tiles, j)

                    if kind != "sum":
                        wait(dve, s, "exp", gi + 1)
                        wait(dve, s, "gath", (it + 1) * (16 * S4), u)
                        rows = R[1][:, (u % 2) * 512:(u % 2) * 512 + 512].rearrange("p (s w) -> p s w", s=S4)
                    if kind == "diff":
                        wait(dve, s, "msg", gi)
                        V.tensor_tensor(PROD[:, :, :], rows, G[:, u, :, 0:D], ALU.subtract).then_inc(s["att"], 1)
                        sums(0)
                        if exists(gi + 3):
                            onehot(*later)
                        sums(1, 2, 3)
                    elif kind == "sum":
                        sums(0)
                        if exists(gi + 3):
                            onehot(*later)
                        sums(1, 2, 3)
                    else:
                        V.tensor_tensor(PROD[:, :, :], rows, G[:, u, :, 0:D], ALU.mult).then_inc(s["prod"], 1)
                        wait(dve, s, "prod", gi + 1)
                        wait(dve, s, "ex", gi)
                        V.tensor_reduce(EATT[:, :, :], heads(PROD[:, :, :]), AX.X, ALU.add).then_inc(s["red"], 1)
                        sums(0)
                        wait(dve, s, "red", gi + 1)
                        V.tensor_scalar(EATT[:, :, :], EATT[:, :, :], -50.0, 50.0, ALU.max, ALU.min)\
                            .then_inc(s["att"], 1)
                        if exists(gi + 3):
                            onehot(*later)
                        sums(1)
                        wait(dve, s, "ex", gi + 1)
                        V.tensor_tensor(heads(M[:, u % 2, :, 0:D]), heads(G[:, u, :, D:2 * D]),
                                        over_heads(M[:, u % 2, :, D:D + HEADS]), ALU.mult).then_inc(s["msg"], 1)
                        sums(2, 3)

                if kind == "att":
                    V.memset(M[:, :, :, D + HEADS:L1W], 1.0)
                if kind == "diff":
                    V.memset(M[:, :, :, D:D + 1], 1.0)
                for u in range(3):
                    onehot(0, u)
                per_group(dve, body)
                tiles = step_tiles(dve, o, GROUPS - 1)
                for j in range(S4):
                    add(GROUPS // 4 - 1, 3, tiles, j)
                if kind == "diff":
                    wait(dve, s, "acc", S4 * GROUPS)
                    V.tensor_copy(OUTD, accv[AW][:, :, 2 * D])
                end_phase(dve, "dve")

            edge_pass("diff", 0)

            c = Chain(dve, dB["steps"], CHAIN["b"], dB.base["steps"])
            with dve.Fori(0, NG) as g:
                c.turn(g)
                copied(CT[:, 0, :], OUTD[:, bass.ds(g * TG, TG)])
                c.link(V.tensor_scalar(CT[:, 1, :], OUTD[:, bass.ds(g * TG, TG)], 1.0, None, ALU.max))
                c.link(V.reciprocal(CT[:, 1, :], CT[:, 1, :]))
                wait(dve, dB, "mm", g + 1)
                for j in range(TG):
                    ins = V.scalar_tensor_tensor(XN[:, j, :], bias["be"], CT[:, 0, j:j + 1], Rt[3][:, j, :],
                                                 ALU.mult, ALU.add)
                c.link(ins)
                c.link(V.tensor_tensor(XN[:, :, :], XN[:, :, :], turn_of(Q, g), ALU.add))
                signal(V.tensor_tensor(XN[:, :, :], XN[:, :, :], over_features(CT[:, 1, :]), ALU.mult), dB, "s", g)
                wait(dve, dB, "z", g + 1)
                c.link(V.tensor_tensor(XN[:, :, :], Rt[1], over_tiles(bias["bl"]), ALU.add))
                c.link(V.tensor_tensor(turn_of(X, g), turn_of(X, g), XN[:, :, :], ALU.add))
                layer_norm(c, dB, g, tile_in(X, g), XN)
                c.link(V.tensor_scalar(turn_of(Y, g), XN[:, :, :], 0.0, None, ALU.max))
                c.end()
            mean = (E + N) / N
            c = Chain(dve, deg_step, 100)
            c.turn(0)
            c.link(V.tensor_scalar(DEGN, OUTD, 1.0, -mean, ALU.add, ALU.add))
            c.link(V.tensor_tensor(TMPN, DEGN, MASK, ALU.mult))
            c.link(V.tensor_tensor(TMPN, TMPN, TMPN, ALU.mult))
            V.tensor_reduce(SMALL[:, 0:1], TMPN, AX.X, ALU.add).then_inc(deg_sum, 1)
            dve.wait_ge(deg_tot, 1)
            V.tensor_scalar(RO, OUTD, 1.0, None, ALU.max).then_inc(root_in, 2)
            dve.wait_ge(root_out, 2)
            c.link(V.tensor_scalar(SMALL[:, 2:3], SMALL[:, 1:2], 1e-6, None, ALU.add))
            c.link(V.reciprocal(SMALL[:, 3:4], SMALL[:, 2:3]))
            c.link(V.tensor_scalar(DEGN, DEGN, SMALL[:, 3:4], None, ALU.mult))
            c.link(V.reciprocal(RO, RO))
            end_dense(dve)

            for l in range(2):
                s = dD[l]
                dve.wait_ge(w_l1, 16 * L1LOADS * (l + 1))
                c = Chain(dve, dD_pre[l], 3)
                c.turn(0)
                c.link(V.tensor_tensor(row["bpos"], row["bpos"], row["bdeg"], ALU.add))
                c.link(V.tensor_tensor(row["bpos"], row["bpos"], row["ln1_b"], ALU.add))
                c.link(V.tensor_scalar(row["bq"], row["bq"], float(HD) ** -0.5, None, ALU.mult))
                head = Chain(dve, s["steps"], CHAIN[f"d{l}"], s.base["steps"])
                place = Chain(dve, s["agg_steps"], 2, s.base["agg_steps"])
                tail = Chain(dve, s["tail"], TAIL[f"d{l}"], s.base["tail"])

                def normed(g):
                    head.turn(g)
                    wait(dve, s, "xt", g)
                    layer_norm(head, s, g, tile_in(Y, g), XN, "xn", g)
                    head.link(V.tensor_tensor(XG[:, :, :], XN[:, :, :], over_tiles(row["ln1_g"]), ALU.mult))
                    head.end()

                def placed(g):
                    place.turn(g)
                    copied(CT[:, 0, :], DEGN[:, bass.ds(g * TG, TG)])
                    wait(dve, s, "pos", g + 1)
                    place.link(V.tensor_tensor(XP[:, :, :], Rt[0], over_tiles(row["bpos"]), ALU.add))
                    for j in range(TG):
                        ins = V.scalar_tensor_tensor(XP[:, j, :], row["Wdeg"], CT[:, 0, j:j + 1], XP[:, j, :],
                                                     ALU.mult, ALU.add)
                    place.link(ins)
                    signal(V.tensor_tensor(XP[:, :, :], XP[:, :, :], XG[:, :, :], ALU.add), s, "xp", g)
                    place.end()

                def projected(g):
                    tail.turn(g)
                    wait(dve, s, "qkv", g + 1)
                    tail.link(V.scalar_tensor_tensor(turn_of(Q, g), Rt[1], float(HD) ** -0.5, over_tiles(row["bq"]),
                                                     ALU.mult, ALU.add))
                    wait(dve, s, "free", g + 1)
                    tail.link(V.tensor_tensor(KV[:, :, 0:D], Rt[2], over_tiles(row["bk"]), ALU.add))
                    signal(V.tensor_tensor(KV[:, :, D:2 * D], Rt[3], over_tiles(row["bv"]), ALU.add), s, "kv", g)
                    tail.link(V.tensor_tensor(XB[:, :, :], turn_of(Q, g), KV[:, :, 0:D], ALU.mult))
                    tail.link(V.tensor_reduce(ATT[:, :, :], heads(XB[:, :, :]), AX.X, ALU.add))
                    signal(V.tensor_scalar(ATT[:, :, :], ATT[:, :, :], -50.0, 50.0, ALU.max, ALU.min), s, "att", g)
                    wait(dve, s, "ex", g + 1)
                    acc = turn_of(accv[L1W], g)
                    tail.link(V.tensor_tensor(heads(acc[:, :, 0:D]), heads(KV[:, :, D:2 * D]),
                                              over_heads(EX[:, :, :]), ALU.mult))
                    tail.link(copied(acc[:, :, D:D + HEADS], EX[:, :, :]))
                    tail.link(copied(acc[:, :, D + HEADS:L1W], ZERO[:, 0:TG].unsqueeze(2)))
                    tail.end()

                normed(0)
                placed(0)
                normed(1)
                with dve.Fori(0, NG - 2) as g:
                    placed(g + 1)
                    normed(g + 2)
                    projected(g)
                placed(NG - 1)
                projected(NG - 2)
                projected(NG - 1)
                end_phase(dve, "dve")
                if l == 0:
                    take_list(1)
                edge_pass(f"att{l}", 1)
                if l == 0:
                    c = Chain(dve, ind_step, 5)
                    c.turn(0)
                    c.link(V.tensor_copy(IND, accv[L1W][:, :, D + HEADS]))
                    c.link(V.tensor_scalar(RI, IND, 1.0, None, ALU.max))
                    V.tensor_scalar(DI, IND, 1.0, None, ALU.add).then_inc(root_in, 1)
                    dve.wait_ge(root_out, 3)
                    c.link(V.reciprocal(NODE[:, 4:6, :], NODE[:, 4:6, :]))
                s = dE[l]
                head = Chain(dve, s["steps"], CHAIN[f"e{l}"], s.base["steps"])
                mean = Chain(dve, s["agg_steps"], 1, s.base["agg_steps"])
                tail = Chain(dve, s["tail"], TAIL[f"e{l}"], s.base["tail"])

                def aggregate(g):
                    mean.turn(g)
                    acc = turn_of(accv[L1W], g)
                    mean.link(V.reciprocal(RSUM[:, :, :], acc[:, :, D:D + HEADS]))
                    wait(dve, s, "xt", g)
                    signal(V.tensor_tensor(heads(XN[:, :, :]), heads(acc[:, :, 0:D]), over_heads(RSUM[:, :, :]),
                                           ALU.mult), s, "ag", g)

                def normed(g):
                    head.turn(g)
                    wait(dve, s, "o", g + 1)
                    head.link(V.tensor_tensor(XN[:, :, :], Rt[1], over_tiles(row["bo"]), ALU.add))
                    head.link(V.tensor_tensor(turn_of(Y, g), turn_of(Y, g), XN[:, :, :], ALU.add))
                    n = g * (1 + l) if isinstance(g, int) and g == 0 else g * (1 + l) - l
                    layer_norm(head, s, n, tile_in(Y, g), XN, "xn", g)
                    head.end()

                def ffn_added(g, last=False):
                    tail.turn(g)
                    wait(dve, s, "o2", g + 1)
                    tail.link(V.tensor_tensor(XB[:, :, :], Rt[1], over_tiles(row["b2"]), ALU.add))
                    tail.link(V.tensor_tensor(turn_of(Y, g), turn_of(Y, g), XB[:, :, :], ALU.add))
                    if l == 1:
                        tail.link(V.tensor_tensor(turn_of(X, g), turn_of(X, g), turn_of(Y, g), ALU.add))
                        layer_norm(tail, s, 2 * g + (1 if last else 2), tile_in(X, g), XB)
                        wait(dve, s, "free", g + 1)
                        signal(V.scalar_tensor_tensor(XP[:, :, :], XB[:, :, :], 0.0,
                                                      over_features(RO[:, bass.ds(g * TG, TG)]), ALU.max, ALU.mult),
                               s, "hs", g)
                    tail.end()

                aggregate(0)
                normed(0)
                aggregate(1)
                with dve.Fori(0, NG - 2) as g:
                    normed(g + 1)
                    aggregate(g + 2)
                    ffn_added(g)
                normed(NG - 1)
                ffn_added(NG - 2)
                ffn_added(NG - 1, last=True)
                if l == 1:
                    V.memset(ACC[:, 0:NT * D], 0.0)
                end_phase(dve, "dve")

            edge_pass("conv", 1)
            head = Chain(dve, dF["steps"], CHAIN["f"], dF.base["steps"])
            tail = Chain(dve, dF["tail"], TAIL["f"], dF.base["tail"])

            def sums_in(g):
                wait(dve, dF, "ht", g)
                signal(V.tensor_tensor(XN[:, :, :], turn_of(accv[D], g), over_features(RI[:, bass.ds(g * TG, TG)]),
                                       ALU.mult), dF, "ag", g)

            def conv_out(g):
                head.turn(g)
                wait(dve, dF, "o", g + 1)
                head.link(V.tensor_tensor(XN[:, :, :], Rt[1], over_tiles(bias["bg"]), ALU.add))
                head.link(V.scalar_tensor_tensor(turn_of(X, g), XN[:, :, :], 0.0, turn_of(X, g), ALU.max, ALU.add))
                layer_norm(head, dF, g, tile_in(X, g), XN, "h", g)
                head.end()

            def rows_out(g):
                tail.turn(g)
                wait(dve, dF, "mm", g + 1)
                wait(dve, dF, "free", g + 1)
                signal(V.tensor_tensor(HS[:, :, :], Rt[3], over_features(DI[:, bass.ds(g * TG, TG)]), ALU.mult),
                       dF, "hs", g)
                tail.link(copied(turn_of(accv[D], g), HS[:, :, :]))
                tail.end()

            sums_in(0)
            conv_out(0)
            sums_in(1)
            with dve.Fori(0, NG - 2) as g:
                conv_out(g + 1)
                sums_in(g + 2)
                rows_out(g)
            conv_out(NG - 1)
            rows_out(NG - 2)
            rows_out(NG - 1)
            end_phase(dve, "dve")
            edge_pass("gcn1", 1)
            tail = Chain(dve, dG["tail"], TAIL["g"], dG.base["tail"])

            def rows_in(g):
                wait(dve, dG, "ht", g)
                signal(V.tensor_tensor(XN[:, :, :], turn_of(accv[D], g), over_features(DI[:, bass.ds(g * TG, TG)]),
                                       ALU.mult), dG, "h", g)

            def rows_out(g, tail=tail):
                tail.turn(g)
                wait(dve, dG, "mm", g + 1)
                wait(dve, dG, "free", g + 1)
                signal(V.tensor_tensor(HS64[:, :, :], R[1][:, 0:TG * DZ].rearrange("p (t d) -> p t d", t=TG),
                                       over_features(DI[:, bass.ds(g * TG, TG)], DZ), ALU.mult), dG, "hs", g)
                tail.link(copied(turn_of(accv[DZ], g), HS64[:, :, :]))
                tail.end()

            rows_in(0)
            with dve.Fori(0, NG - 1) as g:
                rows_in(g + 1)
                rows_out(g)
            rows_out(NG - 1)
            end_phase(dve, "dve")
            edge_pass("gcn2", 1)
            tail = Chain(dve, dH["tail"], TAIL["h"], dH.base["tail"])

            def z_in(g):
                wait(dve, dH, "zt", g)
                signal(V.tensor_tensor(Z64[:, :, :], turn_of(accv[DZ], g),
                                       over_features(DI[:, bass.ds(g * TG, TG)], DZ), ALU.mult), dH, "z", g)

            def x_out(g):
                tail.turn(g)
                wait(dve, dH, "mm", g + 1)
                signal(V.tensor_tensor(XN[:, :, :], Rt[1], over_tiles(bias["bd"]), ALU.add), dH, "y", g)
                wait(dve, dH, "sg", g + 1)
                tail.link(V.tensor_tensor(turn_of(X, g), turn_of(X, g), XP[:, :, :], ALU.add))
                tail.end()

            z_in(0)
            with dve.Fori(0, NG - 1) as g:
                z_in(g + 1)
                x_out(g)
            x_out(NG - 1)
            end_phase(dve, "dve")


def kernel(**inputs):
    import numpy as np
    import concourse.bacc as bacc
    from concourse.bass_utils import run_bass_kernel_spmd as run

    i = {k: np.asarray(v) for k, v in inputs.items()}
    t = np.ascontiguousarray
    host = {"x": i["x"], "src": i["src"], "dst": i["dst"]}
    host["Wn"] = t(i["L0_gnn_W_neigh"].T)
    host["We1"], host["We2"] = t(i["L0_gnn_W_edge"].T[:D]), t(i["L0_gnn_W_edge"].T[D:])
    host["Wl1"], host["Wl2"] = t(i["L0_gnn_W_lin"].T[:D]), t(i["L0_gnn_W_lin"].T[D:])
    host["bn"], host["be"], host["bl"] = i["L0_gnn_b_neigh"], i["L0_gnn_b_edge"], i["L0_gnn_b_lin"]
    for n in ("Wpos", "Wq", "Wk", "Wv", "Wo", "bpos", "bdeg", "Wdeg", "bq", "bk", "bv", "bo", "ln1_g", "ln1_b",
              "ln2_g", "ln2_b", "b2", "W1", "W2"):
        host[n] = i["L1_gnn_" + n]
    host["b1t"] = t(i["L1_gnn_b1"].reshape(2, FF // P, P).transpose(0, 2, 1))
    host["Wg"], host["bg"] = i["L2_gnn_weight"], i["L2_gnn_bias"]
    host["W31"], host["b31"], host["W32"], host["b32"] = (i["L3_gnn_" + n] for n in ("W1", "b1", "W2", "b2"))
    host["Wd"], host["bd"] = i["L3_gnn_Wd"], i["L3_gnn_bd"]

    nc = bacc.Bacc("TRN2", target_bir_lowering=False, num_devices=1)
    a, arrays = {}, {}
    for n, v in host.items():
        arrays["in_" + n] = t(v)
        a[n] = nc.dram_tensor("in_" + n, v.shape, mybir.dt.from_np(v.dtype), kind="ExternalInput").ap()
    out = nc.dram_tensor("out_x", (N, D), F32, kind="ExternalOutput").ap()
    build(nc, a, out)
    return run(nc, [arrays], core_ids=[0]).results[0]["out_x"]
```
